# Optimizing a Trainium2 kernel written in Bass

```python
import numpy as np
import jax
import jax.numpy as jnp

def _softmax(x, axis=-1):
    return jax.nn.softmax(x, axis=axis)

def _gelu(x):
    return jax.nn.gelu(x, approximate=True)

def _silu(x):
    return jax.nn.silu(x)

def _sigmoid(x):
    return jax.nn.sigmoid(x)

def _layernorm(x, axis=-1, eps=1e-05):
    m = jnp.mean(x, axis=axis, keepdims=True)
    v = jnp.var(x, axis=axis, keepdims=True)
    return (x - m) / jnp.sqrt(v + eps)

def _scatter_add(tgt, idx, src, axis=0):
    return tgt.at[idx].add(src)

def _segment_sum(src, seg, n):
    return jax.ops.segment_sum(src, seg, n)
kernel_name = 'mk_audio_tower_d1_tok_audfeat1024_r4_bd32a4'

def setup_inputs(seed: int=0):
    np.random.seed(seed)
    _w = jnp.asarray

    def _rec_inputs():
        import jax
        import jax.numpy as jnp
        _rk = jax.random.key(seed)
        x = -0.000212499 + 0.999965 * jax.random.normal(jax.random.fold_in(_rk, 1), (16, 375, 256), jnp.float32)
        return x
    x = _rec_inputs()

    def _L0_tok_setup():
        import jax, jax.numpy as jnp
        import numpy as np
        NUM_PATCHES = 196
        key = jax.random.key(seed)
        k1, k2, k3 = jax.random.split(key, 3)
        B, D = (128, 256)
        X = jax.random.normal(k1, (B, 1 + NUM_PATCHES, D), dtype=jnp.float32)
        W = jax.random.normal(k2, (2 * D, D), dtype=jnp.float32) * (1.0 / np.sqrt(2 * D))
        b = jax.random.normal(k3, (D,), dtype=jnp.float32) * 0.01
        return {'X': X, 'W': W, 'b': b}
    _L0_tok_all = _L0_tok_setup()
    _L0_tok_in = {k: v for k, v in _L0_tok_all.items() if k in ('W', 'b')}
    del _L0_tok_all

    def _L0_attn_setup():
        import jax, jax.numpy as jnp
        import numpy as np
        EPS = 1e-08
        key = jax.random.key(seed)
        x = jax.random.normal(key, (64, 200, 256), dtype=jnp.float32)
        return {'x': x}
    _L0_attn_all = _L0_attn_setup()
    _L0_attn_in = {k: v for k, v in _L0_attn_all.items() if k in ()}
    del _L0_attn_all

    def _L0_ffn_setup():
        import jax, jax.numpy as jnp
        import numpy as np
        B, T, C, D = (2, 1024, 256, 128)
        E = 8
        MIN_E = 2
        EPS = 1e-12
        NEG = -1000000000.0

        def _xavier(key, shape, fan_in, fan_out):
            bound = (6.0 / (fan_in + fan_out)) ** 0.5
            return jax.random.uniform(key, shape, jnp.float32, -bound, bound)

        def _forward(hidden_states, sim_matrix, gates, q_proj, k_proj, v_proj, o_proj):
            b, t, c = hidden_states.shape
            x = hidden_states.reshape(b * t, c)
            xn = x / jnp.maximum(jnp.linalg.norm(x, axis=-1, keepdims=True), EPS)
            sn = sim_matrix / jnp.maximum(jnp.linalg.norm(sim_matrix, axis=0, keepdims=True), EPS)
            logits = xn @ sn - jax.nn.sigmoid(gates)
            gated = jax.nn.relu(logits)
            mask = (gated > 0).astype(logits.dtype)
            inactive = jnp.sum(mask, axis=1) == 0
            top_idx = jax.lax.top_k(logits, MIN_E)[1]
            n = mask.shape[0]
            fb = jnp.zeros_like(mask).at[jnp.arange(n)[:, None], top_idx].set(1.0)
            mask = jnp.where(inactive[:, None] & (fb > 0), 1.0, mask)
            masked_logits = jnp.where(mask > 0, gated, NEG)
            routing_weights = jax.nn.softmax(masked_logits, axis=-1)
            m = jax.lax.stop_gradient(mask)
            q = jnp.einsum('tc,ecd,te->td', x, q_proj, m)
            k = jnp.einsum('tc,ecd,te->td', x, k_proj, m)
            v = jnp.einsum('tc,ecd,te->td', x, v_proj, m)
            qh = q.reshape(b, t, D)
            kh = k.reshape(b, t, D)
            vh = v.reshape(b, t, D)
            scores = jnp.einsum('bqd,bkd->bqk', qh, kh) / jnp.sqrt(jnp.asarray(D, qh.dtype))
            causal = jnp.tril(jnp.ones((t, t), bool))
            scores = jnp.where(causal, scores, jnp.finfo(scores.dtype).min)
            attn = jax.nn.softmax(scores, axis=-1)
            attn_out = jnp.einsum('bqk,bkd->bqd', attn, vh).reshape(b * t, D)
            final = jnp.einsum('td,edc,te->tc', attn_out, o_proj, m * routing_weights)
            return final.reshape(b, t, c)
        key = jax.random.key(seed)
        k = jax.random.split(key, 6)
        hidden_states = jax.random.normal(k[0], (B, T, C), jnp.float32)
        sim_matrix = jax.random.normal(k[1], (C, E), jnp.float32)
        gates = jnp.zeros((E,), jnp.float32)
        q_proj = _xavier(k[2], (E, C, D), C, D)
        k_proj = _xavier(k[3], (E, C, D), C, D)
        v_proj = _xavier(k[4], (E, C, D), C, D)
        o_proj = _xavier(k[5], (E, D, C), D, C)
        return dict(hidden_states=hidden_states, sim_matrix=sim_matrix, gates=gates, q_proj=q_proj, k_proj=k_proj, v_proj=v_proj, o_proj=o_proj)
    _L0_ffn_all = _L0_ffn_setup()
    _L0_ffn_in = {k: v for k, v in _L0_ffn_all.items() if k in ('sim_matrix', 'gates', 'q_proj', 'k_proj', 'v_proj', 'o_proj')}
    del _L0_ffn_all
    return {'x': x, 'L0_tok_W': _L0_tok_in['W'], 'L0_tok_b': _L0_tok_in['b'], 'L0_ffn_sim_matrix': _L0_ffn_in['sim_matrix'], 'L0_ffn_gates': _L0_ffn_in['gates'], 'L0_ffn_q_proj': _L0_ffn_in['q_proj'], 'L0_ffn_k_proj': _L0_ffn_in['k_proj'], 'L0_ffn_v_proj': _L0_ffn_in['v_proj'], 'L0_ffn_o_proj': _L0_ffn_in['o_proj']}

def reference(x, L0_tok_W, L0_tok_b, L0_ffn_sim_matrix, L0_ffn_gates, L0_ffn_q_proj, L0_ffn_k_proj, L0_ffn_v_proj, L0_ffn_o_proj):
    import jax
    import jax.numpy as jnp

    def _L0_tok_ref(X, W, b):
        import jax, jax.numpy as jnp
        import numpy as np
        NUM_PATCHES = 196
        D = X.shape[-1]
        readout = X[:, :1, :]
        other = X[:, 1:, :]
        W_other, W_read = (W[:D], W[D:])
        proj = jnp.einsum('bpd,de->bpe', other, W_other) + jnp.einsum('bod,de->boe', readout, W_read) + b
        return jax.nn.gelu(proj, approximate=False)

    def _L0_attn_ref(x):
        import jax, jax.numpy as jnp
        import numpy as np
        EPS = 1e-08
        norms = jnp.linalg.norm(x, axis=-1)
        dots = jnp.einsum('bil,bjl->bij', x, x)
        sim = dots / jnp.maximum(norms[:, :, None] * norms[:, None, :], EPS)
        atten = jax.nn.softmax(sim, axis=-1)
        out = jnp.einsum('bij,bjl->bil', atten, x) + x
        return out

    def _L0_ffn_ref(hidden_states, sim_matrix, gates, q_proj, k_proj, v_proj, o_proj):
        import jax, jax.numpy as jnp
        import numpy as np
        B, T, C, D = (2, 1024, 256, 128)
        E = 8
        MIN_E = 2
        EPS = 1e-12
        NEG = -1000000000.0

        def _xavier(key, shape, fan_in, fan_out):
            bound = (6.0 / (fan_in + fan_out)) ** 0.5
            return jax.random.uniform(key, shape, jnp.float32, -bound, bound)

        def _forward(hidden_states, sim_matrix, gates, q_proj, k_proj, v_proj, o_proj):
            b, t, c = hidden_states.shape
            x = hidden_states.reshape(b * t, c)
            xn = x / jnp.maximum(jnp.linalg.norm(x, axis=-1, keepdims=True), EPS)
            sn = sim_matrix / jnp.maximum(jnp.linalg.norm(sim_matrix, axis=0, keepdims=True), EPS)
            logits = xn @ sn - jax.nn.sigmoid(gates)
            gated = jax.nn.relu(logits)
            mask = (gated > 0).astype(logits.dtype)
            inactive = jnp.sum(mask, axis=1) == 0
            top_idx = jax.lax.top_k(logits, MIN_E)[1]
            n = mask.shape[0]
            fb = jnp.zeros_like(mask).at[jnp.arange(n)[:, None], top_idx].set(1.0)
            mask = jnp.where(inactive[:, None] & (fb > 0), 1.0, mask)
            masked_logits = jnp.where(mask > 0, gated, NEG)
            routing_weights = jax.nn.softmax(masked_logits, axis=-1)
            m = jax.lax.stop_gradient(mask)
            q = jnp.einsum('tc,ecd,te->td', x, q_proj, m)
            k = jnp.einsum('tc,ecd,te->td', x, k_proj, m)
            v = jnp.einsum('tc,ecd,te->td', x, v_proj, m)
            qh = q.reshape(b, t, D)
            kh = k.reshape(b, t, D)
            vh = v.reshape(b, t, D)
            scores = jnp.einsum('bqd,bkd->bqk', qh, kh) / jnp.sqrt(jnp.asarray(D, qh.dtype))
            causal = jnp.tril(jnp.ones((t, t), bool))
            scores = jnp.where(causal, scores, jnp.finfo(scores.dtype).min)
            attn = jax.nn.softmax(scores, axis=-1)
            attn_out = jnp.einsum('bqk,bkd->bqd', attn, vh).reshape(b * t, D)
            final = jnp.einsum('td,edc,te->tc', attn_out, o_proj, m * routing_weights)
            return final.reshape(b, t, c)
        return _forward(hidden_states, sim_matrix, gates, q_proj, k_proj, v_proj, o_proj)
    h = _L0_tok_ref(x, L0_tok_W, L0_tok_b)
    h = h + _L0_attn_ref(_layernorm(h, axis=-1))
    h = h + _L0_ffn_ref(_layernorm(h, axis=-1), L0_ffn_sim_matrix, L0_ffn_gates, L0_ffn_q_proj, L0_ffn_k_proj, L0_ffn_v_proj, L0_ffn_o_proj)
    return h

_drawn_inputs = setup_inputs


def setup_inputs(seed=0):
    import zlib

    import numpy as np

    out = dict(_drawn_inputs(seed))
    spreads = {'L0_ffn_gates': (0.0, 0.1)}
    factors = {}
    for name, (base, spread) in spreads.items():
        noise = np.random.default_rng([zlib.crc32(name.encode()), seed]).standard_normal(out[name].shape)
        drawn = base * np.exp(spread * noise) if base else spread * noise
        out[name] = jnp.asarray(drawn.astype(out[name].dtype))
    for name, factor in factors.items():
        out[name] = (out[name] * factor).astype(out[name].dtype)
    return out
```

```python
import math
from contextlib import ExitStack

import concourse.bass as bass
from concourse import mybir

P = 128
ALU = mybir.AluOpType
ACT = mybir.ActivationFunctionType
F32 = mybir.dt.float32
F16 = mybir.dt.float16
AX_X = mybir.AxisListType.X

X_SCALE = 2.0 ** 6
LN_SCALE = 2.0 ** 11
W_SCALE = 2.0 ** 8
Q_SCALE = 2.0 ** 4
P_SCALE = 2.0 ** 13
LN_EPS = 1e-5
COS_EPS = 1e-8
NORM_EPS = 1e-12
MASKED = -1e30


def audio_tower_kernel(nc, x, tok_w, tok_b, sim_matrix, gates, q_proj, k_proj, v_proj, o_proj, out):
    B, T1, C = x.shape
    T = T1 - 1
    E, _, D = q_proj.shape
    NT = -(-T // P)
    TP = NT * P
    LAST = T - (NT - 1) * P
    NC = C // P
    PAIRS = NT * E // 2
    KEYS = [min((i + 1) * P, T) for i in range(NT)]
    S_OFF = [P * i * (i + 1) // 2 for i in range(NT)]
    PT_OFF = [sum(TP - P * jj for jj in range(j)) for j in range(NT)]
    PW = S_OFF[-1] + TP
    SCORE_SCALE = 1.0 / (Q_SCALE * Q_SCALE * math.sqrt(D))
    LOG_P = math.log(P_SCALE)

    with ExitStack() as ctx:
        def sb(name, shape, dt=F32):
            return ctx.enter_context(nc.sbuf_tensor(name, shape, dt))

        def sem(name):
            return ctx.enter_context(nc.semaphore(name))

        h = sb("h", [P, B, NT, C])
        w_qkv = sb("w_qkv", [P, 2, 3, NC, E, D], F16)
        w_o = sb("w_o", [P, 2, E * C], F16)
        w_tok = sb("w_tok", [P, 2, NC, C], F16)
        w_sim = sb("w_sim", [P, NC, 2, E], F16)
        ident = sb("ident", [P, P])
        ident16 = sb("ident16", [P, P], F16)
        causal = sb("causal", [P, TP])
        lower = sb("lower", [P, E, E])
        sig = sb("sig", [P, E])
        p_half = sb("p_half", [P, NT])
        m_half = sb("m_half", [P, NT])
        ones = sb("ones", [P, P])
        log_p = sb("log_p", [P, 1])
        region_a = sb("region_a", [P, max(B * C, 3 * NT * TP + PW)])
        region_b = sb("region_b", [P, 4 * NT * C])

        def part(region, start, *dims):
            flat = region[:, start:start + math.prod(dims)]
            names = "abcd"[:len(dims)]
            sizes = {k: n for k, n in zip(names[1:], dims[1:])}
            return flat.rearrange(f"p ({' '.join(names)}) -> p {' '.join(names)}", **sizes)

        read_add = part(region_a, 0, B, C)

        xin = sb("xin", [P, 2, NT, C])
        xinT = sb("xinT", [P, 2, 2, NC, TP], F16)
        pre = sb("pre", [P, 2, NT, C])

        stats = [sb(f"stats{n}", [P, NT, 6]) for n in (1, 2)]
        moments = [sb(f"moments{n}", [P, NT, 2]) for n in (1, 2)]
        small = [sb(f"small{n}", [P, 6, NT]) for n in (1, 2)]
        xs = [part(region_b, n * NT * C, NT, C) for n in (0, 1)]
        xhl = [sb(f"xhl{n}", [P, 2, NT, C], F16) for n in (1, 2)]
        xT = [sb(f"xT{n}", [P, 2, NC, TP], F16) for n in (1, 2)]
        rnorm_row = sb("rnorm_row", [P, TP])
        inv_norms = part(region_a, 0, NT, TP)
        cosine = part(region_a, NT * TP, NT, T)
        exp1 = part(region_a, 2 * NT * TP, NT, T)
        exp1_hl = sb("exp1_hl", [P, 2, NT, TP], F16)
        sum1 = sb("sum1", [P, NT])
        sum1_scaled = sb("sum1_scaled", [P, NT])
        inv_sum1 = sb("inv_sum1", [P, NT])
        hx_scaled = part(region_b, 2 * NT * C, NT, C)
        hx = part(region_b, 3 * NT * C, NT, C)

        logit_parts = sb("logit_parts", [P, NT, 2 * E])
        lg = sb("lg", [P, 10, NT, E])
        cmp = sb("cmp", [P, 4, NT, E * E])
        row3 = sb("row3", [P, 6, NT])
        mask16 = sb("mask16", [P, NT, E], F16)
        maskT = sb("maskT", [E, TP], F16)
        mask_all = sb("mask_all", [P, E, TP], F16)
        route_w = sb("route_w", [P, B, NT, E])
        xm = sb("xm", [P, E, 2 * NC, TP], F16)

        qT = sb("qT", [P, 2, TP], F16)
        kT = sb("kT", [P, 2, TP], F16)
        vT = sb("vT", [P, 2, TP], F16)
        v_tok = sb("v_tok", [P, 2, NT, D], F16)
        scores = region_a[:, 3 * NT * TP:3 * NT * TP + PW]
        row_max = sb("row_max", [P, NT])
        neg_max = sb("neg_max", [P, NT])
        exp2 = sb("exp2", [P, PW])
        exp2_hl = sb("exp2_hl", [P, 2, PW], F16)
        sum2 = sb("sum2", [P, NT])
        sum2_scaled = sb("sum2_scaled", [P, NT])
        inv_sum2 = sb("inv_sum2", [P, NT])
        pT = sb("pT", [P, 2, PW], F16)
        aoT = sb("aoT", [P, 2, TP], F16)
        out_w = sb("out_w", [P, NT, E])

        stage = xm[:, :, :, :].rearrange("p e m t -> p (e m t)")[:, 0:2 * (3 * NC * E * D)].bitcast(F32)
        stage_qkv = stage.rearrange("p (m c e d) -> p m c e d", m=3, c=NC, e=E)
        stage_o = region_b[:, 0:E * C]
        stage_tok = part(region_b, E * C, 2, NC, C)
        stage_sim = sb("stage_sim", [P, 4, NC, E])
        sim_norm = sb("sim_norm", [P, 4, E])
        gate_tmp = sb("gate_tmp", [P, 3, E])
        read_x = sb("read_x", [B, C])
        read_xT = sb("read_xT", [P, NC, B])
        read_bias = sb("read_bias", [B, C])
        read_row = sb("read_row", [B, C])

        d_read = nc.dram_tensor("d_read", [B * C], F32, kind="Internal").ap()
        d_rnorm = nc.dram_tensor("d_rnorm", [B, TP], F32, kind="Internal").ap()
        d_mask = nc.dram_tensor("d_mask", [B, E * TP], F16, kind="Internal").ap()

        bank = [ctx.enter_context(nc.psum_tensor(f"bank{i}", [P, 512], F32)) for i in range(8)]
        qkv_bank = [bank[0], bank[1], bank[0]]
        out_bank = [bank[2], bank[3]]
        work = [bank[4], bank[5]]
        turn = [bank[6], bank[7]]

        def as16(b, n):
            return b[:, 0:n // 2].bitcast(F16)

        s_w_loaded = sem("w_loaded")
        s_wo_loaded = sem("wo_loaded")
        s_tok_loaded = sem("tok_loaded")
        s_small_loaded = sem("small_loaded")
        s_read_stored = sem("read_stored")
        s_read_loaded = sem("read_loaded")
        s_consts = sem("consts")
        s_zeroed = sem("zeroed")
        s_setup_pe = sem("setup_pe")
        s_weigh_pool = sem("weigh_pool")
        s_setup_dve = sem("setup_dve")
        s_setup_pool = sem("setup_pool")
        s_wsplit_hi = sem("wsplit_hi")
        s_wsplit_lo = sem("wsplit_lo")
        s_x_loaded0 = sem("x_loaded0")
        s_x_loaded1 = sem("x_loaded1")
        s_in_turned = sem("in_turned")
        s_in_hi = sem("in_hi")
        s_in_lo = sem("in_lo")
        s_tok_done = sem("tok_done")
        s_pre_ready = sem("pre_ready")
        s_h_ready = sem("h_ready")
        s_stats1 = sem("stats1")
        s_moments1 = sem("moments1")
        s_scale1 = sem("scale1")
        s_rnorm1 = sem("rnorm1")
        s_xs1 = sem("xs1")
        s_hi1 = sem("hi1")
        s_lo1 = sem("lo1")
        s_turned1_hi = sem("turned1_hi")
        s_turned1_lo = sem("turned1_lo")
        s_T1_hi = sem("T1_hi")
        s_T1_lo = sem("T1_lo")
        s_rn_stored = sem("rn_stored")
        s_rn_loaded = sem("rn_loaded")
        s_invn_ready = sem("invn_ready")
        s_dots_done = sem("dots_done")
        s_cos_ready = sem("cos_ready")
        s_exp1_full = sem("exp1_full")
        s_exp1_hi = sem("exp1_hi")
        s_exp1_lo = sem("exp1_lo")
        s_sum1_s = sem("sum1_s")
        s_sum1_i = sem("sum1_i")
        s_att_done = sem("att_done")
        s_hx_s = sem("hx_s")
        s_hx_ready = sem("hx_ready")
        s_h2_ready = sem("h2_ready")
        s_stats2 = sem("stats2")
        s_moments2 = sem("moments2")
        s_scale2 = sem("scale2")
        s_xs2 = sem("xs2")
        s_hi2 = sem("hi2")
        s_lo2 = sem("lo2")
        s_turned2_hi = sem("turned2_hi")
        s_turned2_lo = sem("turned2_lo")
        s_T2_hi = sem("T2_hi")
        s_T2_lo = sem("T2_lo")
        s_logits_done = sem("logits_done")
        s_logits_out = sem("logits_out")
        s_routed_dve = sem("routed_dve")
        s_route_pool = sem("route_pool")
        s_route_dve = sem("route_dve")
        s_route_exp = sem("route_exp")
        s_mask_turned = sem("mask_turned")
        s_mask_row = sem("mask_row")
        s_mask_stored = sem("mask_stored")
        s_mask_loaded = sem("mask_loaded")
        s_xm_ready = sem("xm_ready")
        s_q_done = sem("q_done")
        s_k_done = sem("k_done")
        s_v_done = sem("v_done")
        s_q_hi = sem("q_hi")
        s_q_lo = sem("q_lo")
        s_k_hi = sem("k_hi")
        s_k_lo = sem("k_lo")
        s_v_hi = sem("v_hi")
        s_v_lo = sem("v_lo")
        s_v_turned = sem("v_turned")
        s_v_tok_ready = sem("v_tok_ready")
        s_scores_done = sem("scores_done")
        s_scores_out = sem("scores_out")
        s_negmax_ready = sem("negmax_ready")
        s_exp2_full = sem("exp2_full")
        s_exp2_hi = sem("exp2_hi")
        s_exp2_lo = sem("exp2_lo")
        s_pT_hi_turned = sem("pT_hi_turned")
        s_pT_lo_turned = sem("pT_lo_turned")
        s_pT_hi = sem("pT_hi")
        s_pT_lo = sem("pT_lo")
        s_pv_done = sem("pv_done")
        s_ao_hi = sem("ao_hi")
        s_ao_lo = sem("ao_lo")
        s_sum2_s = sem("sum2_s")
        s_sum2_i = sem("sum2_i")
        s_out_w_ready = sem("out_w_ready")
        s_pair_done = sem("pair_done")
        s_pair_added = sem("pair_added")
        s_pool1 = sem("pool1")
        s_pool2 = sem("pool2")
        s_stored = sem("stored")
        s_pool_passed = sem("pool_passed")
        s_dve_passed = sem("dve_passed")
        s_sp_passed = sem("sp_passed")

        LOADS = 2
        N_SMALL = 16 * 5

        def tok_batches(loop_engine, body):
            body(0, 0, False)
            body(1, 1, False)
            with loop_engine.Fori(2, B - 3, 2) as i:
                body(i, 0, False)
                body(i + 1, 1, False)
            body(B - 2, 0, False)
            body(B - 1, 1, True)

        def pipeline(loop_engine, step):
            step(-1, 0, None, None, None)
            step(0, 1, 0, None, None)
            step(1, 2, 1, 0, None)
            step(2, 3, 2, 1, 0)
            with loop_engine.Fori(3, B - 1) as i:
                step(i, i + 1, i, i - 1, i - 2)
            step(B - 1, None, B - 1, B - 2, B - 3)
            step(B, None, None, B - 1, B - 2)
            step(B + 1, None, None, None, B - 1)

        RP = 17
        RANKED = 12

        def later(b):
            return not isinstance(b, int) or b > 0

        block = ctx.enter_context(nc.Block())

        @block.sync
        def _(sp):
            def load(b, par, waits):
                if waits:
                    sp.wait_ge(s_in_turned, (b - 1) * NC).then_inc(s_sp_passed, 1)
                sem_in = s_x_loaded1 if par else s_x_loaded0
                sp.dma_start(xin[:, par, 0:NT - 1, :],
                             x[b, 1:1 + (NT - 1) * P, :].rearrange("(t p) c -> p t c", p=P)).then_inc(sem_in, 16)
                sp.dma_start(xin[0:LAST, par, NT - 1, :], x[b, 1 + (NT - 1) * P:T1, :]).then_inc(sem_in, 16)

            sp.dma_start(read_x[:, :], x[:, 0, :]).then_inc(s_small_loaded, 16)
            sp.dma_start(stage_tok[:, :, :, :],
                         tok_w.rearrange("(g c p) n -> p g c n", g=2, c=NC)).then_inc(s_tok_loaded, 16)
            sp.wait_ge(s_zeroed, 1).then_inc(s_sp_passed, 1)
            load(0, 0, False)
            load(1, 1, False)
            sp.dma_start(read_bias[:, :], tok_b.partition_broadcast(B)).then_inc(s_small_loaded, 16)
            sp.dma_start(gate_tmp[:, 0, :], gates.partition_broadcast(P)).then_inc(s_small_loaded, 16)
            for c in range(NC):
                sp.dma_start(stage_sim[:, 0, c, :], sim_matrix[c * P:(c + 1) * P, :]).then_inc(s_small_loaded, 16)
            sp.wait_ge(s_setup_dve, 3).then_inc(s_sp_passed, 1)
            sp.dma_start(d_read.rearrange("(b c) -> b c", c=C), read_row[:, :]).then_inc(s_read_stored, 16)
            sp.wait_ge(s_read_stored, 16).then_inc(s_sp_passed, 1)
            sp.dma_start(read_add[:, :, :].rearrange("p b c -> p (b c)"),
                         d_read.partition_broadcast(P)).then_inc(s_read_loaded, 16)
            with sp.Fori(2, B - 1, 2) as i:
                load(i, 0, True)
                load(i + 1, 1, True)

            def store(n, t):
                sp.wait_ge(s_pair_added, n * NT * E + (t + 1) * E).then_inc(s_sp_passed, 1)
                rows = P if t < NT - 1 else LAST
                sp.dma_start(out[n, t * P:t * P + rows, :], h[0:rows, n, t, :]).then_inc(s_stored, 16)

            def step(_, g, f, m, n):
                if n is not None:
                    store(n, 0)
                if f is not None:
                    sp.wait_ge(s_mask_row, f + 1).then_inc(s_sp_passed, 1)
                    sp.dma_start(d_mask[f, :].rearrange("(e t) -> e t", e=E), maskT[:, :]).then_inc(s_mask_stored, 16)
                    sp.wait_ge(s_mask_stored, 16 * (f + 1)).then_inc(s_sp_passed, 1)
                    if later(f):
                        sp.wait_ge(s_xm_ready, E * f).then_inc(s_sp_passed, 1)
                    sp.dma_start(mask_all[:, :, :].rearrange("p e t -> p (e t)"),
                                 d_mask[f, :].partition_broadcast(P)).then_inc(s_mask_loaded, 16)
                if g is not None:
                    sp.wait_ge(s_rnorm1, g + 1).then_inc(s_sp_passed, 1)
                    sp.dma_start(d_rnorm[g, :].rearrange("(p t) -> p t", p=P), small[0][:, 5, :]).then_inc(s_rn_stored, 16)
                    sp.wait_ge(s_rn_stored, 16 * (g + 1)).then_inc(s_sp_passed, 1)
                    if later(g):
                        sp.wait_ge(s_invn_ready, NT * g).then_inc(s_sp_passed, 1)
                    sp.dma_start(rnorm_row[:, :], d_rnorm[g, :].partition_broadcast(P)).then_inc(s_rn_loaded, 16)
                if n is not None:
                    for t in range(1, NT):
                        store(n, t)

            pipeline(sp, step)
            sp.wait_ge(s_stored, 16 * NT * B).then_inc(s_sp_passed, 1)

        @block.gpsimd
        def _(pool):
            g = nc.gpsimd
            g.memset(ident[:, :], 0.0).then_inc(s_setup_pool, 1)
            pool.wait_ge(s_setup_pool, 1).then_inc(s_pool_passed, 1)
            g.affine_select(out=ident[:, :], in_=ident[:, :], compare_op=ALU.not_equal, fill=1.0, base=0,
                            pattern=[[-1, P]], channel_multiplier=1).then_inc(s_setup_pool, 1)
            pool.wait_ge(s_setup_pool, 2).then_inc(s_pool_passed, 1)
            g.tensor_copy(ident16[:, :], ident[:, :]).then_inc(s_consts, 1)
            g.memset(ones[:, :], 1.0)
            g.memset(p_half[:, :], 0.5)
            g.memset(m_half[:, :], -0.5)
            g.memset(log_p[:, :], LOG_P)
            g.memset(causal[:, :], 0.0)
            for b in (qT, kT, vT, aoT):
                g.memset(b[:, :, :], 0.0)
            g.memset(exp2_hl[:, :, :], 0.0)
            g.memset(exp1_hl[:, :, :, :], 0.0)
            g.memset(lower[:, :, :], 1.0).then_inc(s_setup_pool, 1)
            pool.wait_ge(s_setup_pool, 3).then_inc(s_pool_passed, 1)
            g.affine_select(out=causal[:, TP - P:TP], in_=causal[:, TP - P:TP], compare_op=ALU.is_ge, fill=MASKED,
                            base=0, pattern=[[-1, P]], channel_multiplier=1)
            g.affine_select(out=lower[:, :, :], in_=lower[:, :, :], compare_op=ALU.is_gt, fill=0.0,
                            base=0, pattern=[[1, E], [-1, E]], channel_multiplier=0).then_inc(s_consts, 1)
            pool.wait_ge(s_setup_dve, 5).then_inc(s_pool_passed, 1)
            g.tensor_tensor(sim_norm[:, 1, :], sim_norm[:, 0, :],
                            p_half[:, 0:1].broadcast_to([P, E]), ALU.pow).then_inc(s_setup_pool, 1)
            def norm_rows(n, b, floor):
                sm, v, chain = small[n], moments[n][:, :, 1], (s_pool1, s_pool2)[n]
                per = 5
                pool.wait_ge((s_moments1, s_moments2)[n], NT * (b + 1)).then_inc(s_pool_passed, 1)
                g.tensor_scalar(sm[:, 0, :], v, LN_EPS, None, ALU.add).then_inc(chain, 1)
                pool.wait_ge(chain, per * b + 1).then_inc(s_pool_passed, 1)
                g.tensor_tensor(sm[:, 1, :], sm[:, 0, :], m_half[:, :], ALU.pow).then_inc(chain, 1)
                pool.wait_ge(chain, per * b + 2).then_inc(s_pool_passed, 1)
                g.tensor_scalar(sm[:, 4, :], sm[:, 1, :], LN_SCALE, None, ALU.mult).then_inc((s_scale1, s_scale2)[n], 1)
                g.tensor_tensor(sm[:, 2, :], v, sm[:, 1, :], ALU.mult).then_inc(chain, 1)
                pool.wait_ge(chain, per * b + 3).then_inc(s_pool_passed, 1)
                g.tensor_tensor(sm[:, 3, :], sm[:, 2, :], sm[:, 1, :], ALU.mult).then_inc(chain, 1)
                pool.wait_ge(chain, per * b + 4).then_inc(s_pool_passed, 1)
                g.tensor_scalar(sm[:, 2, :], sm[:, 3, :], float(C), floor, ALU.mult, ALU.max).then_inc(chain, 1)
                pool.wait_ge(chain, per * b + 5).then_inc(s_pool_passed, 1)
                if n == 0 and later(b):
                    pool.wait_ge(s_rn_stored, 16 * b).then_inc(s_pool_passed, 1)
                    pool.wait_ge(s_invn_ready, NT * b).then_inc(s_pool_passed, 1)
                g.tensor_tensor(sm[:, 5, :], sm[:, 2, :], m_half[:, :], ALU.pow).then_inc(
                    s_rnorm1 if n == 0 else s_route_pool, 1)

            def low(n, b):
                pool.wait_ge((s_hi1, s_hi2)[n], b + 1).then_inc(s_pool_passed, 1)
                if later(b):
                    pool.wait_ge((s_att_done, s_turned2_lo)[n], (NT, 1)[n] * b).then_inc(s_pool_passed, 1)
                g.tensor_tensor(xhl[n][:, 1, :, :], xs[n][:, :, :], xhl[n][:, 0, :, :],
                                ALU.subtract).then_inc((s_lo1, s_lo2)[n], 1)


            def route(b):
                at = [1]

                def after(ins):
                    ins.then_inc(s_route_pool, 1)
                    at[0] += 1
                    pool.wait_ge(s_route_pool, RP * b + at[0]).then_inc(s_pool_passed, 1)

                L, M, GT = lg[:, 2, :, :], lg[:, 3, :, :], cmp[:, 0, :, :]
                pool.wait_ge(s_logits_out, b + 1).then_inc(s_pool_passed, 1)
                after(g.tensor_tensor(lg[:, 0, :, :], logit_parts[:, :, 0:E], logit_parts[:, :, E:2 * E], ALU.add))
                after(g.tensor_tensor(lg[:, 1, :, :], lg[:, 0, :, :],
                                      small[1][:, 5, :].unsqueeze(2).broadcast_to([P, NT, E]), ALU.mult))
                after(g.tensor_scalar(lg[:, 1, :, :], lg[:, 1, :, :], 1.0 / (LN_SCALE * LN_SCALE), None, ALU.mult))
                after(g.tensor_tensor(L, lg[:, 1, :, :], sig[:, :].unsqueeze(1).broadcast_to([P, NT, E]), ALU.subtract))
                after(g.tensor_scalar(M, L, 0.0, None, ALU.is_gt))
                after(g.tensor_scalar(lg[:, 4, :, :], L, 0.0, None, ALU.max))
                for t in range(NT):
                    mine = L[:, t, :].unsqueeze(2).broadcast_to([P, E, E])
                    others = L[:, t, :].unsqueeze(1).broadcast_to([P, E, E])
                    last = g.tensor_tensor(cmp[:, 0, t, :].rearrange("p (a b) -> p a b", a=E), others, mine,
                                           ALU.subtract)
                after(last)
                after(g.tensor_scalar(cmp[:, 1, :, :], cmp[:, 0, :, :], 0.0, None, ALU.is_gt))
                after(g.tensor_scalar(cmp[:, 2, :, :], cmp[:, 0, :, :], 0.0, None, ALU.is_equal))
                after(g.tensor_tensor(cmp[:, 3, :, :], cmp[:, 2, :, :],
                                      lower[:, :, :].rearrange("p a b -> p (a b)").unsqueeze(1).broadcast_to([P, NT, E * E]),
                                      ALU.mult))
                after(g.tensor_tensor(cmp[:, 0, :, :], cmp[:, 3, :, :], cmp[:, 1, :, :], ALU.add))
                assert at[0] == RANKED
                pool.wait_ge(s_route_dve, 4 * b + 2).then_inc(s_pool_passed, 1)
                after(g.tensor_scalar(lg[:, 6, :, :], lg[:, 5, :, :], 2.0, None, ALU.is_lt))
                after(g.tensor_scalar(row3[:, 1, :], row3[:, 0, :], 0.0, None, ALU.is_equal))
                after(g.tensor_tensor(lg[:, 7, :, :], lg[:, 6, :, :],
                                      row3[:, 1, :].unsqueeze(2).broadcast_to([P, NT, E]), ALU.mult))
                after(g.tensor_tensor(lg[:, 8, :, :], lg[:, 7, :, :], M, ALU.add))
                if later(b):
                    pool.wait_ge(s_mask_turned, b).then_inc(s_pool_passed, 1)
                after(g.tensor_copy(mask16[:, :, :], lg[:, 8, :, :]))
                assert at[0] == RP

            def route_weights(b):
                at = [0]
                per = 6

                def after(ins):
                    ins.then_inc(s_weigh_pool, 1)
                    at[0] += 1
                    pool.wait_ge(s_weigh_pool, per * b + at[0]).then_inc(s_pool_passed, 1)

                mask = lg[:, 8, :, :]
                after(g.tensor_tensor(lg[:, 9, :, :], lg[:, 4, :, :], mask, ALU.mult))
                after(g.tensor_scalar(lg[:, 7, :, :], mask, -1.0, 1e9, ALU.add, ALU.mult))
                after(g.tensor_tensor(lg[:, 9, :, :], lg[:, 9, :, :], lg[:, 7, :, :], ALU.add))
                pool.wait_ge(s_route_dve, 4 * b + 3).then_inc(s_pool_passed, 1)
                after(g.tensor_tensor(lg[:, 6, :, :], lg[:, 9, :, :],
                                      row3[:, 2, :].unsqueeze(2).broadcast_to([P, NT, E]), ALU.subtract))
                pool.wait_ge(s_route_dve, 4 * b + 4).then_inc(s_pool_passed, 1)
                after(g.tensor_tensor(lg[:, 9, :, :], lg[:, 7, :, :],
                                      row3[:, 4, :].unsqueeze(2).broadcast_to([P, NT, E]), ALU.mult))
                after(g.tensor_tensor(route_w[:, b, :, :], lg[:, 9, :, :], mask, ALU.mult))
                assert at[0] == per

            def step(i, g1, f, m, n):
                if n is not None:
                    pool.wait_ge(s_scores_out, NT * (n + 1)).then_inc(s_pool_passed, 1)
                    if later(n):
                        pool.wait_ge(s_exp2_hi, NT * n).then_inc(s_pool_passed, 1)
                    g.tensor_scalar(neg_max[:, :], row_max[:, :], -SCORE_SCALE, LOG_P,
                                    ALU.mult, ALU.add).then_inc(s_negmax_ready, 1)
                if f is not None:
                    if later(f):
                        pool.wait_ge(s_h2_ready, NT * f).then_inc(s_pool_passed, 1)
                    g.tensor_scalar(hx_scaled[:, :, :], xs[0][:, :, :], 1.0 / LN_SCALE, None, ALU.mult).then_inc(s_hx_s, 1)
                    pool.wait_ge(s_hx_s, f + 1).then_inc(s_pool_passed, 1)
                    g.tensor_tensor(hx[:, :, :], hx_scaled[:, :, :], h[:, f, :, :], ALU.add).then_inc(s_hx_ready, 1)
                if n is not None:
                    pool.wait_ge(s_exp2_hi, NT * (n + 1)).then_inc(s_pool_passed, 1)
                    if later(n):
                        pool.wait_ge(s_pT_lo_turned, n).then_inc(s_pool_passed, 1)
                    for i in range(NT):
                        sl = slice(S_OFF[i], S_OFF[i] + KEYS[i])
                        last = g.tensor_tensor(exp2_hl[:, 1, sl], exp2[:, sl], exp2_hl[:, 0, sl], ALU.subtract)
                    last.then_inc(s_exp2_lo, 1)
                if f is not None:
                    for t in range(NT):
                        pool.wait_ge(s_exp1_hi, NT * f + t + 1).then_inc(s_pool_passed, 1)
                        g.tensor_tensor(exp1_hl[:, 1, t, 0:T], exp1[:, t, :], exp1_hl[:, 0, t, 0:T],
                                        ALU.subtract).then_inc(s_exp1_lo, 1)
                    norm_rows(1, f, NORM_EPS * NORM_EPS)
                    low(1, f)
                    route(f)
                if g1 is not None:
                    norm_rows(0, g1, 1e-38)
                    low(0, g1)
                if f is not None:
                    route_weights(f)

            pool.wait_ge(s_h_ready, B).then_inc(s_pool_passed, 1)
            pool.wait_ge(s_setup_dve, 9).then_inc(s_pool_passed, 1)
            pipeline(pool, step)

        @block.scalar
        def _(act):
            a = nc.scalar

            for n, w in enumerate((q_proj, k_proj, v_proj)):
                for c in range(NC):
                    act.dma_start(stage_qkv[:, n, c, :, :],
                                  w[:, c * P:(c + 1) * P, :].rearrange("e p d -> p e d")).then_inc(s_w_loaded, 16)
            act.dma_start(stage_o[:, :].rearrange("p (e c) -> p e c", e=E),
                          o_proj.rearrange("e d c -> d e c")).then_inc(s_wo_loaded, 16)
            act.wait_ge(s_tok_loaded, 16)
            a.activation(w_tok[:, 0, :, :], stage_tok[:, 0, :, :], ACT.Copy, scale=W_SCALE).then_inc(s_wsplit_hi, 1)

            def split_in(b, par):
                for c in range(NC):
                    act.wait_ge(s_in_turned, NC * b + c + 1)
                    if c == 0 and (not isinstance(b, int) or b >= 2):
                        act.wait_ge(s_tok_done, b - 1)
                    a.activation(xinT[:, par, 0, c, :], turn[c][:, 0:TP], ACT.Copy, scale=X_SCALE).then_inc(s_in_hi, 1)

            def gelu(b, par):
                act.wait_ge(s_pre_ready, 2 * (b + 1))
                a.activation(h[:, b, 0:NT - 1, :], pre[:, par, 0:NT - 1, :], ACT.Gelu)
                a.activation(h[0:LAST, b, NT - 1, :], pre[0:LAST, par, NT - 1, :], ACT.Gelu).then_inc(s_h_ready, 1)

            def body(b, par, last):
                if not last:
                    split_in(b + 1, 1 - par)
                gelu(b, par)

            split_in(0, 0)
            act.wait_ge(s_zeroed, 2)
            tok_batches(act, body)
            act.wait_ge(s_w_loaded, 16 * 3 * NC)
            for n in range(3):
                a.activation(w_qkv[:, 0, n, :, :, :], stage_qkv[:, n, :, :, :], ACT.Copy,
                             scale=W_SCALE).then_inc(s_wsplit_hi, 1)
            act.wait_ge(s_wo_loaded, 16)
            a.activation(w_o[:, 0, :], stage_o[:, :], ACT.Copy, scale=W_SCALE).then_inc(s_wsplit_hi, 1)
            act.wait_ge(s_setup_dve, 7)
            a.activation(w_sim[:, :, 0, :], stage_sim[:, 3, :, :], ACT.Copy).then_inc(s_wsplit_hi, 1)
            act.wait_ge(s_small_loaded, N_SMALL)
            a.activation(gate_tmp[:, 1, :], gate_tmp[:, 0, :], ACT.Exp, scale=-1.0).then_inc(s_wsplit_hi, 1)

            def high(n, b):
                act.wait_ge((s_xs1, s_xs2)[n], NT * (b + 1))
                if later(b):
                    act.wait_ge((s_att_done, s_turned2_hi)[n], (NT, 1)[n] * b)
                a.activation(xhl[n][:, 0, :, :], xs[n][:, :, :], ACT.Copy).then_inc((s_hi1, s_hi2)[n], 1)

            def head_high(dst, src, done, count, ready, waits, scale):
                act.wait_ge(done, count)
                for q, v in waits:
                    act.wait_ge(q, v)
                a.activation(dst[:, 0, 0:T], src[:, 0:T], ACT.Copy, scale=scale).then_inc(ready, 1)

            qkv_out = 1.0 / (LN_SCALE * W_SCALE) * Q_SCALE

            def step(i, g1, f, m, n):
                if n is not None:
                    head_high(vT, qkv_bank[2], s_v_done, n + 1, s_v_hi,
                              [(s_v_turned, n)] if later(n) else [], qkv_out)
                if f is not None:
                    act.wait_ge(s_turned1_hi, f + 1)
                    if later(f):
                        act.wait_ge(s_dots_done, NT * f)
                    a.activation(xT[0][:, 0, :, :].rearrange("p c t -> p (c t)"), as16(turn[0], NC * TP),
                                 ACT.Copy).then_inc(s_T1_hi, 1)
                if n is not None:
                    act.wait_ge(s_negmax_ready, n + 1)
                    if later(n):
                        act.wait_ge(s_pT_lo_turned, n)
                        act.wait_ge(s_sum2_s, n)
                        act.wait_ge(s_exp2_lo, n)
                    for i in range(NT):
                        sl = slice(S_OFF[i], S_OFF[i] + KEYS[i])
                        a.activation(exp2[:, sl], scores[:, sl], ACT.Exp, bias=neg_max[:, i:i + 1],
                                     scale=SCORE_SCALE, accum_out=sum2[:, i:i + 1]).then_inc(s_exp2_full, 1)
                        a.activation(exp2_hl[:, 0, sl], scores[:, sl], ACT.Exp, bias=neg_max[:, i:i + 1],
                                     scale=SCORE_SCALE).then_inc(s_exp2_hi, 1)
                if f is not None:
                    for t in range(NT):
                        act.wait_ge(s_cos_ready, NT * f + t + 1)
                        if t == 0 and later(f):
                            act.wait_ge(s_exp1_lo, NT * f)
                            act.wait_ge(s_att_done, NT * f)
                            act.wait_ge(s_sum1_s, f)
                        a.activation(exp1[:, t, :], cosine[:, t, :], ACT.Exp, bias=log_p[:, :],
                                     scale=1.0 / (LN_SCALE * LN_SCALE),
                                     accum_out=sum1[:, t:t + 1]).then_inc(s_exp1_full, 1)
                        a.activation(exp1_hl[:, 0, t, 0:T], cosine[:, t, :], ACT.Exp, bias=log_p[:, :],
                                     scale=1.0 / (LN_SCALE * LN_SCALE)).then_inc(s_exp1_hi, 1)
                if n is not None:
                    act.wait_ge(s_pT_hi_turned, n + 1)
                    if later(n):
                        act.wait_ge(s_pv_done, n)
                    a.activation(pT[:, 0, :], as16(turn[1], PW), ACT.Copy).then_inc(s_pT_hi, 1)
                if m is not None:
                    head_high(qT, qkv_bank[0], s_q_done, m + 1, s_q_hi,
                              [(s_scores_done, NT * m)] if later(m) else [], qkv_out)
                if n is not None:
                    head_high(aoT, work[1], s_pv_done, n + 1, s_ao_hi,
                              [(s_pair_done, PAIRS * n)] if later(n) else [], 1.0 / (P_SCALE * Q_SCALE))
                if f is not None:
                    high(1, f)
                    act.wait_ge(s_turned2_hi, f + 1)
                    if later(f):
                        act.wait_ge(s_xm_ready, E * f)
                    a.activation(xT[1][:, 0, :, :].rearrange("p c t -> p (c t)"), as16(turn[0], NC * TP),
                                 ACT.Copy).then_inc(s_T2_hi, 1)
                if m is not None:
                    head_high(kT, qkv_bank[1], s_k_done, m + 1, s_k_hi,
                              [(s_scores_done, NT * m)] if later(m) else [], qkv_out)
                if f is not None:
                    act.wait_ge(s_mask_turned, f + 1)
                    if later(f):
                        act.wait_ge(s_mask_stored, 16 * f)
                    a.activation(maskT[:, :], as16(turn[1], TP)[0:E, :], ACT.Copy).then_inc(s_mask_row, 1)
                if g1 is not None:
                    high(0, g1)
                if f is not None:
                    act.wait_ge(s_weigh_pool, 6 * f + 4)
                    a.activation(lg[:, 7, :, :], lg[:, 6, :, :], ACT.Exp).then_inc(s_route_exp, 1)

            act.wait_ge(s_consts, 2)
            pipeline(act, step)

        @block.vector
        def _(dve):
            v = nc.vector

            v.memset(xin[96:P, :, NT - 1, :], 0.0).then_inc(s_zeroed, 1)
            v.memset(h[96:P, :, NT - 1, :], 0.0).then_inc(s_zeroed, 1)
            dve.wait_ge(s_wsplit_hi, 1)
            v.scalar_tensor_tensor(w_tok[:, 1, :, :].rearrange("p c n -> p (c n)"),
                                   stage_tok[:, 0, :, :].rearrange("p c n -> p (c n)"), W_SCALE,
                                   w_tok[:, 0, :, :].rearrange("p c n -> p (c n)"),
                                   ALU.mult, ALU.subtract).then_inc(s_wsplit_lo, 1)
            dve.wait_ge(s_setup_pe, 1)
            v.tensor_copy(read_xT[:, :, :].rearrange("p c b -> p (c b)"), bank[2][:, 0:NC * B]).then_inc(s_setup_dve, 1)
            dve.wait_ge(s_small_loaded, N_SMALL)
            v.tensor_tensor(stage_sim[:, 1, :, :], stage_sim[:, 0, :, :], stage_sim[:, 0, :, :],
                            ALU.mult).then_inc(s_setup_dve, 1)
            dve.wait_ge(s_setup_pe, 2)
            v.tensor_tensor(read_row[:, :], bank[2][0:B, 0:C], read_bias[:, :], ALU.add).then_inc(s_setup_dve, 1)
            dve.wait_ge(s_setup_pe, 3)
            v.memset(gate_tmp[:, 2, :], 1.0).then_inc(s_setup_dve, 1)
            v.tensor_copy(sim_norm[:, 0, :], bank[3][:, 0:E]).then_inc(s_setup_dve, 1)

            def split_low(b, par):
                for c in range(NC):
                    dve.wait_ge(s_in_hi, NC * b + c + 1)
                    v.scalar_tensor_tensor(xinT[:, par, 1, c, :], turn[c][:, 0:TP], X_SCALE, xinT[:, par, 0, c, :],
                                           ALU.mult, ALU.subtract).then_inc(s_in_lo, 1)

            def add_read(b, par):
                dve.wait_ge(s_tok_done, b + 1)
                if not isinstance(b, int) or b >= 2:
                    dve.wait_ge(s_h_ready, b - 1)
                for lo, n, src in ((0, NT - 1, tok_bank[par][0]), (NT - 1, 1, tok_bank[par][1])):
                    v.scalar_tensor_tensor(
                        pre[:, par, lo:lo + n, :], src[:, 0:n * C].rearrange("p (t c) -> p t c", t=n),
                        1.0 / (X_SCALE * W_SCALE), read_add[:, b, :].unsqueeze(1).broadcast_to([P, n, C]),
                        ALU.mult, ALU.add).then_inc(s_pre_ready, 1)

            tok_bank = [[bank[0], bank[1]], [bank[4], bank[5]]]

            def body(b, par, last):
                if not last:
                    split_low(b + 1, 1 - par)
                add_read(b, par)

            split_low(0, 0)
            dve.wait_ge(s_read_loaded, 16)
            tok_batches(dve, body)

            dve.wait_ge(s_setup_pool, 4)
            v.tensor_scalar(sim_norm[:, 2, :], sim_norm[:, 1, :], NORM_EPS, 1.0 / LN_SCALE, ALU.max,
                            ALU.mult).then_inc(s_setup_dve, 1)
            dve.wait_ge(s_setup_dve, 6)
            v.reciprocal(sim_norm[:, 3, :], sim_norm[:, 2, :]).then_inc(s_routed_dve, 1)
            dve.wait_ge(s_routed_dve, 1)
            v.tensor_tensor(stage_sim[:, 3, :, :], stage_sim[:, 0, :, :],
                            sim_norm[:, 3, :].unsqueeze(1).broadcast_to([P, NC, E]), ALU.mult).then_inc(s_setup_dve, 1)
            for n in range(3):
                dve.wait_ge(s_wsplit_hi, n + 2)
                v.scalar_tensor_tensor(w_qkv[:, 1, n, :, :, :].rearrange("p c e d -> p (c e d)"),
                                       stage_qkv[:, n, :, :, :].rearrange("p c e d -> p (c e d)"), W_SCALE,
                                       w_qkv[:, 0, n, :, :, :].rearrange("p c e d -> p (c e d)"),
                                       ALU.mult, ALU.subtract).then_inc(s_wsplit_lo, 1)
            dve.wait_ge(s_wsplit_hi, 5)
            v.scalar_tensor_tensor(w_o[:, 1, :], stage_o[:, :], W_SCALE, w_o[:, 0, :],
                                   ALU.mult, ALU.subtract).then_inc(s_wsplit_lo, 1)
            dve.wait_ge(s_wsplit_hi, 6)
            v.tensor_tensor(w_sim[:, :, 1, :], stage_sim[:, 3, :, :], w_sim[:, :, 0, :],
                            ALU.subtract).then_inc(s_wsplit_lo, 1)
            dve.wait_ge(s_wsplit_hi, 7)
            v.tensor_scalar(gate_tmp[:, 2, :], gate_tmp[:, 1, :], 1.0, None, ALU.add).then_inc(s_setup_dve, 1)
            dve.wait_ge(s_setup_dve, 8)
            v.reciprocal(sig[:, :], gate_tmp[:, 2, :]).then_inc(s_setup_dve, 1)

            def norm_stats(n, b):
                st, mo = (s_stats1, s_stats2)[n], (s_moments1, s_moments2)[n]
                for t in range(NT):
                    v.bn_stats(stats[n][:, t, :], h[:, b, t, :]).then_inc(st, 1)
                for t in range(NT):
                    dve.wait_ge(st, NT * b + t + 1).then_inc(s_dve_passed, 1)
                    v.bn_aggr(moments[n][:, t, :], stats[n][:, t, :]).then_inc(mo, 1)

            def norm_apply(n, b):
                dve.wait_ge((s_scale1, s_scale2)[n], b + 1)
                if later(b):
                    dve.wait_ge((s_lo1, s_lo2)[n], b)
                if n == 0 and later(b):
                    dve.wait_ge(s_hx_ready, b).then_inc(s_dve_passed, 1)
                for t in range(NT):
                    v.tensor_scalar(xs[n][:, t, :], h[:, b, t, :], moments[n][:, t, 0:1], small[n][:, 4, t:t + 1],
                                    ALU.subtract, ALU.mult).then_inc((s_xs1, s_xs2)[n], 1)

            def head_low(dst, src, hi, count, ready, scale):
                dve.wait_ge(hi, count)
                v.scalar_tensor_tensor(dst[:, 1, 0:T], src[:, 0:T], scale, dst[:, 0, 0:T],
                                       ALU.mult, ALU.subtract).then_inc(ready, 1)

            qkv_out = 1.0 / (LN_SCALE * W_SCALE) * Q_SCALE

            def add_pair(n, p):
                t, e0 = p // (E // 2), 2 * (p % (E // 2))
                dve.wait_ge(s_pair_done, PAIRS * n + p + 1)
                for k in range(2):
                    if k or e0:
                        dve.wait_ge(s_pair_added, NT * E * n + 2 * p + k)
                    v.scalar_tensor_tensor(h[:, n, t, :], out_bank[p % 2][:, k * C:(k + 1) * C],
                                           out_w[:, t, e0 + k:e0 + k + 1], h[:, n, t, :],
                                           ALU.mult, ALU.add).then_inc(s_pair_added, 1)

            def step(i, g1, f, m, n):
                if n is not None:
                    head_low(vT, qkv_bank[2], s_v_hi, n + 1, s_v_lo, qkv_out)
                if f is not None:
                    dve.wait_ge(s_turned1_lo, f + 1)
                    v.tensor_copy(xT[0][:, 1, :, :].rearrange("p c t -> p (c t)"),
                                  as16(turn[1], NC * TP)).then_inc(s_T1_lo, 1)
                if n is not None:
                    for i in range(NT):
                        dve.wait_ge(s_scores_done, NT * n + i + 1).then_inc(s_dve_passed, 1)
                        if i == 0 and later(n):
                            dve.wait_ge(s_exp2_hi, NT * n).then_inc(s_dve_passed, 1)
                            dve.wait_ge(s_negmax_ready, n).then_inc(s_dve_passed, 1)
                        v.tensor_tensor_reduce(scores[:, S_OFF[i]:S_OFF[i] + KEYS[i]], work[i % 2][:, 0:KEYS[i]],
                                               causal[:, TP - P - i * P:TP - P - i * P + KEYS[i]], 1.0, -3e38,
                                               ALU.add, ALU.max, row_max[:, i:i + 1]).then_inc(s_scores_out, 1)
                if f is not None:
                    dve.wait_ge(s_rn_loaded, 16 * (f + 1)).then_inc(s_dve_passed, 1)
                    for t in range(NT):
                        v.tensor_scalar(inv_norms[:, t, :].rearrange("p (a b) -> p a b", a=NT),
                                        rnorm_row[:, :].rearrange("p (b a) -> p a b", a=NT), small[0][:, 5, t:t + 1],
                                        1.0 / COS_EPS, ALU.mult, ALU.min).then_inc(s_invn_ready, 1)
                    for t in range(NT):
                        dve.wait_ge(s_invn_ready, NT * f + t + 1)
                        dve.wait_ge(s_dots_done, NT * f + t + 1)
                        if t == 0 and later(f):
                            dve.wait_ge(s_exp1_hi, NT * f)
                        v.tensor_tensor(cosine[:, t, :], work[t % 2][:, 0:T], inv_norms[:, t, 0:T],
                                        ALU.mult).then_inc(s_cos_ready, 1)
                if n is not None:
                    dve.wait_ge(s_v_turned, n + 1)
                    if later(n):
                        dve.wait_ge(s_pv_done, n)
                    v.tensor_copy(v_tok[:, :, :, :].rearrange("p a t d -> p (a t d)"),
                                  as16(turn[0], 2 * NT * D)).then_inc(s_v_tok_ready, 1)
                if f is not None:
                    dve.wait_ge(s_exp1_full, NT * (f + 1))
                    v.tensor_scalar(sum1_scaled[:, :], sum1[:, :], LN_SCALE, None, ALU.mult).then_inc(s_sum1_s, 1)
                    dve.wait_ge(s_sum1_s, f + 1)
                    v.reciprocal(inv_sum1[:, :], sum1_scaled[:, :]).then_inc(s_sum1_i, 1)
                if n is not None:
                    dve.wait_ge(s_pT_lo_turned, n + 1)
                    v.tensor_copy(pT[:, 1, :], as16(turn[0], PW)).then_inc(s_pT_lo, 1)
                if f is not None:
                    dve.wait_ge(s_sum1_i, f + 1).then_inc(s_dve_passed, 1)
                    dve.wait_ge(s_hx_ready, f + 1).then_inc(s_dve_passed, 1)
                    for t in range(NT):
                        dve.wait_ge(s_att_done, NT * f + t + 1)
                        v.scalar_tensor_tensor(h[:, f, t, :], work[(t + 1) % 2][:, 0:C], inv_sum1[:, t:t + 1],
                                               hx[:, t, :], ALU.mult, ALU.add).then_inc(s_h2_ready, 1)
                    dve.wait_ge(s_h2_ready, NT * (f + 1)).then_inc(s_dve_passed, 1)
                    norm_stats(1, f)
                if m is not None:
                    head_low(qT, qkv_bank[0], s_q_hi, m + 1, s_q_lo, qkv_out)
                if n is not None:
                    head_low(aoT, work[1], s_ao_hi, n + 1, s_ao_lo, 1.0 / (P_SCALE * Q_SCALE))
                    v.tensor_scalar(sum2_scaled[:, :], sum2[:, :], W_SCALE / P_SCALE, None,
                                    ALU.mult).then_inc(s_sum2_s, 1)
                    dve.wait_ge(s_sum2_s, n + 1)
                    v.reciprocal(inv_sum2[:, :], sum2_scaled[:, :]).then_inc(s_sum2_i, 1)
                    dve.wait_ge(s_sum2_i, n + 1)
                    v.tensor_tensor(out_w[:, :, :], route_w[:, n, :, :],
                                    inv_sum2[:, :].unsqueeze(2).broadcast_to([P, NT, E]),
                                    ALU.mult).then_inc(s_out_w_ready, 1)
                    dve.wait_ge(s_out_w_ready, n + 1)
                if f is not None:
                    norm_apply(1, f)
                if n is not None:
                    for p in range(0, 3):
                        add_pair(n, p)
                if f is not None:
                    dve.wait_ge(s_turned2_lo, f + 1)
                    v.tensor_copy(xT[1][:, 1, :, :].rearrange("p c t -> p (c t)"),
                                  as16(turn[1], NC * TP)).then_inc(s_T2_lo, 1)
                if g1 is not None:
                    norm_stats(0, g1)
                if n is not None:
                    add_pair(n, 3)
                if f is not None:
                    dve.wait_ge(s_logits_done, f + 1)
                    v.tensor_copy(logit_parts[:, :, :].rearrange("p t e -> p (t e)"),
                                  turn[0][:, 0:NT * 2 * E]).then_inc(s_logits_out, 1)
                if n is not None:
                    for p in range(4, 6):
                        add_pair(n, p)
                if f is not None:
                    dve.wait_ge(s_route_pool, RP * f + RANKED)
                    v.tensor_reduce(lg[:, 5, :, :].rearrange("p t e -> p (t e)"),
                                    cmp[:, 0, :, :].rearrange("p t (a b) -> p (t a) b", a=E),
                                    AX_X, ALU.add).then_inc(s_route_dve, 1)
                    v.tensor_reduce(row3[:, 0, :], lg[:, 3, :, :], AX_X, ALU.max).then_inc(s_route_dve, 1)
                if m is not None:
                    head_low(kT, qkv_bank[1], s_k_hi, m + 1, s_k_lo, qkv_out)
                if g1 is not None:
                    norm_apply(0, g1)
                if n is not None:
                    for p in range(6, 8):
                        add_pair(n, p)
                if f is not None:
                    dve.wait_ge(s_weigh_pool, 6 * f + 3)
                    v.tensor_reduce(row3[:, 2, :], lg[:, 9, :, :], AX_X, ALU.max).then_inc(s_route_dve, 1)
                if n is not None:
                    for p in range(8, 10):
                        add_pair(n, p)
                if f is not None:
                    dve.wait_ge(s_route_exp, f + 1)
                    v.tensor_reduce(row3[:, 3, :], lg[:, 7, :, :], AX_X, ALU.add).then_inc(s_routed_dve, 1)
                    dve.wait_ge(s_routed_dve, f + 2)
                    v.reciprocal(row3[:, 4, :], row3[:, 3, :]).then_inc(s_route_dve, 1)
                if n is not None:
                    for p in range(10, 12):
                        add_pair(n, p)
                if f is not None:
                    dve.wait_ge(s_mask_loaded, 16 * (f + 1))
                    dve.wait_ge(s_T2_hi, f + 1)
                    dve.wait_ge(s_T2_lo, f + 1)
                    if later(f):
                        dve.wait_ge(s_v_done, f)
                    for e in range(E):
                        v.tensor_tensor(xm[:, e, :, 0:T],
                                        xT[1][:, :, :, 0:T].rearrange("p a c t -> p (a c) t"),
                                        mask_all[:, e, 0:T].unsqueeze(1).broadcast_to([P, 2 * NC, T]),
                                        ALU.mult).then_inc(s_xm_ready, 1)

            dve.wait_ge(s_h_ready, B)
            dve.wait_ge(s_consts, 2)
            pipeline(dve, step)

        @block.tensor
        def _(pe):
            t_ = nc.tensor
            tok_bank = [[bank[0], bank[1]], [bank[4], bank[5]]]

            pe.wait_ge(s_consts, 1)
            pe.wait_ge(s_small_loaded, N_SMALL)
            for c in range(NC):
                last = t_.transpose(bank[2][:, c * B:(c + 1) * B], read_x[:, c * P:(c + 1) * P], ident[0:B, 0:B])
            last.then_inc(s_setup_pe, 1)
            pe.wait_ge(s_tok_loaded, 16)
            pe.wait_ge(s_setup_dve, 1)
            for c in range(NC):
                last = t_.matmul(bank[2][0:B, 0:C], read_xT[:, c, :], stage_tok[:, 1, c, :],
                                 start=(c == 0), stop=(c == NC - 1))
            last.then_inc(s_setup_pe, 1)
            pe.wait_ge(s_setup_dve, 2)
            pe.wait_ge(s_consts, 2)
            for c in range(NC):
                last = t_.matmul(bank[3][:, 0:E], ones[:, :], stage_sim[:, 1, c, :], start=(c == 0), stop=(c == NC - 1))
            last.then_inc(s_setup_pe, 1)

            def turn_in(b, par):
                pe.wait_ge(s_x_loaded1 if par else s_x_loaded0, 16 * LOADS * (b // 2 + 1) if isinstance(b, int)
                           else (b + (2 - par)) * (8 * LOADS))
                for c in range(NC):
                    if later(b):
                        pe.wait_ge(s_in_lo, NC * (b - 1) + c + 1)
                    for t in range(NT):
                        last = t_.transpose(turn[c][:, t * P:(t + 1) * P], xin[:, par, t, c * P:(c + 1) * P], ident[:, :])
                    last.then_inc(s_in_turned, 1)

            def project(b, par):
                pe.wait_ge(s_in_lo, NC * (b + 1))
                if not isinstance(b, int) or b >= 2:
                    pe.wait_ge(s_pre_ready, 2 * (b - 1))
                for t in range(NT):
                    dst = tok_bank[par][t // 2][:, (t % 2) * C:(t % 2 + 1) * C]
                    k = 0
                    for c in range(NC):
                        for xp, wp in ((0, 0), (0, 1), (1, 0)):
                            last = t_.matmul(dst, xinT[:, par, xp, c, t * P:(t + 1) * P], w_tok[:, wp, c, :],
                                             start=(k == 0), stop=(k == 3 * NC - 1))
                            k += 1
                last.then_inc(s_tok_done, 1)

            def body(b, par, last):
                if not last:
                    turn_in(b + 1, 1 - par)
                project(b, par)

            turn_in(0, 0)
            pe.wait_ge(s_wsplit_lo, 1)
            tok_batches(pe, body)

            def turn_rows(n, b, part, dst, done):
                for c in range(NC):
                    for t in range(NT):
                        last = t_.transpose(as16(dst, NC * TP)[:, c * TP + t * P:c * TP + (t + 1) * P],
                                            xhl[n][:, part, t, c * P:(c + 1) * P], ident16[:, :])
                last.then_inc(done, 1)

            def split_product(dst, left, right, starts, stops, done=None):
                k = 0
                for lp, rp in ((0, 0), (0, 1), (1, 0)):
                    last = t_.matmul(dst, left[lp], right[rp], start=(starts and k == 0), stop=(stops and k == 2),
                                     skip_group_check=True)
                    k += 1
                if done is not None:
                    last.then_inc(done, 1)

            def unit(m, which, e):
                done = (s_q_done, s_k_done, s_v_done)[which]
                if which == 0:
                    pe.wait_ge(s_xm_ready, E * m + e + 1)
                if e == 0:
                    if which == 0 and later(m):
                        pe.wait_ge(s_v_lo, m)
                    if which == 1 and later(m):
                        pe.wait_ge(s_k_lo, m)
                    if which == 2:
                        pe.wait_ge(s_q_lo, m + 1)
                dst = qkv_bank[which][:, 0:T]
                for c in range(NC):
                    split_product(dst, [w_qkv[:, p, which, c, e, :] for p in range(2)],
                                  [xm[:, e, p * NC + c, 0:T] for p in range(2)],
                                  e == 0 and c == 0, e == E - 1 and c == NC - 1,
                                  done if e == E - 1 and c == NC - 1 else None)

            def dots(f, t):
                if t == 0:
                    pe.wait_ge(s_T1_hi, f + 1)
                    pe.wait_ge(s_T1_lo, f + 1)
                if t == 2:
                    pe.wait_ge(s_cos_ready, NT * f + 1)
                for c in range(NC):
                    split_product(work[t % 2][:, 0:T], [xT[0][:, p, c, t * P:(t + 1) * P] for p in range(2)],
                                  [xT[0][:, p, c, 0:T] for p in range(2)], c == 0, c == NC - 1,
                                  s_dots_done if c == NC - 1 else None)

            def attend(f, t):
                if t == 0:
                    pe.wait_ge(s_exp1_lo, NT * (f + 1))
                    pe.wait_ge(s_cos_ready, NT * (f + 1))
                if t == 2:
                    pe.wait_ge(s_h2_ready, NT * f + 1)
                for j in range(NT):
                    split_product(work[(t + 1) % 2][:, 0:C], [exp1_hl[:, p, j, t * P:(t + 1) * P] for p in range(2)],
                                  [xhl[0][:, p, j, :] for p in range(2)], j == 0, j == NT - 1,
                                  s_att_done if j == NT - 1 else None)

            def logits(f):
                pe.wait_ge(s_T2_hi, f + 1)
                pe.wait_ge(s_T2_lo, f + 1)
                for t in range(NT):
                    dst = turn[0][:, t * 2 * E:(t + 1) * 2 * E]
                    for c in range(NC):
                        t_.matmul(dst, xT[1][:, 0, c, t * P:(t + 1) * P], w_sim[:, c, :, :].rearrange("p a e -> p (a e)"),
                                  start=(c == 0), stop=False, skip_group_check=True)
                    for c in range(NC):
                        last = t_.matmul(dst[:, 0:E], xT[1][:, 1, c, t * P:(t + 1) * P], w_sim[:, c, 0, :],
                                         start=False, stop=(c == NC - 1), skip_group_check=True)
                last.then_inc(s_logits_done, 1)

            def turn_mask(f):
                pe.wait_ge(s_route_pool, RP * (f + 1))
                pe.wait_ge(s_T2_lo, f + 1)
                for t in range(NT):
                    last = t_.transpose(as16(turn[1], TP)[0:E, t * P:(t + 1) * P], mask16[:, t, :], ident16[:, :])
                last.then_inc(s_mask_turned, 1)

            def score(n, i):
                if i == 0:
                    pe.wait_ge(s_q_lo, n + 1)
                    pe.wait_ge(s_k_lo, n + 1)
                    pe.wait_ge(s_h2_ready, NT * (n + 2) if not isinstance(n, int) else NT * min(n + 2, B))
                if i == 2:
                    pe.wait_ge(s_scores_out, NT * n + 1)
                split_product(work[i % 2][:, 0:KEYS[i]], [qT[:, p, i * P:(i + 1) * P] for p in range(2)],
                              [kT[:, p, 0:KEYS[i]] for p in range(2)], True, True, s_scores_done)

            def turn_v(n):
                pe.wait_ge(s_v_hi, n + 1)
                pe.wait_ge(s_v_lo, n + 1)
                for p in range(2):
                    for t in range(NT):
                        last = t_.transpose(as16(turn[0], 2 * NT * D)[:, (p * NT + t) * D:(p * NT + t + 1) * D],
                                            vT[:, p, t * P:(t + 1) * P], ident16[:, :])
                last.then_inc(s_v_turned, 1)

            def turn_probs(n):
                pe.wait_ge(s_exp2_hi, NT * (n + 1))
                pe.wait_ge(s_exp2_lo, n + 1)
                pe.wait_ge(s_v_tok_ready, n + 1)
                for p, dst, done in ((0, turn[1], s_pT_hi_turned), (1, turn[0], s_pT_lo_turned)):
                    for i in range(NT):
                        for j in range(i + 1):
                            at = PT_OFF[j] + (i - j) * P
                            last = t_.transpose(as16(dst, PW)[:, at:at + P],
                                                exp2_hl[:, p, S_OFF[i] + j * P:S_OFF[i] + (j + 1) * P], ident16[:, :])
                    last.then_inc(done, 1)

            def probs_v(n):
                pe.wait_ge(s_pT_hi, n + 1)
                pe.wait_ge(s_pT_lo, n + 1)
                for j in range(NT):
                    nq = T - j * P
                    split_product(work[1][:, j * P:T], [v_tok[:, p, j, :] for p in range(2)],
                                  [pT[:, p, PT_OFF[j]:PT_OFF[j] + nq] for p in range(2)], j == 0, j == NT - 1,
                                  s_pv_done if j == NT - 1 else None)

            def pair(n, p):
                t, q = p // (E // 2), p % (E // 2)
                if p == 0:
                    pe.wait_ge(s_ao_hi, n + 1)
                    pe.wait_ge(s_ao_lo, n + 1)
                if p >= 2:
                    pe.wait_ge(s_pair_added, NT * E * n + 2 * (p - 1))
                elif later(n):
                    pe.wait_ge(s_pair_added, NT * E * n - 2 * (1 - p))
                split_product(out_bank[p % 2][:, :], [aoT[:, k, t * P:(t + 1) * P] for k in range(2)],
                              [w_o[:, k, 2 * q * C:(2 * q + 2) * C] for k in range(2)], True, True, s_pair_done)

            def step(i, g1, f, m, n):
                def F(fn, *a):
                    if f is not None:
                        fn(f, *a)

                def M(*us):
                    if m is not None:
                        for u in us:
                            unit(m, u // E, u % E)

                def N(fn, *a):
                    if n is not None:
                        fn(n, *a)

                if f is not None:
                    pe.wait_ge(s_hi1, f + 1)
                    if later(f):
                        pe.wait_ge(s_logits_out, f)
                        pe.wait_ge(s_mask_row, f)
                    turn_rows(0, f, 0, turn[0], s_turned1_hi)
                    pe.wait_ge(s_lo1, f + 1)
                    turn_rows(0, f, 1, turn[1], s_turned1_lo)
                N(score, 0)
                N(score, 1)
                M(0)
                N(score, 2)
                M(1, 2)
                if n is not None and f is not None:
                    pe.wait_ge(s_scores_out, NT * (n + 1))
                F(dots, 0)
                F(dots, 1)
                M(3)
                F(dots, 2)
                if f is not None:
                    pe.wait_ge(s_T1_hi, f + 1)
                elif n == B - 2:
                    pe.wait_ge(s_logits_out, B)
                    pe.wait_ge(s_mask_row, B)
                N(turn_v)
                M(4, 5)
                N(turn_probs)
                M(6)
                for t in range(NT):
                    F(attend, t)
                M(7)
                if f is not None:
                    pe.wait_ge(s_h2_ready, NT * (f + 1))
                N(probs_v)
                M(8)
                N(pair, 0)
                M(9)
                N(pair, 1)
                N(pair, 2)
                M(10)
                if f is not None:
                    pe.wait_ge(s_hi2, f + 1)
                    if n is not None:
                        pe.wait_ge(s_pT_lo, n + 1)
                    turn_rows(1, f, 0, turn[0], s_turned2_hi)
                    pe.wait_ge(s_lo2, f + 1)
                    turn_rows(1, f, 1, turn[1], s_turned2_lo)
                M(11)
                N(pair, 3)
                F(logits)
                M(12)
                N(pair, 4)
                M(13)
                N(pair, 5)
                M(14)
                M(15)
                F(turn_mask)
                N(pair, 6)
                M(16)
                N(pair, 7)
                M(17)
                N(pair, 8)
                M(18)
                N(pair, 9)
                M(19, 20)
                N(pair, 10)
                M(21, 22)
                N(pair, 11)
                M(23)

            pe.wait_ge(s_h_ready, B)
            pe.wait_ge(s_wsplit_lo, 6)
            pipeline(pe, step)


_INS = ['x', 'L0_tok_W', 'L0_tok_b', 'L0_ffn_sim_matrix', 'L0_ffn_gates', 'L0_ffn_q_proj', 'L0_ffn_k_proj',
        'L0_ffn_v_proj', 'L0_ffn_o_proj']


def kernel(**inputs):
    import numpy as _np
    import concourse.bacc as _bacc
    from concourse import mybir as _mybir
    from concourse.bass_utils import run_bass_kernel_spmd as _run

    nc = _bacc.Bacc("TRN2", target_bir_lowering=False, num_devices=1)
    arrays, args = {}, []
    for name in _INS:
        a = _np.ascontiguousarray(inputs[name])
        arrays[f"in_{name}_dram"] = a
        args.append(nc.dram_tensor(f"in_{name}_dram", a.shape, _mybir.dt.from_np(a.dtype), kind="ExternalInput").ap())
    B, T1, C = inputs['x'].shape
    args.append(nc.dram_tensor("out_0_dram", (B, T1 - 1, C), _mybir.dt.from_np(_np.dtype('float32')),
                               kind="ExternalOutput").ap())
    audio_tower_kernel(nc, *args)
    r = _run(nc, [arrays], core_ids=[0])
    return r.results[0]["out_0_dram"]
```

```python
import math
from contextlib import ExitStack

import concourse.bass as bass
from concourse import mybir

P = 128
ALU = mybir.AluOpType
ACT = mybir.ActivationFunctionType
F32 = mybir.dt.float32
F16 = mybir.dt.float16
AX_X = mybir.AxisListType.X

X_SCALE = 2.0 ** 6
LN_SCALE = 2.0 ** 11
W_SCALE = 2.0 ** 8
Q_SCALE = 2.0 ** 4
P_SCALE = 2.0 ** 13
LN_EPS = 1e-5
COS_EPS = 1e-8
NORM_EPS = 1e-12
MASKED = -1e30


def audio_tower_kernel(nc, x, tok_w, tok_b, sim_matrix, gates, q_proj, k_proj, v_proj, o_proj, out):
    B, T1, C = x.shape
    T = T1 - 1
    E, _, D = q_proj.shape
    NT = -(-T // P)
    TP = NT * P
    LAST = T - (NT - 1) * P
    NC = C // P
    PAIRS = NT * E // 2
    KEYS = [min((i + 1) * P, T) for i in range(NT)]
    S_OFF = [P * i * (i + 1) // 2 for i in range(NT)]
    PT_OFF = [sum(TP - P * jj for jj in range(j)) for j in range(NT)]
    PW = S_OFF[-1] + TP
    SCORE_SCALE = 1.0 / (Q_SCALE * Q_SCALE * math.sqrt(D))
    LOG_P = math.log(P_SCALE)

    with ExitStack() as ctx:
        def sb(name, shape, dt=F32):
            return ctx.enter_context(nc.sbuf_tensor(name, shape, dt))

        def sem(name):
            return ctx.enter_context(nc.semaphore(name))

        h = sb("h", [P, B, NT, C])
        w_qkv = sb("w_qkv", [P, 2, 3, NC, E, D], F16)
        w_o = sb("w_o", [P, 2, E * C], F16)
        w_tok = sb("w_tok", [P, 2, NC, C], F16)
        w_sim = sb("w_sim", [P, NC, 2, E], F16)
        ident = sb("ident", [P, P])
        ident16 = sb("ident16", [P, P], F16)
        causal = sb("causal", [P, TP])
        lower = sb("lower", [P, E, E])
        sig = sb("sig", [P, E])
        p_half = sb("p_half", [P, NT])
        m_half = sb("m_half", [P, NT])
        ones = sb("ones", [P, P])
        log_p = sb("log_p", [P, 1])
        region_a = sb("region_a", [P, max(B * C, 3 * NT * TP + PW)])
        region_b = sb("region_b", [P, 4 * NT * C])
        region_c = sb("region_c", [P, 4 * NT * C])

        def part(region, start, *dims):
            flat = region[:, start:start + math.prod(dims)]
            names = "abcd"[:len(dims)]
            sizes = {k: n for k, n in zip(names[1:], dims[1:])}
            return flat.rearrange(f"p ({' '.join(names)}) -> p {' '.join(names)}", **sizes)

        read_add = part(region_a, 0, B, C)

        xin = part(region_c, 0, 2, NT, C)
        xinT = sb("xinT", [P, 2, 2, NC, TP], F16)
        pre = part(region_c, 2 * NT * C, 2, NT, C)

        stats = [sb(f"stats{n}", [P, NT, 6]) for n in (1, 2)]
        moments = [sb(f"moments{n}", [P, NT, 2]) for n in (1, 2)]
        small = [sb(f"small{n}", [P, 6, NT]) for n in (1, 2)]
        xs = [part(region_b, n * NT * C, NT, C) for n in (0, 1)]
        xhl = [sb(f"xhl{n}", [P, 2, NT, C], F16) for n in (1, 2)]
        xT = [sb(f"xT{n}", [P, 2, NC, TP], F16) for n in (1, 2)]
        rnorm_row = sb("rnorm_row", [P, TP])
        inv_norms = part(region_a, 0, NT, TP)
        cosine = part(region_a, NT * TP, NT, T)
        exp1 = part(region_a, 2 * NT * TP, NT, T)
        exp1_hl = sb("exp1_hl", [P, 2, NT, TP], F16)
        sum1 = sb("sum1", [P, NT])
        sum1_scaled = sb("sum1_scaled", [P, NT])
        inv_sum1 = sb("inv_sum1", [P, NT])
        hx_scaled = part(region_b, 2 * NT * C, NT, C)
        hx = part(region_b, 3 * NT * C, NT, C)

        logit_parts = sb("logit_parts", [P, NT, 2 * E])
        lg = sb("lg", [P, 10, NT, E])
        cmp = sb("cmp", [P, 4, NT, E * E])
        row3 = sb("row3", [P, 6, NT])
        mask16 = sb("mask16", [P, NT, E], F16)
        maskT = sb("maskT", [E, TP], F16)
        mask_all = sb("mask_all", [P, E, TP], F16)
        route_w = sb("route_w", [P, B, NT, E])
        xm = sb("xm", [P, E, 2 * NC, TP], F16)

        qT = sb("qT", [P, 2, TP], F16)
        kT = sb("kT", [P, 2, TP], F16)
        vT = sb("vT", [P, 2, TP], F16)
        v_tok = sb("v_tok", [P, 2, NT, D], F16)
        scores = region_a[:, 3 * NT * TP:3 * NT * TP + PW]
        row_max = sb("row_max", [P, NT])
        neg_max = sb("neg_max", [P, NT])
        exp2 = sb("exp2", [P, PW])
        exp2_hl = sb("exp2_hl", [P, 2, PW], F16)
        sum2 = sb("sum2", [P, NT])
        sum2_scaled = sb("sum2_scaled", [P, NT])
        inv_sum2 = sb("inv_sum2", [P, NT])
        pT = sb("pT", [P, 2, PW], F16)
        aoT = sb("aoT", [P, 2, TP], F16)
        out_w = sb("out_w", [P, NT, E])
        prod = part(region_c, 0, 2, E // 2, C)
        prod_sum = part(region_c, E * C, 3, C)

        stage = xm[:, :, :, :].rearrange("p e m t -> p (e m t)")[:, 0:2 * (3 * NC * E * D)].bitcast(F32)
        stage_qkv = stage.rearrange("p (m c e d) -> p m c e d", m=3, c=NC, e=E)
        stage_o = region_b[:, 0:E * C]
        stage_tok = part(region_b, E * C, 2, NC, C)
        stage_sim = sb("stage_sim", [P, 4, NC, E])
        sim_norm = sb("sim_norm", [P, 4, E])
        gate_tmp = sb("gate_tmp", [P, 3, E])
        read_x = sb("read_x", [B, C])
        read_xT = sb("read_xT", [P, NC, B])
        read_bias = sb("read_bias", [B, C])
        read_row = sb("read_row", [B, C])

        d_read = nc.dram_tensor("d_read", [B * C], F32, kind="Internal").ap()
        d_rnorm = nc.dram_tensor("d_rnorm", [B, TP], F32, kind="Internal").ap()
        d_mask = nc.dram_tensor("d_mask", [B, E * TP], F16, kind="Internal").ap()

        bank = [ctx.enter_context(nc.psum_tensor(f"bank{i}", [P, 512], F32)) for i in range(8)]
        qkv_bank = [bank[0], bank[1], bank[5]]
        out_bank = [bank[2], bank[3]]
        work = [bank[4], bank[5]]
        turn = [bank[6], bank[7]]

        def as16(b, n):
            return b[:, 0:n // 2].bitcast(F16)

        s_w_loaded = sem("w_loaded")
        s_wo_loaded = sem("wo_loaded")
        s_tok_loaded = sem("tok_loaded")
        s_small_loaded = sem("small_loaded")
        s_read_stored = sem("read_stored")
        s_read_loaded = sem("read_loaded")
        s_consts = sem("consts")
        s_zeroed = sem("zeroed")
        s_setup_pe = sem("setup_pe")
        s_weigh_pool = sem("weigh_pool")
        s_setup_dve = sem("setup_dve")
        s_setup_pool = sem("setup_pool")
        s_wsplit_hi = sem("wsplit_hi")
        s_wsplit_lo = sem("wsplit_lo")
        s_x_loaded0 = sem("x_loaded0")
        s_x_loaded1 = sem("x_loaded1")
        s_in_turned = sem("in_turned")
        s_in_hi = sem("in_hi")
        s_in_lo = sem("in_lo")
        s_tok_done = sem("tok_done")
        s_pre_ready = sem("pre_ready")
        s_h_ready = sem("h_ready")
        s_stats1 = sem("stats1")
        s_moments1 = sem("moments1")
        s_scale1 = sem("scale1")
        s_rnorm1 = sem("rnorm1")
        s_xs1 = sem("xs1")
        s_hi1 = sem("hi1")
        s_lo1 = sem("lo1")
        s_turned1_hi = sem("turned1_hi")
        s_turned1_lo = sem("turned1_lo")
        s_T1_hi = sem("T1_hi")
        s_T1_lo = sem("T1_lo")
        s_rn_stored = sem("rn_stored")
        s_rn_loaded = sem("rn_loaded")
        s_invn_ready = sem("invn_ready")
        s_dots_done = sem("dots_done")
        s_cos_ready = sem("cos_ready")
        s_exp1_full = sem("exp1_full")
        s_exp1_hi = sem("exp1_hi")
        s_exp1_lo = sem("exp1_lo")
        s_sum1_s = sem("sum1_s")
        s_sum1_i = sem("sum1_i")
        s_att_done = sem("att_done")
        s_hx_s = sem("hx_s")
        s_hx_ready = sem("hx_ready")
        s_h2_ready = sem("h2_ready")
        s_stats2 = sem("stats2")
        s_moments2 = sem("moments2")
        s_scale2 = sem("scale2")
        s_xs2 = sem("xs2")
        s_hi2 = sem("hi2")
        s_lo2 = sem("lo2")
        s_turned2_hi = sem("turned2_hi")
        s_turned2_lo = sem("turned2_lo")
        s_T2_hi = sem("T2_hi")
        s_T2_lo = sem("T2_lo")
        s_logits_done = sem("logits_done")
        s_logits_out = sem("logits_out")
        s_routed_dve = sem("routed_dve")
        s_rnorm2 = sem("rnorm2")
        s_mask_ready = sem("mask_ready")
        s_weigh_dve = sem("weigh_dve")
        s_route_dve = sem("route_dve")
        s_route_exp = sem("route_exp")
        s_mask_turned = sem("mask_turned")
        s_mask_row = sem("mask_row")
        s_mask_stored = sem("mask_stored")
        s_mask_loaded = sem("mask_loaded")
        s_xm_ready = sem("xm_ready")
        s_q_done = sem("q_done")
        s_k_done = sem("k_done")
        s_v_done = sem("v_done")
        s_q_hi = sem("q_hi")
        s_q_lo = sem("q_lo")
        s_k_hi = sem("k_hi")
        s_k_lo = sem("k_lo")
        s_v_hi = sem("v_hi")
        s_v_lo = sem("v_lo")
        s_v_turned = sem("v_turned")
        s_v_tok_ready = sem("v_tok_ready")
        s_scores_done = sem("scores_done")
        s_scores_out = sem("scores_out")
        s_negmax_ready = sem("negmax_ready")
        s_exp2_full = sem("exp2_full")
        s_exp2_hi = sem("exp2_hi")
        s_exp2_lo = sem("exp2_lo")
        s_pT_hi_turned = sem("pT_hi_turned")
        s_pT_lo_turned = sem("pT_lo_turned")
        s_pT_hi = sem("pT_hi")
        s_pT_lo = sem("pT_lo")
        s_pv_done = sem("pv_done")
        s_ao_hi = sem("ao_hi")
        s_ao_lo = sem("ao_lo")
        s_sum2_s = sem("sum2_s")
        s_sum2_i = sem("sum2_i")
        s_out_w_ready = sem("out_w_ready")
        s_pair_done = sem("pair_done")
        s_pair_added = sem("pair_added")
        s_pair_scaled = sem("pair_scaled")
        s_tile_summed = sem("tile_summed")
        s_tile_ready = sem("tile_ready")
        s_pool1 = sem("pool1")
        s_pool2 = sem("pool2")
        s_stored = sem("stored")
        s_pool_passed = sem("pool_passed")
        s_dve_passed = sem("dve_passed")
        s_sp_passed = sem("sp_passed")

        LOADS = 2
        N_SMALL = 16 * 5

        def tok_batches(loop_engine, body):
            body(0, 0, False)
            body(1, 1, False)
            with loop_engine.Fori(2, B - 3, 2) as i:
                body(i, 0, False)
                body(i + 1, 1, False)
            body(B - 2, 0, False)
            body(B - 1, 1, True)

        def pipeline(loop_engine, step):
            step(-1, 0, None, None, None)
            step(0, 1, 0, None, None)
            step(1, 2, 1, 0, None)
            step(2, 3, 2, 1, 0)
            with loop_engine.Fori(3, B - 1) as i:
                step(i, i + 1, i, i - 1, i - 2)
            step(B - 1, None, B - 1, B - 2, B - 3)
            step(B, None, None, B - 1, B - 2)
            step(B + 1, None, None, None, B - 1)

        RP = 8

        def later(b):
            return not isinstance(b, int) or b > 0

        block = ctx.enter_context(nc.Block())

        @block.sync
        def _(sp):
            def load(b, par, waits):
                if waits:
                    sp.wait_ge(s_in_turned, (b - 1) * NC).then_inc(s_sp_passed, 1)
                sem_in = s_x_loaded1 if par else s_x_loaded0
                sp.dma_start(xin[:, par, 0:NT - 1, :],
                             x[b, 1:1 + (NT - 1) * P, :].rearrange("(t p) c -> p t c", p=P)).then_inc(sem_in, 16)
                sp.dma_start(xin[0:LAST, par, NT - 1, :], x[b, 1 + (NT - 1) * P:T1, :]).then_inc(sem_in, 16)

            sp.dma_start(read_x[:, :], x[:, 0, :]).then_inc(s_small_loaded, 16)
            sp.dma_start(stage_tok[:, :, :, :],
                         tok_w.rearrange("(g c p) n -> p g c n", g=2, c=NC)).then_inc(s_tok_loaded, 16)
            sp.wait_ge(s_zeroed, 1).then_inc(s_sp_passed, 1)
            load(0, 0, False)
            load(1, 1, False)
            sp.dma_start(read_bias[:, :], tok_b.partition_broadcast(B)).then_inc(s_small_loaded, 16)
            sp.dma_start(gate_tmp[:, 0, :], gates.partition_broadcast(P)).then_inc(s_small_loaded, 16)
            for c in range(NC):
                sp.dma_start(stage_sim[:, 0, c, :], sim_matrix[c * P:(c + 1) * P, :]).then_inc(s_small_loaded, 16)
            sp.wait_ge(s_setup_dve, 3).then_inc(s_sp_passed, 1)
            sp.dma_start(d_read.rearrange("(b c) -> b c", c=C), read_row[:, :]).then_inc(s_read_stored, 16)
            sp.wait_ge(s_read_stored, 16).then_inc(s_sp_passed, 1)
            sp.dma_start(read_add[:, :, :].rearrange("p b c -> p (b c)"),
                         d_read.partition_broadcast(P)).then_inc(s_read_loaded, 16)
            with sp.Fori(2, B - 1, 2) as i:
                load(i, 0, True)
                load(i + 1, 1, True)

            def store(n, t):
                sp.wait_ge(s_tile_ready, n * NT + t + 1).then_inc(s_sp_passed, 1)
                rows = P if t < NT - 1 else LAST
                sp.dma_start(out[n, t * P:t * P + rows, :], h[0:rows, n, t, :]).then_inc(s_stored, 16)

            def step(i, g, f, m, n):
                if g is not None:
                    sp.wait_ge(s_rnorm1, g + 1).then_inc(s_sp_passed, 1)
                    sp.dma_start(d_rnorm[g, :].rearrange("(p t) -> p t", p=P), small[0][:, 5, :]).then_inc(s_rn_stored, 16)
                    sp.wait_ge(s_rn_stored, 16 * (g + 1)).then_inc(s_sp_passed, 1)
                    if later(g):
                        sp.wait_ge(s_invn_ready, NT * g).then_inc(s_sp_passed, 1)
                    sp.dma_start(rnorm_row[:, :], d_rnorm[g, :].partition_broadcast(P)).then_inc(s_rn_loaded, 16)
                if f is not None:
                    sp.wait_ge(s_mask_row, f + 1).then_inc(s_sp_passed, 1)
                    sp.dma_start(d_mask[f, :].rearrange("(e t) -> e t", e=E), maskT[:, :]).then_inc(s_mask_stored, 16)
                    sp.wait_ge(s_mask_stored, 16 * (f + 1)).then_inc(s_sp_passed, 1)
                    if later(f):
                        sp.wait_ge(s_xm_ready, E * f).then_inc(s_sp_passed, 1)
                    sp.dma_start(mask_all[:, :, :].rearrange("p e t -> p (e t)"),
                                 d_mask[f, :].partition_broadcast(P)).then_inc(s_mask_loaded, 16)
                if n is not None:
                    for t in range(NT):
                        store(n, t)

            pipeline(sp, step)
            sp.wait_ge(s_stored, 16 * NT * B).then_inc(s_sp_passed, 1)

        @block.gpsimd
        def _(pool):
            g = nc.gpsimd
            g.memset(ident[:, :], 0.0).then_inc(s_setup_pool, 1)
            pool.wait_ge(s_setup_pool, 1).then_inc(s_pool_passed, 1)
            g.affine_select(out=ident[:, :], in_=ident[:, :], compare_op=ALU.not_equal, fill=1.0, base=0,
                            pattern=[[-1, P]], channel_multiplier=1).then_inc(s_setup_pool, 1)
            pool.wait_ge(s_setup_pool, 2).then_inc(s_pool_passed, 1)
            g.tensor_copy(ident16[:, :], ident[:, :]).then_inc(s_consts, 1)
            g.memset(ones[:, :], 1.0)
            g.memset(p_half[:, :], 0.5)
            g.memset(m_half[:, :], -0.5)
            g.memset(log_p[:, :], LOG_P)
            g.memset(causal[:, :], 0.0)
            for b in (qT, kT, vT, aoT):
                g.memset(b[:, :, :], 0.0)
            g.memset(exp2_hl[:, :, :], 0.0)
            g.memset(exp1_hl[:, :, :, :], 0.0)
            g.memset(lower[:, :, :], 1.0).then_inc(s_setup_pool, 1)
            pool.wait_ge(s_setup_pool, 3).then_inc(s_pool_passed, 1)
            g.affine_select(out=causal[:, TP - P:TP], in_=causal[:, TP - P:TP], compare_op=ALU.is_ge, fill=MASKED,
                            base=0, pattern=[[-1, P]], channel_multiplier=1)
            g.affine_select(out=lower[:, :, :], in_=lower[:, :, :], compare_op=ALU.is_gt, fill=0.0,
                            base=0, pattern=[[1, E], [-1, E]], channel_multiplier=0).then_inc(s_consts, 1)
            pool.wait_ge(s_setup_dve, 5).then_inc(s_pool_passed, 1)
            g.tensor_tensor(sim_norm[:, 1, :], sim_norm[:, 0, :],
                            p_half[:, 0:1].broadcast_to([P, E]), ALU.pow).then_inc(s_setup_pool, 1)
            def norm_rows(n, b, scale, floor):
                sm, v, chain = small[n], moments[n][:, :, 1], (s_pool1, s_pool2)[n]
                per = 5
                pool.wait_ge((s_moments1, s_moments2)[n], NT * (b + 1)).then_inc(s_pool_passed, 1)
                g.tensor_scalar(sm[:, 0, :], v, LN_EPS, None, ALU.add).then_inc(chain, 1)
                pool.wait_ge(chain, per * b + 1).then_inc(s_pool_passed, 1)
                g.tensor_tensor(sm[:, 1, :], sm[:, 0, :], m_half[:, :], ALU.pow).then_inc(chain, 1)
                pool.wait_ge(chain, per * b + 2).then_inc(s_pool_passed, 1)
                g.tensor_scalar(sm[:, 4, :], sm[:, 1, :], LN_SCALE, None, ALU.mult).then_inc((s_scale1, s_scale2)[n], 1)
                g.tensor_tensor(sm[:, 2, :], v, sm[:, 1, :], ALU.mult).then_inc(chain, 1)
                pool.wait_ge(chain, per * b + 3).then_inc(s_pool_passed, 1)
                g.tensor_tensor(sm[:, 3, :], sm[:, 2, :], sm[:, 1, :], ALU.mult).then_inc(chain, 1)
                pool.wait_ge(chain, per * b + 4).then_inc(s_pool_passed, 1)
                g.tensor_scalar(sm[:, 2, :], sm[:, 3, :], C * scale, floor * scale, ALU.mult, ALU.max).then_inc(chain, 1)
                pool.wait_ge(chain, per * b + 5).then_inc(s_pool_passed, 1)
                if n == 0 and later(b):
                    pool.wait_ge(s_rn_stored, 16 * b).then_inc(s_pool_passed, 1)
                    pool.wait_ge(s_invn_ready, NT * b).then_inc(s_pool_passed, 1)
                g.tensor_tensor(sm[:, 5, :], sm[:, 2, :], m_half[:, :], ALU.pow).then_inc((s_rnorm1, s_rnorm2)[n], 1)

            def low_1(b):
                pool.wait_ge(s_hi1, b + 1).then_inc(s_pool_passed, 1)
                if later(b):
                    pool.wait_ge(s_att_done, NT * b).then_inc(s_pool_passed, 1)
                g.tensor_tensor(xhl[0][:, 1, :, :], xs[0][:, :, :], xhl[0][:, 0, :, :],
                                ALU.subtract).then_inc(s_lo1, 1)

            def route_weights(b):
                at = [0]
                per = 6

                def after(ins):
                    ins.then_inc(s_weigh_pool, 1)
                    at[0] += 1
                    pool.wait_ge(s_weigh_pool, per * b + at[0]).then_inc(s_pool_passed, 1)

                mask = lg[:, 8, :, :]
                pool.wait_ge(s_mask_ready, 2 * (b + 1)).then_inc(s_pool_passed, 1)
                after(g.tensor_tensor(lg[:, 9, :, :], lg[:, 4, :, :], mask, ALU.mult))
                after(g.tensor_scalar(lg[:, 7, :, :], mask, -1.0, 1e9, ALU.add, ALU.mult))
                after(g.tensor_tensor(lg[:, 9, :, :], lg[:, 9, :, :], lg[:, 7, :, :], ALU.add))
                pool.wait_ge(s_weigh_dve, 3 * b + 1).then_inc(s_pool_passed, 1)
                after(g.tensor_tensor(lg[:, 6, :, :], lg[:, 9, :, :],
                                      row3[:, 2, :].unsqueeze(2).broadcast_to([P, NT, E]), ALU.subtract))
                pool.wait_ge(s_weigh_dve, 3 * b + 3).then_inc(s_pool_passed, 1)
                after(g.tensor_tensor(lg[:, 9, :, :], lg[:, 7, :, :],
                                      row3[:, 4, :].unsqueeze(2).broadcast_to([P, NT, E]), ALU.mult))
                after(g.tensor_tensor(route_w[:, b, :, :], lg[:, 9, :, :], mask, ALU.mult))
                assert at[0] == per

            def add_tile(n, t):
                buf, per = t % 2, 2 * NT
                pool.wait_ge(s_pair_scaled, PAIRS * n + (t + 1) * (E // 2)).then_inc(s_pool_passed, 1)
                g.tensor_tensor(prod_sum[:, 0:2, :], prod[:, buf, 0:2, :], prod[:, buf, 2:4, :],
                                ALU.add).then_inc(s_tile_summed, 1)
                pool.wait_ge(s_tile_summed, per * n + 2 * t + 1).then_inc(s_pool_passed, 1)
                g.tensor_tensor(prod_sum[:, 2, :], prod_sum[:, 0, :], prod_sum[:, 1, :], ALU.add).then_inc(s_tile_summed, 1)
                pool.wait_ge(s_tile_summed, per * n + 2 * t + 2).then_inc(s_pool_passed, 1)
                pool.wait_ge(s_pair_added, PAIRS * n + (t + 1) * (E // 2)).then_inc(s_pool_passed, 1)
                g.tensor_tensor(h[:, n, t, :], prod_sum[:, 2, :], h[:, n, t, :], ALU.add).then_inc(s_tile_ready, 1)

            def step(i, g1, f, m, n):
                if f is not None:
                    if later(f):
                        pool.wait_ge(s_h2_ready, NT * f).then_inc(s_pool_passed, 1)
                    g.tensor_scalar(hx_scaled[:, :, :], xs[0][:, :, :], 1.0 / LN_SCALE, None, ALU.mult).then_inc(s_hx_s, 1)
                    pool.wait_ge(s_hx_s, f + 1).then_inc(s_pool_passed, 1)
                    g.tensor_tensor(hx[:, :, :], hx_scaled[:, :, :], h[:, f, :, :], ALU.add).then_inc(s_hx_ready, 1)
                if n is not None:
                    if later(n):
                        pool.wait_ge(s_pT_lo_turned, n).then_inc(s_pool_passed, 1)
                    for i in range(NT):
                        pool.wait_ge(s_exp2_hi, NT * n + i + 1).then_inc(s_pool_passed, 1)
                        sl = slice(S_OFF[i], S_OFF[i] + KEYS[i])
                        last = g.tensor_tensor(exp2_hl[:, 1, sl], exp2[:, sl], exp2_hl[:, 0, sl], ALU.subtract)
                    last.then_inc(s_exp2_lo, 1)
                if f is not None:
                    norm_rows(1, f, LN_SCALE ** 4, NORM_EPS * NORM_EPS)
                if g1 is not None:
                    norm_rows(0, g1, 1.0, 1e-38)
                if f is not None:
                    route_weights(f)
                if n is not None:
                    add_tile(n, 0)
                if g1 is not None:
                    low_1(g1)
                    pool.wait_ge(s_rn_loaded, 16 * (g1 + 1)).then_inc(s_pool_passed, 1)
                    if later(g1):
                        pool.wait_ge(s_cos_ready, NT * g1).then_inc(s_pool_passed, 1)
                    for t in range(NT):
                        g.tensor_scalar(inv_norms[:, t, :].rearrange("p (a b) -> p a b", a=NT),
                                        rnorm_row[:, :].rearrange("p (b a) -> p a b", a=NT), small[0][:, 5, t:t + 1],
                                        1.0 / COS_EPS, ALU.mult, ALU.min).then_inc(s_invn_ready, 1)
                if n is not None:
                    for t in range(1, NT):
                        add_tile(n, t)

            pool.wait_ge(s_h_ready, B).then_inc(s_pool_passed, 1)
            pool.wait_ge(s_setup_dve, 9).then_inc(s_pool_passed, 1)
            pipeline(pool, step)

        @block.scalar
        def _(act):
            a = nc.scalar

            for n, w in enumerate((q_proj, k_proj, v_proj)):
                for c in range(NC):
                    act.dma_start(stage_qkv[:, n, c, :, :],
                                  w[:, c * P:(c + 1) * P, :].rearrange("e p d -> p e d")).then_inc(s_w_loaded, 16)
            act.dma_start(stage_o[:, :].rearrange("p (e c) -> p e c", e=E),
                          o_proj.rearrange("e d c -> d e c")).then_inc(s_wo_loaded, 16)
            act.wait_ge(s_tok_loaded, 16)
            a.activation(w_tok[:, 0, :, :], stage_tok[:, 0, :, :], ACT.Copy, scale=W_SCALE).then_inc(s_wsplit_hi, 1)

            def split_in(b, par):
                for c in range(NC):
                    act.wait_ge(s_in_turned, NC * b + c + 1)
                    if c == 0 and (not isinstance(b, int) or b >= 2):
                        act.wait_ge(s_tok_done, b - 1)
                    a.activation(xinT[:, par, 0, c, :], turn[c][:, 0:TP], ACT.Copy, scale=X_SCALE).then_inc(s_in_hi, 1)

            def gelu(b, par):
                act.wait_ge(s_pre_ready, 2 * (b + 1))
                a.activation(h[:, b, 0:NT - 1, :], pre[:, par, 0:NT - 1, :], ACT.Gelu)
                a.activation(h[0:LAST, b, NT - 1, :], pre[0:LAST, par, NT - 1, :], ACT.Gelu).then_inc(s_h_ready, 1)

            def body(b, par, last):
                if not last:
                    split_in(b + 1, 1 - par)
                gelu(b, par)

            split_in(0, 0)
            act.wait_ge(s_zeroed, 2)
            tok_batches(act, body)
            act.wait_ge(s_w_loaded, 16 * 3 * NC)
            for n in range(3):
                a.activation(w_qkv[:, 0, n, :, :, :], stage_qkv[:, n, :, :, :], ACT.Copy,
                             scale=W_SCALE).then_inc(s_wsplit_hi, 1)
            act.wait_ge(s_wo_loaded, 16)
            a.activation(w_o[:, 0, :], stage_o[:, :], ACT.Copy, scale=W_SCALE).then_inc(s_wsplit_hi, 1)
            act.wait_ge(s_setup_dve, 7)
            a.activation(w_sim[:, :, 0, :], stage_sim[:, 3, :, :], ACT.Copy).then_inc(s_wsplit_hi, 1)
            act.wait_ge(s_small_loaded, N_SMALL)
            a.activation(gate_tmp[:, 1, :], gate_tmp[:, 0, :], ACT.Exp, scale=-1.0).then_inc(s_wsplit_hi, 1)

            def high(n, b):
                act.wait_ge((s_xs1, s_xs2)[n], NT * (b + 1))
                if later(b):
                    act.wait_ge((s_att_done, s_turned2_hi)[n], (NT, 1)[n] * b)
                a.activation(xhl[n][:, 0, :, :], xs[n][:, :, :], ACT.Copy).then_inc((s_hi1, s_hi2)[n], 1)

            def head_high(dst, src, done, count, ready, waits, scale):
                act.wait_ge(done, count)
                for q, v in waits:
                    act.wait_ge(q, v)
                a.activation(dst[:, 0, 0:T], src[:, 0:T], ACT.Copy, scale=scale).then_inc(ready, 1)

            qkv_out = 1.0 / (LN_SCALE * W_SCALE) * Q_SCALE

            def step(i, g1, f, m, n):
                def scale_pairs(lo, hi):
                    for p in range(lo, hi) if n is not None else ():
                        t, q = p // (E // 2), p % (E // 2)
                        act.wait_ge(s_pair_done, PAIRS * n + p + 1)
                        if p == 0:
                            act.wait_ge(s_out_w_ready, n + 1)
                        if q == 0 and t == 2:
                            act.wait_ge(s_tile_summed, 2 * NT * n + 1)
                        elif q == 0 and later(n):
                            act.wait_ge(s_tile_summed, 2 * NT * n - (1 if t == 0 else 3))
                        a.activation(prod[:, t % 2, q, :], out_bank[p % 2][:, C:2 * C], ACT.Copy,
                                     scale=out_w[:, t, 2 * q + 1:2 * q + 2]).then_inc(s_pair_scaled, 1)

                if f is not None:
                    for t in range(NT):
                        act.wait_ge(s_cos_ready, NT * f + t + 1)
                        if t == 0 and later(f):
                            act.wait_ge(s_exp1_lo, NT * f)
                            act.wait_ge(s_att_done, NT * f)
                            act.wait_ge(s_sum1_s, f)
                        a.activation(exp1[:, t, :], cosine[:, t, :], ACT.Exp, bias=log_p[:, :],
                                     scale=1.0 / (LN_SCALE * LN_SCALE),
                                     accum_out=sum1[:, t:t + 1]).then_inc(s_exp1_full, 1)
                        a.activation(exp1_hl[:, 0, t, 0:T], cosine[:, t, :], ACT.Exp, bias=log_p[:, :],
                                     scale=1.0 / (LN_SCALE * LN_SCALE)).then_inc(s_exp1_hi, 1)
                if n is not None:
                    act.wait_ge(s_scores_out, NT * (n + 1))
                    a.activation(neg_max[:, :], row_max[:, :], ACT.Identity, bias=log_p[:, :],
                                 scale=-SCORE_SCALE).then_inc(s_negmax_ready, 1)
                    act.wait_ge(s_negmax_ready, n + 1)
                    if later(n):
                        act.wait_ge(s_pT_lo_turned, n)
                        act.wait_ge(s_sum2_s, n)
                        act.wait_ge(s_exp2_lo, n)
                    for i in range(NT):
                        sl = slice(S_OFF[i], S_OFF[i] + KEYS[i])
                        a.activation(exp2[:, sl], scores[:, sl], ACT.Exp, bias=neg_max[:, i:i + 1],
                                     scale=SCORE_SCALE, accum_out=sum2[:, i:i + 1]).then_inc(s_exp2_full, 1)
                        a.activation(exp2_hl[:, 0, sl], scores[:, sl], ACT.Exp, bias=neg_max[:, i:i + 1],
                                     scale=SCORE_SCALE).then_inc(s_exp2_hi, 1)
                    act.wait_ge(s_pT_hi_turned, n + 1)
                    if later(n):
                        act.wait_ge(s_pv_done, n)
                    a.activation(pT[:, 0, :], as16(turn[1], PW), ACT.Copy).then_inc(s_pT_hi, 1)
                    head_high(aoT, out_bank[1], s_pv_done, n + 1, s_ao_hi,
                              [(s_pair_done, PAIRS * n)] if later(n) else [], 1.0 / (P_SCALE * Q_SCALE))
                if f is not None:
                    high(1, f)
                if m is not None:
                    head_high(qT, qkv_bank[0], s_q_done, m + 1, s_q_hi,
                              [(s_scores_done, NT * m)] if later(m) else [], qkv_out)
                if f is not None:
                    act.wait_ge(s_turned2_hi, f + 1)
                    if later(f):
                        act.wait_ge(s_xm_ready, E * f)
                    a.activation(xT[1][:, 0, :, :].rearrange("p c t -> p (c t)"), as16(turn[0], NC * TP),
                                 ACT.Copy).then_inc(s_T2_hi, 1)
                scale_pairs(0, 2)
                if f is not None:
                    act.wait_ge(s_mask_turned, f + 1)
                    if later(f):
                        act.wait_ge(s_mask_stored, 16 * f)
                    a.activation(maskT[:, :], as16(turn[1], TP)[0:E, :], ACT.Copy).then_inc(s_mask_row, 1)
                scale_pairs(2, 3)
                if f is not None:
                    act.wait_ge(s_weigh_pool, 6 * f + 4)
                    a.activation(lg[:, 7, :, :], lg[:, 6, :, :], ACT.Exp).then_inc(s_route_exp, 1)
                scale_pairs(3, 5)
                if g1 is not None:
                    high(0, g1)
                scale_pairs(5, 6)
                if m is not None:
                    head_high(kT, qkv_bank[1], s_k_done, m + 1, s_k_hi,
                              [(s_scores_done, NT * m)] if later(m) else [], qkv_out)
                scale_pairs(6, PAIRS)
                if g1 is not None:
                    act.wait_ge(s_turned1_hi, g1 + 1)
                    if later(g1):
                        act.wait_ge(s_dots_done, NT * g1)
                    a.activation(xT[0][:, 0, :, :].rearrange("p c t -> p (c t)"), as16(turn[0], NC * TP),
                                 ACT.Copy).then_inc(s_T1_hi, 1)
                    act.wait_ge(s_turned1_lo, g1 + 1)
                    a.activation(xT[0][:, 1, :, :].rearrange("p c t -> p (c t)"), as16(turn[1], NC * TP),
                                 ACT.Copy).then_inc(s_T1_lo, 1)
                if m is not None:
                    head_high(vT, qkv_bank[2], s_v_done, E * (m + 1), s_v_hi,
                              [(s_v_turned, m)] if later(m) else [], qkv_out)

            act.wait_ge(s_consts, 2)
            pipeline(act, step)

        @block.vector
        def _(dve):
            v = nc.vector

            v.memset(xin[96:P, :, NT - 1, :], 0.0).then_inc(s_zeroed, 1)
            v.memset(h[96:P, :, NT - 1, :], 0.0).then_inc(s_zeroed, 1)
            dve.wait_ge(s_wsplit_hi, 1)
            v.scalar_tensor_tensor(w_tok[:, 1, :, :].rearrange("p c n -> p (c n)"),
                                   stage_tok[:, 0, :, :].rearrange("p c n -> p (c n)"), W_SCALE,
                                   w_tok[:, 0, :, :].rearrange("p c n -> p (c n)"),
                                   ALU.mult, ALU.subtract).then_inc(s_wsplit_lo, 1)
            dve.wait_ge(s_setup_pe, 1)
            v.tensor_copy(read_xT[:, :, :].rearrange("p c b -> p (c b)"), bank[2][:, 0:NC * B]).then_inc(s_setup_dve, 1)
            dve.wait_ge(s_small_loaded, N_SMALL)
            v.tensor_tensor(stage_sim[:, 1, :, :], stage_sim[:, 0, :, :], stage_sim[:, 0, :, :],
                            ALU.mult).then_inc(s_setup_dve, 1)
            dve.wait_ge(s_setup_pe, 2)
            v.tensor_tensor(read_row[:, :], bank[2][0:B, 0:C], read_bias[:, :], ALU.add).then_inc(s_setup_dve, 1)
            dve.wait_ge(s_setup_pe, 3)
            v.memset(gate_tmp[:, 2, :], 1.0).then_inc(s_setup_dve, 1)
            v.tensor_copy(sim_norm[:, 0, :], bank[3][:, 0:E]).then_inc(s_setup_dve, 1)

            def split_low(b, par):
                for c in range(NC):
                    dve.wait_ge(s_in_hi, NC * b + c + 1)
                    v.scalar_tensor_tensor(xinT[:, par, 1, c, :], turn[c][:, 0:TP], X_SCALE, xinT[:, par, 0, c, :],
                                           ALU.mult, ALU.subtract).then_inc(s_in_lo, 1)

            def add_read(b, par):
                dve.wait_ge(s_tok_done, b + 1)
                if not isinstance(b, int) or b >= 2:
                    dve.wait_ge(s_h_ready, b - 1)
                for lo, n, src in ((0, NT - 1, tok_bank[par][0]), (NT - 1, 1, tok_bank[par][1])):
                    v.scalar_tensor_tensor(
                        pre[:, par, lo:lo + n, :], src[:, 0:n * C].rearrange("p (t c) -> p t c", t=n),
                        1.0 / (X_SCALE * W_SCALE), read_add[:, b, :].unsqueeze(1).broadcast_to([P, n, C]),
                        ALU.mult, ALU.add).then_inc(s_pre_ready, 1)

            tok_bank = [[bank[0], bank[1]], [bank[4], bank[5]]]

            def body(b, par, last):
                if not last:
                    split_low(b + 1, 1 - par)
                add_read(b, par)

            split_low(0, 0)
            dve.wait_ge(s_read_loaded, 16)
            tok_batches(dve, body)

            dve.wait_ge(s_setup_pool, 4)
            v.tensor_scalar(sim_norm[:, 2, :], sim_norm[:, 1, :], NORM_EPS, 1.0 / LN_SCALE, ALU.max,
                            ALU.mult).then_inc(s_setup_dve, 1)
            dve.wait_ge(s_setup_dve, 6)
            v.reciprocal(sim_norm[:, 3, :], sim_norm[:, 2, :]).then_inc(s_routed_dve, 1)
            dve.wait_ge(s_routed_dve, 1)
            v.tensor_tensor(stage_sim[:, 3, :, :], stage_sim[:, 0, :, :],
                            sim_norm[:, 3, :].unsqueeze(1).broadcast_to([P, NC, E]), ALU.mult).then_inc(s_setup_dve, 1)
            for n in range(3):
                dve.wait_ge(s_wsplit_hi, n + 2)
                v.scalar_tensor_tensor(w_qkv[:, 1, n, :, :, :].rearrange("p c e d -> p (c e d)"),
                                       stage_qkv[:, n, :, :, :].rearrange("p c e d -> p (c e d)"), W_SCALE,
                                       w_qkv[:, 0, n, :, :, :].rearrange("p c e d -> p (c e d)"),
                                       ALU.mult, ALU.subtract).then_inc(s_wsplit_lo, 1)
            dve.wait_ge(s_wsplit_hi, 5)
            v.scalar_tensor_tensor(w_o[:, 1, :], stage_o[:, :], W_SCALE, w_o[:, 0, :],
                                   ALU.mult, ALU.subtract).then_inc(s_wsplit_lo, 1)
            dve.wait_ge(s_wsplit_hi, 6)
            v.tensor_tensor(w_sim[:, :, 1, :], stage_sim[:, 3, :, :], w_sim[:, :, 0, :],
                            ALU.subtract).then_inc(s_wsplit_lo, 1)
            dve.wait_ge(s_wsplit_hi, 7)
            v.tensor_scalar(gate_tmp[:, 2, :], gate_tmp[:, 1, :], 1.0, None, ALU.add).then_inc(s_setup_dve, 1)
            dve.wait_ge(s_setup_dve, 8)
            v.reciprocal(sig[:, :], gate_tmp[:, 2, :]).then_inc(s_setup_dve, 1)

            def norm_stats(n, b):
                st, mo = (s_stats1, s_stats2)[n], (s_moments1, s_moments2)[n]
                for t in range(NT):
                    v.bn_stats(stats[n][:, t, :], h[:, b, t, :]).then_inc(st, 1)
                for t in range(NT):
                    dve.wait_ge(st, NT * b + t + 1).then_inc(s_dve_passed, 1)
                    v.bn_aggr(moments[n][:, t, :], stats[n][:, t, :]).then_inc(mo, 1)

            def norm_apply(n, b):
                dve.wait_ge((s_scale1, s_scale2)[n], b + 1)
                if later(b):
                    dve.wait_ge((s_lo1, s_lo2)[n], b)
                if n == 0 and later(b):
                    dve.wait_ge(s_hx_ready, b).then_inc(s_dve_passed, 1)
                for t in range(NT):
                    v.tensor_scalar(xs[n][:, t, :], h[:, b, t, :], moments[n][:, t, 0:1], small[n][:, 4, t:t + 1],
                                    ALU.subtract, ALU.mult).then_inc((s_xs1, s_xs2)[n], 1)

            def head_low(dst, src, hi, count, ready, scale):
                dve.wait_ge(hi, count)
                v.scalar_tensor_tensor(dst[:, 1, 0:T], src[:, 0:T], scale, dst[:, 0, 0:T],
                                       ALU.mult, ALU.subtract).then_inc(ready, 1)

            qkv_out = 1.0 / (LN_SCALE * W_SCALE) * Q_SCALE

            def add_pair(n, p):
                t, e0 = p // (E // 2), 2 * (p % (E // 2))
                dve.wait_ge(s_pair_scaled, PAIRS * n + p + 1)
                if e0:
                    dve.wait_ge(s_pair_added, PAIRS * n + p)
                v.scalar_tensor_tensor(h[:, n, t, :], out_bank[p % 2][:, 0:C], out_w[:, t, e0:e0 + 1], h[:, n, t, :],
                                       ALU.mult, ALU.add).then_inc(s_pair_added, 1)

            def route(b):
                at = [0]

                def after(ins):
                    ins.then_inc(s_route_dve, 1)
                    at[0] += 1
                    dve.wait_ge(s_route_dve, RP * b + at[0])

                L, M = lg[:, 2, :, :], lg[:, 3, :, :]
                square = [x.rearrange("p t (a b) -> p t a b", a=E) for x in (cmp[:, k, :, :] for k in range(4))]
                mine = L.unsqueeze(3).broadcast_to([P, NT, E, E])
                others = L.unsqueeze(2).broadcast_to([P, NT, E, E])
                dve.wait_ge(s_logits_done, b + 1)
                v.tensor_copy(logit_parts[:, :, :].rearrange("p t e -> p (t e)"),
                              turn[0][:, 0:NT * 2 * E]).then_inc(s_logits_out, 1)
                dve.wait_ge(s_logits_out, b + 1)
                after(v.tensor_tensor(lg[:, 0, :, :], logit_parts[:, :, 0:E], logit_parts[:, :, E:2 * E], ALU.add))
                dve.wait_ge(s_rnorm2, b + 1)
                after(v.tensor_tensor(lg[:, 1, :, :], lg[:, 0, :, :],
                                      small[1][:, 5, :].unsqueeze(2).broadcast_to([P, NT, E]), ALU.mult))
                if later(b):
                    dve.wait_ge(s_weigh_pool, 6 * b)
                after(v.tensor_tensor(L, lg[:, 1, :, :], sig[:, :].unsqueeze(1).broadcast_to([P, NT, E]), ALU.subtract))
                v.tensor_scalar(M, L, 0.0, None, ALU.is_gt)
                v.tensor_scalar(lg[:, 4, :, :], L, 0.0, None, ALU.max)
                v.tensor_tensor(square[0], others, mine, ALU.is_gt)
                after(v.tensor_tensor(square[1], others, mine, ALU.is_equal))
                v.tensor_reduce(row3[:, 0, :], M, AX_X, ALU.max)
                after(v.tensor_tensor(cmp[:, 2, :, :], cmp[:, 1, :, :],
                                      lower[:, :, :].rearrange("p a b -> p (a b)").unsqueeze(1).broadcast_to([P, NT, E * E]),
                                      ALU.mult))
                v.tensor_scalar(row3[:, 1, :], row3[:, 0, :], 0.0, None, ALU.is_equal)
                after(v.tensor_tensor(cmp[:, 3, :, :], cmp[:, 2, :, :], cmp[:, 0, :, :], ALU.add))
                after(v.tensor_reduce(lg[:, 5, :, :].rearrange("p t e -> p (t e)"),
                                      cmp[:, 3, :, :].rearrange("p t (a b) -> p (t a) b", a=E), AX_X, ALU.add))
                after(v.scalar_tensor_tensor(lg[:, 0, :, :], lg[:, 5, :, :], 2.0,
                                             row3[:, 1, :].unsqueeze(2).broadcast_to([P, NT, E]),
                                             ALU.is_lt, ALU.mult))
                if later(b):
                    dve.wait_ge(s_mask_turned, b)
                v.tensor_tensor(mask16[:, :, :], lg[:, 0, :, :], M, ALU.add).then_inc(s_mask_ready, 1)
                v.tensor_tensor(lg[:, 8, :, :], lg[:, 0, :, :], M, ALU.add).then_inc(s_mask_ready, 1)
                assert at[0] == RP

            def mask_tokens(b, e):
                if e == 0:
                    dve.wait_ge(s_mask_loaded, 16 * (b + 1))
                    dve.wait_ge(s_T2_hi, b + 1)
                    dve.wait_ge(s_T2_lo, b + 1)
                if later(b):
                    dve.wait_ge(s_v_done, E * (b - 1) + e + 1)
                v.tensor_tensor(xm[:, e, :, 0:T], xT[1][:, :, :, 0:T].rearrange("p a c t -> p (a c) t"),
                                mask_all[:, e, 0:T].unsqueeze(1).broadcast_to([P, 2 * NC, T]),
                                ALU.mult).then_inc(s_xm_ready, 1)

            def step(i, g1, f, m, n):
                def pairs(a, b):
                    if n is not None:
                        for p in range(a, b):
                            add_pair(n, p)

                if f is not None:
                    for t in range(NT):
                        dve.wait_ge(s_invn_ready, NT * f + t + 1)
                        dve.wait_ge(s_dots_done, NT * f + t + 1)
                        if t == 0 and later(f):
                            dve.wait_ge(s_exp1_hi, NT * f)
                        v.tensor_tensor(cosine[:, t, :], work[t % 2][:, 0:T], inv_norms[:, t, 0:T],
                                        ALU.mult).then_inc(s_cos_ready, 1)
                def exp_low(t):
                    if f is not None:
                        dve.wait_ge(s_exp1_hi, NT * f + t + 1)
                        if t == 0 and later(f):
                            dve.wait_ge(s_att_done, NT * f)
                        v.tensor_tensor(exp1_hl[:, 1, t, 0:T], exp1[:, t, :], exp1_hl[:, 0, t, 0:T],
                                        ALU.subtract).then_inc(s_exp1_lo, 1)

                exp_low(0)
                if n is None:
                    exp_low(1)
                    exp_low(2)
                else:
                    for i in range(NT):
                        if i == NT - 1:
                            exp_low(1)
                            exp_low(2)
                        dve.wait_ge(s_scores_done, NT * n + i + 1).then_inc(s_dve_passed, 1)
                        if i == 0 and later(n):
                            dve.wait_ge(s_exp2_hi, NT * n).then_inc(s_dve_passed, 1)
                            dve.wait_ge(s_negmax_ready, n).then_inc(s_dve_passed, 1)
                        v.tensor_tensor_reduce(scores[:, S_OFF[i]:S_OFF[i] + KEYS[i]], out_bank[i % 2][:, 0:KEYS[i]],
                                               causal[:, TP - P - i * P:TP - P - i * P + KEYS[i]], 1.0, -3e38,
                                               ALU.add, ALU.max, row_max[:, i:i + 1]).then_inc(s_scores_out, 1)
                if f is not None:
                    dve.wait_ge(s_exp1_full, NT * (f + 1))
                    v.tensor_scalar(sum1_scaled[:, :], sum1[:, :], LN_SCALE, None, ALU.mult).then_inc(s_sum1_s, 1)
                if g1 is not None:
                    norm_stats(0, g1)
                if n is not None:
                    dve.wait_ge(s_v_turned, n + 1)
                    if later(n):
                        dve.wait_ge(s_pv_done, n)
                    v.tensor_copy(v_tok[:, :, :, :].rearrange("p a t d -> p (a t d)"),
                                  as16(turn[0], 2 * NT * D)).then_inc(s_v_tok_ready, 1)
                if f is not None:
                    dve.wait_ge(s_sum1_s, f + 1)
                    v.reciprocal(inv_sum1[:, :], sum1_scaled[:, :]).then_inc(s_sum1_i, 1)
                    dve.wait_ge(s_sum1_i, f + 1).then_inc(s_dve_passed, 1)
                    dve.wait_ge(s_hx_ready, f + 1).then_inc(s_dve_passed, 1)
                    for t in range(NT):
                        dve.wait_ge(s_att_done, NT * f + t + 1)
                        v.scalar_tensor_tensor(h[:, f, t, :], work[(t + 1) % 2][:, 0:C], inv_sum1[:, t:t + 1],
                                               hx[:, t, :], ALU.mult, ALU.add).then_inc(s_h2_ready, 1)
                    dve.wait_ge(s_h2_ready, NT * (f + 1)).then_inc(s_dve_passed, 1)
                    norm_stats(1, f)
                if n is not None:
                    dve.wait_ge(s_pT_lo_turned, n + 1)
                    v.tensor_copy(pT[:, 1, :], as16(turn[0], PW)).then_inc(s_pT_lo, 1)
                if f is not None:
                    norm_apply(1, f)
                if n is not None:
                    head_low(aoT, out_bank[1], s_ao_hi, n + 1, s_ao_lo, 1.0 / (P_SCALE * Q_SCALE))
                    v.tensor_scalar(sum2_scaled[:, :], sum2[:, :], W_SCALE / P_SCALE, None,
                                    ALU.mult).then_inc(s_sum2_s, 1)
                if f is not None:
                    dve.wait_ge(s_hi2, f + 1)
                    if later(f):
                        dve.wait_ge(s_turned2_lo, f)
                    v.tensor_tensor(xhl[1][:, 1, :, :], xs[1][:, :, :], xhl[1][:, 0, :, :],
                                    ALU.subtract).then_inc(s_lo2, 1)
                if n is not None:
                    dve.wait_ge(s_sum2_s, n + 1)
                    v.reciprocal(inv_sum2[:, :], sum2_scaled[:, :]).then_inc(s_sum2_i, 1)
                    dve.wait_ge(s_sum2_i, n + 1)
                    v.tensor_tensor(out_w[:, :, :], route_w[:, n, :, :],
                                    inv_sum2[:, :].unsqueeze(2).broadcast_to([P, NT, E]),
                                    ALU.mult).then_inc(s_out_w_ready, 1)
                    dve.wait_ge(s_out_w_ready, n + 1)
                if m is not None:
                    head_low(qT, qkv_bank[0], s_q_hi, m + 1, s_q_lo, qkv_out)
                if f is not None:
                    dve.wait_ge(s_turned2_lo, f + 1)
                    v.tensor_copy(xT[1][:, 1, :, :].rearrange("p c t -> p (c t)"),
                                  as16(turn[1], NC * TP)).then_inc(s_T2_lo, 1)
                pairs(0, 1)
                if f is not None:
                    route(f)
                pairs(1, 3)
                if f is not None:
                    dve.wait_ge(s_weigh_pool, 6 * f + 3)
                    v.tensor_reduce(row3[:, 2, :], lg[:, 9, :, :], AX_X, ALU.max).then_inc(s_weigh_dve, 1)
                pairs(3, 4)
                if f is not None:
                    dve.wait_ge(s_route_exp, f + 1)
                    v.tensor_reduce(row3[:, 3, :], lg[:, 7, :, :], AX_X, ALU.add).then_inc(s_weigh_dve, 1)
                    dve.wait_ge(s_weigh_dve, 3 * f + 2)
                    v.reciprocal(row3[:, 4, :], row3[:, 3, :]).then_inc(s_weigh_dve, 1)
                if g1 is not None:
                    norm_apply(0, g1)
                pairs(4, 6)
                if m is not None:
                    head_low(kT, qkv_bank[1], s_k_hi, m + 1, s_k_lo, qkv_out)
                for e in range(E):
                    if e < 6:
                        pairs(6 + e, 7 + e)
                    if f is not None:
                        mask_tokens(f, e)
                    if e == E - 2 and m is not None:
                        head_low(vT, qkv_bank[2], s_v_hi, m + 1, s_v_lo, qkv_out)

            dve.wait_ge(s_h_ready, B)
            dve.wait_ge(s_consts, 2)
            pipeline(dve, step)

        @block.tensor
        def _(pe):
            t_ = nc.tensor
            tok_bank = [[bank[0], bank[1]], [bank[4], bank[5]]]

            pe.wait_ge(s_consts, 1)
            pe.wait_ge(s_small_loaded, N_SMALL)
            for c in range(NC):
                last = t_.transpose(bank[2][:, c * B:(c + 1) * B], read_x[:, c * P:(c + 1) * P], ident[0:B, 0:B])
            last.then_inc(s_setup_pe, 1)
            pe.wait_ge(s_tok_loaded, 16)
            pe.wait_ge(s_setup_dve, 1)
            for c in range(NC):
                last = t_.matmul(bank[2][0:B, 0:C], read_xT[:, c, :], stage_tok[:, 1, c, :],
                                 start=(c == 0), stop=(c == NC - 1))
            last.then_inc(s_setup_pe, 1)
            pe.wait_ge(s_setup_dve, 2)
            pe.wait_ge(s_consts, 2)
            for c in range(NC):
                last = t_.matmul(bank[3][:, 0:E], ones[:, :], stage_sim[:, 1, c, :], start=(c == 0), stop=(c == NC - 1))
            last.then_inc(s_setup_pe, 1)

            def turn_in(b, par):
                pe.wait_ge(s_x_loaded1 if par else s_x_loaded0, 16 * LOADS * (b // 2 + 1) if isinstance(b, int)
                           else (b + (2 - par)) * (8 * LOADS))
                for c in range(NC):
                    if later(b):
                        pe.wait_ge(s_in_lo, NC * (b - 1) + c + 1)
                    for t in range(NT):
                        last = t_.transpose(turn[c][:, t * P:(t + 1) * P], xin[:, par, t, c * P:(c + 1) * P], ident[:, :])
                    last.then_inc(s_in_turned, 1)

            def project(b, par):
                pe.wait_ge(s_in_lo, NC * (b + 1))
                if not isinstance(b, int) or b >= 2:
                    pe.wait_ge(s_pre_ready, 2 * (b - 1))
                for t in range(NT):
                    dst = tok_bank[par][t // 2][:, (t % 2) * C:(t % 2 + 1) * C]
                    k = 0
                    for c in range(NC):
                        for xp, wp in ((0, 0), (0, 1), (1, 0)):
                            last = t_.matmul(dst, xinT[:, par, xp, c, t * P:(t + 1) * P], w_tok[:, wp, c, :],
                                             start=(k == 0), stop=(k == 3 * NC - 1))
                            k += 1
                last.then_inc(s_tok_done, 1)

            def body(b, par, last):
                if not last:
                    turn_in(b + 1, 1 - par)
                project(b, par)

            turn_in(0, 0)
            pe.wait_ge(s_wsplit_lo, 1)
            tok_batches(pe, body)

            def turn_rows(n, b, part, dst, done):
                for c in range(NC):
                    for t in range(NT):
                        last = t_.transpose(as16(dst, NC * TP)[:, c * TP + t * P:c * TP + (t + 1) * P],
                                            xhl[n][:, part, t, c * P:(c + 1) * P], ident16[:, :])
                last.then_inc(done, 1)

            def split_product(dst, left, right, starts, stops, done=None):
                k = 0
                for lp, rp in ((0, 0), (0, 1), (1, 0)):
                    last = t_.matmul(dst, left[lp], right[rp], start=(starts and k == 0), stop=(stops and k == 2),
                                     skip_group_check=True)
                    k += 1
                if done is not None:
                    last.then_inc(done, 1)

            def unit(m, which, e):
                done = (s_q_done, s_k_done, s_v_done)[which]
                if which == 0:
                    pe.wait_ge(s_xm_ready, E * m + e + 1)
                if e == 0:
                    if which == 0 and later(m):
                        pe.wait_ge(s_q_lo, m)
                    if which == 1 and later(m):
                        pe.wait_ge(s_k_lo, m)
                    if which == 2 and later(m):
                        pe.wait_ge(s_v_lo, m)
                dst = qkv_bank[which][:, 0:T]
                for c in range(NC):
                    split_product(dst, [w_qkv[:, p, which, c, e, :] for p in range(2)],
                                  [xm[:, e, p * NC + c, 0:T] for p in range(2)],
                                  e == 0 and c == 0, e == E - 1 and c == NC - 1,
                                  done if (e == E - 1 or which == 2) and c == NC - 1 else None)

            def dots(f, t, m=None):
                if t == 1 and m is not None and later(m):
                    pe.wait_ge(s_v_lo, m)
                if t == 0:
                    pe.wait_ge(s_T1_hi, f + 1)
                    pe.wait_ge(s_T1_lo, f + 1)
                    if later(f):
                        pe.wait_ge(s_h2_ready, NT * f)
                if t == 2:
                    pe.wait_ge(s_cos_ready, NT * f + 1)
                for c in range(NC):
                    split_product(work[t % 2][:, 0:T], [xT[0][:, p, c, t * P:(t + 1) * P] for p in range(2)],
                                  [xT[0][:, p, c, 0:T] for p in range(2)], c == 0, c == NC - 1,
                                  s_dots_done if c == NC - 1 else None)

            def attend(f, t):
                if t == 0:
                    pe.wait_ge(s_exp1_lo, NT * (f + 1))
                    pe.wait_ge(s_cos_ready, NT * (f + 1))
                if t == 2:
                    pe.wait_ge(s_h2_ready, NT * f + 1)
                for j in range(NT):
                    split_product(work[(t + 1) % 2][:, 0:C], [exp1_hl[:, p, j, t * P:(t + 1) * P] for p in range(2)],
                                  [xhl[0][:, p, j, :] for p in range(2)], j == 0, j == NT - 1,
                                  s_att_done if j == NT - 1 else None)

            def logits(f):
                pe.wait_ge(s_T2_hi, f + 1)
                pe.wait_ge(s_T2_lo, f + 1)
                for t in range(NT):
                    dst = turn[0][:, t * 2 * E:(t + 1) * 2 * E]
                    for c in range(NC):
                        t_.matmul(dst, xT[1][:, 0, c, t * P:(t + 1) * P], w_sim[:, c, :, :].rearrange("p a e -> p (a e)"),
                                  start=(c == 0), stop=False, skip_group_check=True)
                    for c in range(NC):
                        last = t_.matmul(dst[:, 0:E], xT[1][:, 1, c, t * P:(t + 1) * P], w_sim[:, c, 0, :],
                                         start=False, stop=(c == NC - 1), skip_group_check=True)
                last.then_inc(s_logits_done, 1)

            def turn_mask(f):
                pe.wait_ge(s_mask_ready, 2 * (f + 1))
                pe.wait_ge(s_T2_lo, f + 1)
                for t in range(NT):
                    last = t_.transpose(as16(turn[1], TP)[0:E, t * P:(t + 1) * P], mask16[:, t, :], ident16[:, :])
                last.then_inc(s_mask_turned, 1)

            def score(n, i):
                if i == 0:
                    pe.wait_ge(s_q_lo, n + 1)
                    pe.wait_ge(s_k_lo, n + 1)
                    if later(n):
                        pe.wait_ge(s_pair_added, PAIRS * n)
                if i == 2:
                    pe.wait_ge(s_scores_out, NT * n + 1)
                split_product(out_bank[i % 2][:, 0:KEYS[i]], [qT[:, p, i * P:(i + 1) * P] for p in range(2)],
                              [kT[:, p, 0:KEYS[i]] for p in range(2)], True, True, s_scores_done)

            def turn_v(n):
                pe.wait_ge(s_v_hi, n + 1)
                pe.wait_ge(s_v_lo, n + 1)
                for p in range(2):
                    for t in range(NT):
                        last = t_.transpose(as16(turn[0], 2 * NT * D)[:, (p * NT + t) * D:(p * NT + t + 1) * D],
                                            vT[:, p, t * P:(t + 1) * P], ident16[:, :])
                last.then_inc(s_v_turned, 1)

            def turn_probs(n):
                pe.wait_ge(s_exp2_hi, NT * (n + 1))
                pe.wait_ge(s_exp2_lo, n + 1)
                pe.wait_ge(s_v_tok_ready, n + 1)
                for p, dst, done in ((0, turn[1], s_pT_hi_turned), (1, turn[0], s_pT_lo_turned)):
                    for i in range(NT):
                        for j in range(i + 1):
                            at = PT_OFF[j] + (i - j) * P
                            last = t_.transpose(as16(dst, PW)[:, at:at + P],
                                                exp2_hl[:, p, S_OFF[i] + j * P:S_OFF[i] + (j + 1) * P], ident16[:, :])
                    last.then_inc(done, 1)

            def probs_v(n):
                pe.wait_ge(s_pT_hi, n + 1)
                pe.wait_ge(s_pT_lo, n + 1)
                for j in range(NT):
                    nq = T - j * P
                    split_product(out_bank[1][:, j * P:T], [v_tok[:, p, j, :] for p in range(2)],
                                  [pT[:, p, PT_OFF[j]:PT_OFF[j] + nq] for p in range(2)], j == 0, j == NT - 1,
                                  s_pv_done if j == NT - 1 else None)

            def pair(n, p):
                t, q = p // (E // 2), p % (E // 2)
                if p == 0:
                    pe.wait_ge(s_ao_hi, n + 1)
                    pe.wait_ge(s_ao_lo, n + 1)
                if p >= 2:
                    pe.wait_ge(s_pair_added, PAIRS * n + p - 1)
                split_product(out_bank[p % 2][:, :], [aoT[:, k, t * P:(t + 1) * P] for k in range(2)],
                              [w_o[:, k, 2 * q * C:(2 * q + 2) * C] for k in range(2)], True, True, s_pair_done)

            def step(i, g1, f, m, n):
                def F(fn, *a):
                    if f is not None:
                        fn(f, *a)

                def M(*us):
                    if m is not None:
                        for u in us:
                            unit(m, u // E, u % E)

                def N(fn, *a):
                    if n is not None:
                        fn(n, *a)

                M(0)
                F(dots, 0)
                F(dots, 1, m)
                M(1)
                F(dots, 2)
                N(score, 0)
                N(score, 1)
                M(2, 3)
                N(score, 2)
                if f is not None:
                    pe.wait_ge(s_T1_hi, f + 1)
                elif n == B - 2:
                    pe.wait_ge(s_logits_out, B)
                    pe.wait_ge(s_mask_row, B)
                N(turn_v)
                M(4)
                for t in range(NT):
                    F(attend, t)
                M(5)
                N(turn_probs)
                M(6)
                N(probs_v)
                M(7, 8)
                if f is not None:
                    pe.wait_ge(s_hi2, f + 1)
                    if n is not None:
                        pe.wait_ge(s_pT_lo, n + 1)
                    turn_rows(1, f, 0, turn[0], s_turned2_hi)
                M(9)
                if f is not None:
                    pe.wait_ge(s_lo2, f + 1)
                    turn_rows(1, f, 1, turn[1], s_turned2_lo)
                N(pair, 0)
                M(10)
                F(logits)
                N(pair, 1)
                M(11, 12)
                N(pair, 2)
                M(13)
                F(turn_mask)
                N(pair, 3)
                M(14)
                N(pair, 4)
                M(15)
                N(pair, 5)
                for k in range(6):
                    M(16 + k)
                    N(pair, 6 + k)
                if g1 is not None:
                    pe.wait_ge(s_hi1, g1 + 1)
                    if later(g1):
                        pe.wait_ge(s_logits_out, g1)
                        pe.wait_ge(s_mask_row, g1)
                    turn_rows(0, g1, 0, turn[0], s_turned1_hi)
                    pe.wait_ge(s_lo1, g1 + 1)
                    turn_rows(0, g1, 1, turn[1], s_turned1_lo)
                M(22, 23)

            pe.wait_ge(s_h_ready, B)
            pe.wait_ge(s_wsplit_lo, 6)
            pipeline(pe, step)


_INS = ['x', 'L0_tok_W', 'L0_tok_b', 'L0_ffn_sim_matrix', 'L0_ffn_gates', 'L0_ffn_q_proj', 'L0_ffn_k_proj',
        'L0_ffn_v_proj', 'L0_ffn_o_proj']


def kernel(**inputs):
    import numpy as _np
    import concourse.bacc as _bacc
    from concourse import mybir as _mybir
    from concourse.bass_utils import run_bass_kernel_spmd as _run

    nc = _bacc.Bacc("TRN2", target_bir_lowering=False, num_devices=1)
    arrays, args = {}, []
    for name in _INS:
        a = _np.ascontiguousarray(inputs[name])
        arrays[f"in_{name}_dram"] = a
        args.append(nc.dram_tensor(f"in_{name}_dram", a.shape, _mybir.dt.from_np(a.dtype), kind="ExternalInput").ap())
    B, T1, C = inputs['x'].shape
    args.append(nc.dram_tensor("out_0_dram", (B, T1 - 1, C), _mybir.dt.from_np(_np.dtype('float32')),
                               kind="ExternalOutput").ap())
    audio_tower_kernel(nc, *args)
    r = _run(nc, [arrays], core_ids=[0])
    return r.results[0]["out_0_dram"]
```

```python
import math
from contextlib import ExitStack

import concourse.bass as bass
from concourse import mybir

P = 128
ALU = mybir.AluOpType
ACT = mybir.ActivationFunctionType
F32 = mybir.dt.float32
F16 = mybir.dt.float16
AX_X = mybir.AxisListType.X

X_SCALE = 2.0 ** 6
LN_SCALE = 2.0 ** 11
W_SCALE = 2.0 ** 8
R_SCALE = 2.0 ** 4
Q_SCALE = 2.0 ** 4
P_SCALE = 2.0 ** 13
LN_EPS = 1e-5
COS_EPS = 1e-8
NORM_EPS = 1e-12
MASKED = -1e30


def audio_tower_kernel(nc, x, tok_w, tok_b, sim_matrix, gates, q_proj, k_proj, v_proj, o_proj, out):
    B, T1, C = x.shape
    T = T1 - 1
    E, _, D = q_proj.shape
    NT = -(-T // P)
    TP = NT * P
    LAST = T - (NT - 1) * P
    NC = C // P
    PAIRS = NT * E // 2
    KEYS = [min((i + 1) * P, T) for i in range(NT)]
    S_OFF = [P * i * (i + 1) // 2 for i in range(NT)]
    PT_OFF = [sum(TP - P * jj for jj in range(j)) for j in range(NT)]
    PW = S_OFF[-1] + TP
    SCORE_SCALE = 1.0 / (Q_SCALE * Q_SCALE * math.sqrt(D))
    LOG_P = math.log(P_SCALE)

    with ExitStack() as ctx:
        def sb(name, shape, dt=F32):
            return ctx.enter_context(nc.sbuf_tensor(name, shape, dt))

        def sem(name):
            return ctx.enter_context(nc.semaphore(name))

        h = sb("h", [P, B, NT, C])
        w_qkv = sb("w_qkv", [P, 2, 3, NC, E, D], F16)
        w_o = sb("w_o", [P, 2, E * C], F16)
        w_tok = sb("w_tok", [P, 2, NC, C], F16)
        w_sim = sb("w_sim", [P, NC, 2, E], F16)
        ident = sb("ident", [P, P])
        ident16 = sb("ident16", [P, P], F16)
        causal = sb("causal", [P, TP])
        lower = sb("lower", [P, E, E])
        sig = sb("sig", [P, E])
        p_half = sb("p_half", [P, NT])
        m_half = sb("m_half", [P, NT])
        ones = sb("ones", [P, P])
        log_p = sb("log_p", [P, 1])
        region_a = sb("region_a", [P, 3 * NT * TP + PW])
        region_b = sb("region_b", [P, 4 * NT * C])
        region_c = sb("region_c", [P, 2 * NT * C + E * C])

        def part(region, start, *dims):
            flat = region[:, start:start + math.prod(dims)]
            names = "abcd"[:len(dims)]
            sizes = {k: n for k, n in zip(names[1:], dims[1:])}
            return flat.rearrange(f"p ({' '.join(names)}) -> p {' '.join(names)}", **sizes)

        xin = part(region_c, 0, 2, NT, C)
        xinT = sb("xinT", [P, 2, 2, NC, TP], F16)

        stats = [sb(f"stats{n}", [P, NT, 6]) for n in (1, 2)]
        moments = [sb(f"moments{n}", [P, NT, 2]) for n in (1, 2)]
        small = [sb(f"small{n}", [P, 6, NT]) for n in (1, 2)]
        xs = [part(region_b, n * NT * C, NT, C) for n in (0, 1)]
        xhl = [sb(f"xhl{n}", [P, 2, NT, C + 2 * (2 - n)], F16) for n in (1, 2)]
        sum_column = sb("sum_column", [P, NT])
        xT = [sb(f"xT{n}", [P, 2, NC, TP], F16) for n in (1, 2)]
        rnorm_row = sb("rnorm_row", [P, TP])
        inv_norms = part(region_a, 0, NT, TP)
        cosine = part(region_a, NT * TP, NT, T)
        exp1 = part(region_a, 2 * NT * TP, NT, T)
        exp1_hl = sb("exp1_hl", [P, 2, NT, TP], F16)
        inv_sum1 = sb("inv_sum1", [P, NT])
        hx_scaled = part(region_b, 2 * NT * C, NT, C)
        hx = part(region_b, 3 * NT * C, NT, C)
        last_sum = part(region_b, 3 * NT * C, 2, C)

        logit_parts = sb("logit_parts", [P, NT, 2 * E])
        lg = sb("lg", [P, 10, NT, E])
        cmp = sb("cmp", [P, 4, NT, E * E])
        row3 = sb("row3", [P, 6, NT])
        mask16 = sb("mask16", [P, NT, E], F16)
        maskT = sb("maskT", [E, TP], F16)
        mask_all = sb("mask_all", [P, E, TP], F16)
        route_w = sb("route_w", [P, B, NT, E])
        xm = sb("xm", [P, E, 2 * NC, TP], F16)

        qT = sb("qT", [P, 2, TP], F16)
        kT = sb("kT", [P, 2, TP], F16)
        vT = sb("vT", [P, 2, TP], F16)
        v_tok = sb("v_tok", [P, 2, NT, D], F16)
        scores = region_a[:, 3 * NT * TP:3 * NT * TP + PW]
        row_max = sb("row_max", [P, NT])
        neg_max = sb("neg_max", [P, NT])
        exp2 = sb("exp2", [P, PW])
        exp2_hl = sb("exp2_hl", [P, 2, PW], F16)
        sum2 = sb("sum2", [P, NT])
        sum2_scaled = sb("sum2_scaled", [P, NT])
        inv_sum2 = sb("inv_sum2", [P, NT])
        pT = sb("pT", [P, 2, PW], F16)
        aoT = sb("aoT", [P, 2, TP], F16)
        out_w = sb("out_w", [P, NT, E])
        prod = part(region_c, 0, 2, E // 2, C)
        prod_sum = part(region_c, E * C, 3, C)

        stage = xm[:, :, :, :].rearrange("p e m t -> p (e m t)")[:, 0:2 * (3 * NC * E * D)].bitcast(F32)
        stage_qkv = stage.rearrange("p (m c e d) -> p m c e d", m=3, c=NC, e=E)
        w_qkv_hi, w_qkv_lo = (w_qkv[:, k, :, :, :, :].rearrange("p m c e d -> p (m c e d)") for k in range(2))

        def qkv_pieces(flat):
            return flat.rearrange("p (n w) -> p n w", n=3 * NC)

        stage_o = part(region_c, 2 * NT * C, 2, E * C // 2)
        stage_tok = part(region_b, E * C, 2, NC, C)
        stage_sim = sb("stage_sim", [P, 4, NC, E])
        sim_norm = sb("sim_norm", [P, 4, E])
        gate_tmp = sb("gate_tmp", [P, 3, E])
        RR = 32 + B
        read_x = region_b[0:B, E * C // 2:E * C // 2 + C]
        read_bias = region_b[0:RR, E * C // 2 + C:E * C // 2 + 2 * C]
        read_row = region_b[0:RR, E * C // 2 + 2 * C:E * C // 2 + 3 * C]
        read_xT = sb("read_xT", [P, NC, RR])
        read_hl = sb("read_hl", [RR, C], F16)
        pick32 = sb("pick32", [P, B])
        pick = sb("pick", [P, B, 1], F16)

        d_rnorm = nc.dram_tensor("d_rnorm", [B, TP], F32, kind="Internal").ap()
        d_mask = nc.dram_tensor("d_mask", [B, E * TP], F16, kind="Internal").ap()

        bank = [ctx.enter_context(nc.psum_tensor(f"bank{i}", [P, 512], F32)) for i in range(8)]
        qkv_bank = [bank[0], bank[1], bank[5]]
        out_bank = [bank[2], bank[3]]
        work = [bank[4], bank[5]]
        turn = [bank[6], bank[7]]

        att_bank = [bank[5], bank[4], bank[7]]
        last_bank = [bank[4], bank[6], bank[7]]

        def as16(b, n):
            return b[:, 0:n // 2].bitcast(F16)

        s_w_loaded = sem("w_loaded")
        s_wo_loaded = sem("wo_loaded")
        s_tok_loaded = sem("tok_loaded")
        s_small_loaded = sem("small_loaded")
        s_read_loaded = sem("read_loaded")
        s_consts = sem("consts")
        s_zeroed = sem("zeroed")
        s_picked = sem("picked")
        s_setup_pe = sem("setup_pe")
        s_weigh_pool = sem("weigh_pool")
        s_setup_dve = sem("setup_dve")
        s_setup_pool = sem("setup_pool")
        s_tokw_hi = sem("tokw_hi")
        s_tokw_lo = sem("tokw_lo")
        s_w_hi = sem("w_hi")
        s_w_lo = sem("w_lo")
        s_sim_hi = sem("sim_hi")
        s_sim_lo = sem("sim_lo")
        s_gate_exp = sem("gate_exp")
        s_x_loaded0 = sem("x_loaded0")
        s_x_loaded1 = sem("x_loaded1")
        s_in_turned = sem("in_turned")
        s_in_hi = sem("in_hi")
        s_in_lo = sem("in_lo")
        s_tok_first = sem("tok_first")
        s_tok_done = sem("tok_done")
        s_h_first = sem("h_first")
        s_h_ready = sem("h_ready")
        s_stats1 = sem("stats1")
        s_moments1 = sem("moments1")
        s_scale1 = sem("scale1")
        s_rnorm1 = sem("rnorm1")
        s_xs1 = sem("xs1")
        s_hi1 = sem("hi1")
        s_lo1 = sem("lo1")
        s_turned1_hi = sem("turned1_hi")
        s_turned1_lo = sem("turned1_lo")
        s_T1_hi = sem("T1_hi")
        s_T1_lo = sem("T1_lo")
        s_rn_stored = sem("rn_stored")
        s_rn_loaded = sem("rn_loaded")
        s_invn_ready = sem("invn_ready")
        s_dots_done = sem("dots_done")
        s_cos_ready = sem("cos_ready")
        s_exp1_hi = sem("exp1_hi")
        s_exp1_lo = sem("exp1_lo")
        s_exp1_turned = sem("exp1_turned")
        s_exp1_square = sem("exp1_square")
        s_sum1_i = sem("sum1_i")
        s_att_done = sem("att_done")
        s_hx_s = sem("hx_s")
        s_hx_ready = sem("hx_ready")
        s_h2_ready = sem("h2_ready")
        s_stats2 = sem("stats2")
        s_moments2 = sem("moments2")
        s_scale2 = sem("scale2")
        s_xs2 = sem("xs2")
        s_hi2 = sem("hi2")
        s_lo2 = sem("lo2")
        s_turned2_hi = sem("turned2_hi")
        s_turned2_lo = sem("turned2_lo")
        s_T2_hi = sem("T2_hi")
        s_T2_lo = sem("T2_lo")
        s_logits_done = sem("logits_done")
        s_logits_out = sem("logits_out")
        s_routed_dve = sem("routed_dve")
        s_rnorm2 = sem("rnorm2")
        s_mask_ready = sem("mask_ready")
        s_weigh_dve = sem("weigh_dve")
        s_route_dve = sem("route_dve")
        s_route_exp = sem("route_exp")
        s_mask_turned = sem("mask_turned")
        s_mask_row = sem("mask_row")
        s_mask_stored = sem("mask_stored")
        s_mask_loaded = [sem("mask_loaded0"), sem("mask_loaded1")]
        s_xm_ready = sem("xm_ready")
        s_q_done = sem("q_done")
        s_k_done = sem("k_done")
        s_v_done = sem("v_done")
        s_q_hi = sem("q_hi")
        s_q_lo = sem("q_lo")
        s_k_hi = sem("k_hi")
        s_k_lo = sem("k_lo")
        s_v_hi = sem("v_hi")
        s_v_lo = sem("v_lo")
        s_v_turned = sem("v_turned")
        s_v_tok_ready = sem("v_tok_ready")
        s_scores_done = sem("scores_done")
        s_scores_out = sem("scores_out")
        s_negmax_ready = sem("negmax_ready")
        s_exp2_full = sem("exp2_full")
        s_exp2_hi = sem("exp2_hi")
        s_exp2_lo = sem("exp2_lo")
        s_pT_hi_turned = sem("pT_hi_turned")
        s_pT_lo_turned = sem("pT_lo_turned")
        s_pT_hi = sem("pT_hi")
        s_pT_lo = sem("pT_lo")
        s_pv_done = sem("pv_done")
        s_ao_hi = sem("ao_hi")
        s_ao_lo = sem("ao_lo")
        s_sum2_s = sem("sum2_s")
        s_sum2_i = sem("sum2_i")
        s_out_w_ready = sem("out_w_ready")
        s_pair_done = sem("pair_done")
        s_pair_added = sem("pair_added")
        s_pair_scaled = sem("pair_scaled")
        s_tile_summed = sem("tile_summed")
        s_tile_ready = sem("tile_ready")
        s_last_summed = sem("last_summed")
        s_last_ready = sem("last_ready")
        s_pool1 = sem("pool1")
        s_pool2 = sem("pool2")
        s_stored = sem("stored")
        s_pool_passed = sem("pool_passed")
        s_dve_passed = sem("dve_passed")
        s_sp_passed = sem("sp_passed")

        LOADS = 2
        LOOP0, LOOP1 = 3, 3 + 2 * NC

        def looped_slots(loop_engine, slot):
            with loop_engine.Fori(LOOP0, LOOP1 - 1, 2) as i:
                slot(i, 1, i - LOOP0)
                slot(i + 1, 0, i + 1 - LOOP0)

        def pipeline(loop_engine, step):
            step(1, 2, 1, 0, None)
            step(2, 3, 2, 1, 0)
            with loop_engine.Fori(3, B - 1) as i:
                step(i, i + 1, i, i - 1, i - 2)
            step(B - 1, None, B - 1, B - 2, B - 3)
            step(B, None, None, B - 1, B - 2)
            step(B + 1, None, None, None, B - 1)

        RP = 8

        def early(m):
            return isinstance(m, int) and m == 0

        def second(m):
            return isinstance(m, int) and m == 1

        def final(b):
            return isinstance(b, int) and b == B - 1

        def probs_bank(n):
            return qkv_bank[2] if final(n) else out_bank[1]

        def pair_bank(n, p):
            return (out_bank + [bank[0], bank[1]])[p % 4] if final(n) else out_bank[p % 2]

        def later(b):
            return not isinstance(b, int) or b > 0

        block = ctx.enter_context(nc.Block())

        @block.sync
        def _(sp):
            def load(b, par, waits):
                if waits:
                    sp.wait_ge(s_in_turned, (b - 1) * NC).then_inc(s_sp_passed, 1)
                load_whole_tiles(b, par)
                load_rest(b, par)

            def load_whole_tiles(b, par):
                sem_in = s_x_loaded1 if par else s_x_loaded0
                sp.dma_start(xin[:, par, 0:NT - 1, :],
                             x[b, 1:1 + (NT - 1) * P, :].rearrange("(t p) c -> p t c", p=P)).then_inc(sem_in, 16)

            def load_rest(b, par):
                sem_in = s_x_loaded1 if par else s_x_loaded0
                sp.dma_start(xin[0:LAST, par, NT - 1, :], x[b, 1 + (NT - 1) * P:T1, :]).then_inc(sem_in, 16)

            def norms_out(g):
                sp.wait_ge(s_rnorm1, g + 1).then_inc(s_sp_passed, 1)
                sp.dma_start(d_rnorm[g, :].rearrange("(p t) -> p t", p=P), small[0][:, 5, :]).then_inc(s_rn_stored, 16)

            def norms_in(g):
                sp.wait_ge(s_rn_stored, 16 * (g + 1)).then_inc(s_sp_passed, 1)
                if later(g):
                    sp.wait_ge(s_invn_ready, NT * g).then_inc(s_sp_passed, 1)
                sp.dma_start(rnorm_row[:, :], d_rnorm[g, :].partition_broadcast(P)).then_inc(s_rn_loaded, 16)

            def mask_around(f):
                sp.wait_ge(s_mask_row, f + 1).then_inc(s_sp_passed, 1)
                sp.dma_start(d_mask[f, :].rearrange("(e t) -> e t", e=E), maskT[:, :]).then_inc(s_mask_stored, 16)
                sp.wait_ge(s_mask_stored, 16 * (f + 1)).then_inc(s_sp_passed, 1)
                if later(f):
                    sp.wait_ge(s_xm_ready, E * f).then_inc(s_sp_passed, 1)
                for k in range(2):
                    sp.dma_start(mask_all[:, k * (E // 2):(k + 1) * (E // 2), :].rearrange("p e t -> p (e t)"),
                                 d_mask[f, k * (E // 2) * TP:(k + 1) * (E // 2) * TP].partition_broadcast(P)).then_inc(
                                     s_mask_loaded[k], 16)

            load_whole_tiles(0, 0)
            sp.dma_start(stage_tok[:, :, :, :],
                         tok_w.rearrange("(g c p) n -> p g c n", g=2, c=NC)).then_inc(s_tok_loaded, 16)
            sp.wait_ge(s_zeroed, 1).then_inc(s_sp_passed, 1)
            load_rest(0, 0)
            load(1, 1, False)
            load(2, 0, True)
            load(3, 1, True)
            load(4, 0, True)
            load(5, 1, True)
            norms_out(0)
            load(6, 0, True)
            load(7, 1, True)
            norms_in(0)
            with sp.Fori(8, 11, 2) as i:
                load(i, 0, True)
                load(i + 1, 1, True)
            norms_out(1)
            load(12, 0, True)
            norms_in(1)
            for b in range(13, B):
                load(b, b % 2, True)
            mask_around(0)

            def store(n, t):
                if final(n) and t == NT - 1:
                    sp.wait_ge(s_last_ready, 1).then_inc(s_sp_passed, 1)
                else:
                    sp.wait_ge(s_tile_ready, n * NT + t + 1).then_inc(s_sp_passed, 1)
                rows = P if t < NT - 1 else LAST
                sp.dma_start(out[n, t * P:t * P + rows, :], h[0:rows, n, t, :]).then_inc(s_stored, 16)

            def step(i, g, f, m, n):
                if g is not None:
                    norms_out(g)
                    norms_in(g)
                if f is not None:
                    mask_around(f)
                if n is not None:
                    for t in range(NT):
                        store(n, t)

            pipeline(sp, step)
            sp.wait_ge(s_stored, 16 * NT * B).then_inc(s_sp_passed, 1)

        @block.gpsimd
        def _(pool):
            g = nc.gpsimd
            g.memset(ident[:, :], 0.0).then_inc(s_setup_pool, 1)
            pool.wait_ge(s_setup_pool, 1).then_inc(s_pool_passed, 1)
            g.affine_select(out=ident[:, :], in_=ident[:, :], compare_op=ALU.not_equal, fill=1.0, base=0,
                            pattern=[[-1, P]], channel_multiplier=1).then_inc(s_setup_pool, 1)
            pool.wait_ge(s_setup_pool, 2).then_inc(s_pool_passed, 1)
            g.tensor_copy(ident16[:, :], ident[:, :]).then_inc(s_consts, 1)
            g.memset(pick32[:, :], 0.0).then_inc(s_picked, 1)
            pool.wait_ge(s_picked, 1).then_inc(s_pool_passed, 1)
            for n, first in enumerate((0, 32)):
                g.affine_select(out=pick32[:, :], in_=pick32[:, :], compare_op=ALU.not_equal,
                                fill=X_SCALE * W_SCALE / R_SCALE, base=-first, pattern=[[-1, B]],
                                channel_multiplier=1).then_inc(s_picked, 1)
                pool.wait_ge(s_picked, n + 2).then_inc(s_pool_passed, 1)
            g.tensor_copy(pick[:, :, :].rearrange("p b o -> p (b o)"), pick32[:, :]).then_inc(s_picked, 1)
            g.memset(ones[:, :], 1.0)
            g.memset(p_half[:, :], 0.5)
            g.memset(m_half[:, :], -0.5)
            g.memset(log_p[:, :], LOG_P)
            g.memset(causal[:, :], 0.0)
            for b in (qT, kT, vT, aoT):
                g.memset(b[:, :, :], 0.0)
            g.memset(exp2_hl[:, :, :], 0.0)
            g.memset(exp1_hl[:, :, :, :], 0.0)
            g.memset(sum_column[:, :], LN_SCALE)
            g.memset(lower[:, :, :], 1.0).then_inc(s_setup_pool, 1)
            pool.wait_ge(s_setup_pool, 3).then_inc(s_pool_passed, 1)
            g.affine_select(out=causal[:, TP - P:TP], in_=causal[:, TP - P:TP], compare_op=ALU.is_ge, fill=MASKED,
                            base=0, pattern=[[-1, P]], channel_multiplier=1)
            g.affine_select(out=sum_column[:, NT - 1:NT], in_=sum_column[:, NT - 1:NT], compare_op=ALU.is_ge,
                            fill=0.0, base=LAST - 1, pattern=[[0, 1]], channel_multiplier=-1).then_inc(s_setup_pool, 1)
            pool.wait_ge(s_setup_pool, 4).then_inc(s_pool_passed, 1)
            g.tensor_copy(xhl[0][:, 0, :, C:C + 1], sum_column[:, :].unsqueeze(2))
            g.affine_select(out=lower[:, :, :], in_=lower[:, :, :], compare_op=ALU.is_gt, fill=0.0,
                            base=0, pattern=[[1, E], [-1, E]], channel_multiplier=0).then_inc(s_consts, 1)
            pool.wait_ge(s_setup_dve, 7).then_inc(s_pool_passed, 1)
            g.tensor_tensor(sim_norm[:, 1, :], sim_norm[:, 0, :],
                            p_half[:, 0:1].broadcast_to([P, E]), ALU.pow).then_inc(s_setup_pool, 1)
            def norm_rows(n, b, scale, floor):
                sm, v, chain = small[n], moments[n][:, :, 1], (s_pool1, s_pool2)[n]
                per = 5
                pool.wait_ge((s_moments1, s_moments2)[n], NT * (b + 1)).then_inc(s_pool_passed, 1)
                g.tensor_scalar(sm[:, 0, :], v, LN_EPS, None, ALU.add).then_inc(chain, 1)
                pool.wait_ge(chain, per * b + 1).then_inc(s_pool_passed, 1)
                g.tensor_tensor(sm[:, 1, :], sm[:, 0, :], m_half[:, :], ALU.pow).then_inc(chain, 1)
                pool.wait_ge(chain, per * b + 2).then_inc(s_pool_passed, 1)
                g.tensor_scalar(sm[:, 4, :], sm[:, 1, :], LN_SCALE, None, ALU.mult).then_inc((s_scale1, s_scale2)[n], 1)
                g.tensor_tensor(sm[:, 2, :], v, sm[:, 1, :], ALU.mult).then_inc(chain, 1)
                pool.wait_ge(chain, per * b + 3).then_inc(s_pool_passed, 1)
                g.tensor_tensor(sm[:, 3, :], sm[:, 2, :], sm[:, 1, :], ALU.mult).then_inc(chain, 1)
                pool.wait_ge(chain, per * b + 4).then_inc(s_pool_passed, 1)
                g.tensor_scalar(sm[:, 2, :], sm[:, 3, :], C * scale, floor * scale, ALU.mult, ALU.max).then_inc(chain, 1)
                pool.wait_ge(chain, per * b + 5).then_inc(s_pool_passed, 1)
                if n == 0 and later(b):
                    pool.wait_ge(s_rn_stored, 16 * b).then_inc(s_pool_passed, 1)
                    pool.wait_ge(s_invn_ready, NT * b).then_inc(s_pool_passed, 1)
                g.tensor_tensor(sm[:, 5, :], sm[:, 2, :], m_half[:, :], ALU.pow).then_inc((s_rnorm1, s_rnorm2)[n], 1)

            def low_1(b):
                pool.wait_ge(s_hi1, b + 1).then_inc(s_pool_passed, 1)
                if later(b):
                    pool.wait_ge(s_att_done, NT * b).then_inc(s_pool_passed, 1)
                g.tensor_tensor(xhl[0][:, 1, :, 0:C], xs[0][:, :, :], xhl[0][:, 0, :, 0:C],
                                ALU.subtract).then_inc(s_lo1, 1)

            def route_weights(b):
                at = [0]
                per = 6

                def after(ins):
                    ins.then_inc(s_weigh_pool, 1)
                    at[0] += 1
                    pool.wait_ge(s_weigh_pool, per * b + at[0]).then_inc(s_pool_passed, 1)

                mask = lg[:, 8, :, :]
                pool.wait_ge(s_mask_ready, 2 * (b + 1)).then_inc(s_pool_passed, 1)
                after(g.tensor_tensor(lg[:, 9, :, :], lg[:, 4, :, :], mask, ALU.mult))
                after(g.tensor_scalar(lg[:, 7, :, :], mask, -1.0, 1e9, ALU.add, ALU.mult))
                after(g.tensor_tensor(lg[:, 9, :, :], lg[:, 9, :, :], lg[:, 7, :, :], ALU.add))
                pool.wait_ge(s_weigh_dve, 3 * b + 1).then_inc(s_pool_passed, 1)
                after(g.tensor_tensor(lg[:, 6, :, :], lg[:, 9, :, :],
                                      row3[:, 2, :].unsqueeze(2).broadcast_to([P, NT, E]), ALU.subtract))
                pool.wait_ge(s_weigh_dve, 3 * b + 3).then_inc(s_pool_passed, 1)
                after(g.tensor_tensor(lg[:, 9, :, :], lg[:, 7, :, :],
                                      row3[:, 4, :].unsqueeze(2).broadcast_to([P, NT, E]), ALU.mult))
                after(g.tensor_tensor(route_w[:, b, :, :], lg[:, 9, :, :], mask, ALU.mult))
                assert at[0] == per

            def add_tile(n, t):
                buf, per = t % 2, 2 * NT
                pool.wait_ge(s_pair_scaled, PAIRS * n + (t + 1) * (E // 2)).then_inc(s_pool_passed, 1)
                g.tensor_tensor(prod_sum[:, 0:2, :], prod[:, buf, 0:2, :], prod[:, buf, 2:4, :],
                                ALU.add).then_inc(s_tile_summed, 1)
                pool.wait_ge(s_tile_summed, per * n + 2 * t + 1).then_inc(s_pool_passed, 1)
                g.tensor_tensor(prod_sum[:, 2, :], prod_sum[:, 0, :], prod_sum[:, 1, :], ALU.add).then_inc(s_tile_summed, 1)
                pool.wait_ge(s_tile_summed, per * n + 2 * t + 2).then_inc(s_pool_passed, 1)
                pool.wait_ge(s_pair_added, PAIRS * n + (t + 1) * (E // 2)).then_inc(s_pool_passed, 1)
                g.tensor_tensor(h[:, n, t, :], prod_sum[:, 2, :], h[:, n, t, :], ALU.add).then_inc(s_tile_ready, 1)

            def rest_of_residual(f):
                if later(f):
                    pool.wait_ge(s_h2_ready, NT * f).then_inc(s_pool_passed, 1)
                g.tensor_scalar(hx_scaled[:, :, :], xs[0][:, :, :], 1.0 / LN_SCALE, None, ALU.mult).then_inc(s_hx_s, 1)
                pool.wait_ge(s_hx_s, f + 1).then_inc(s_pool_passed, 1)
                g.tensor_tensor(hx[:, :, :], hx_scaled[:, :, :], h[:, f, :, :], ALU.add).then_inc(s_hx_ready, 1)

            def spread_norms(b):
                pool.wait_ge(s_rn_loaded, 16 * (b + 1)).then_inc(s_pool_passed, 1)
                if later(b):
                    pool.wait_ge(s_cos_ready, NT * b).then_inc(s_pool_passed, 1)
                for t in range(NT):
                    g.tensor_scalar(inv_norms[:, t, t * P:TP].rearrange("p (a b) -> p a b", a=NT - t),
                                    rnorm_row[:, :].rearrange("p (b a) -> p a b", a=NT)[:, t:NT, :], small[0][:, 5, t:t + 1],
                                    1.0 / COS_EPS, ALU.mult, ALU.min).then_inc(s_invn_ready, 1)

            def low_probs(n):
                if later(n):
                    pool.wait_ge(s_pT_lo_turned, n).then_inc(s_pool_passed, 1)
                for i in range(NT):
                    pool.wait_ge(s_exp2_hi, NT * n + i + 1).then_inc(s_pool_passed, 1)
                    sl = slice(S_OFF[i], S_OFF[i] + KEYS[i])
                    done = g.tensor_tensor(exp2_hl[:, 1, sl], exp2[:, sl], exp2_hl[:, 0, sl], ALU.subtract)
                done.then_inc(s_exp2_lo, 1)

            def step(i, g1, f, m, n):
                if f is not None and not early(m):
                    rest_of_residual(f)
                if n is not None and not final(n):
                    low_probs(n)
                if f is not None:
                    norm_rows(1, f, LN_SCALE ** 4, NORM_EPS * NORM_EPS)
                if g1 is not None:
                    norm_rows(0, g1, 1.0, 1e-38)
                if early(m):
                    low_1(g1)
                if f is not None:
                    route_weights(f)
                if n is not None:
                    add_tile(n, 0)
                if g1 is not None:
                    if not early(m):
                        low_1(g1)
                    spread_norms(g1)
                if n is not None:
                    add_tile(n, 1)
                    if final(m):
                        low_probs(m)
                    if not final(n):
                        add_tile(n, 2)

            norm_rows(0, 0, 1.0, 1e-38)
            low_1(0)
            spread_norms(0)
            rest_of_residual(0)
            norm_rows(0, 1, 1.0, 1e-38)
            spread_norms(1)
            norm_rows(1, 0, LN_SCALE ** 4, NORM_EPS * NORM_EPS)
            low_1(1)
            rest_of_residual(1)
            route_weights(0)
            pipeline(pool, step)

        @block.scalar
        def _(act):
            a = nc.scalar

            def load_weights(n, w):
                for c in range(NC):
                    act.dma_start(stage_qkv[:, n, c, :, :],
                                  w[:, c * P:(c + 1) * P, :].rearrange("e p d -> p e d")).then_inc(s_w_loaded, 16)

            act.dma_start(read_x[:, :], x[:, 0, :]).then_inc(s_read_loaded, 16)
            act.dma_start(read_bias[:, :], tok_b.partition_broadcast(RR)).then_inc(s_read_loaded, 16)
            for c in range(NC):
                act.dma_start(stage_sim[:, 0, c, :], sim_matrix[c * P:(c + 1) * P, :]).then_inc(s_small_loaded, 16)
            act.dma_start(gate_tmp[:, 0, :], gates.partition_broadcast(P)).then_inc(s_small_loaded, 16)
            act.wait_ge(s_tok_loaded, 16)
            a.activation(w_tok[:, 0, :, :], stage_tok[:, 0, :, :], ACT.Copy, scale=W_SCALE).then_inc(s_tokw_hi, 1)

            def split_in(b, par):
                for c in range(NC):
                    act.wait_ge(s_in_turned, NC * b + c + 1)
                    if c == 0 and (not isinstance(b, int) or b >= 2):
                        act.wait_ge(s_tok_done, b - 1)
                    a.activation(xinT[:, par, 0, c, :], bank[2 + c][:, 0:TP], ACT.Copy, scale=X_SCALE).then_inc(s_in_hi, 1)

            def gelu(b):
                act.wait_ge(s_tok_first, b + 1)
                a.activation(h[:, b, 0:NT - 1, :], bank[0][:, :].rearrange("p (t c) -> p t c", t=NT - 1), ACT.Gelu,
                             scale=1.0 / (X_SCALE * W_SCALE)).then_inc(s_h_first, 1)
                act.wait_ge(s_tok_done, b + 1)
                a.activation(h[0:LAST, b, NT - 1, :], bank[1][0:LAST, 0:C], ACT.Gelu,
                             scale=1.0 / (X_SCALE * W_SCALE)).then_inc(s_h_ready, 1)

            def slot(b, par, piece=None):
                if b is not B - 1:
                    split_in(b + 1, 1 - par)
                if piece is not None:
                    a.activation(qkv_pieces(w_qkv_hi)[:, piece, :], qkv_pieces(stage)[:, piece, :], ACT.Copy,
                                 scale=W_SCALE).then_inc(s_w_hi, 1)
                gelu(b)

            def high(n, b):
                act.wait_ge((s_xs1, s_xs2)[n], NT * (b + 1))
                if later(b):
                    act.wait_ge((s_att_done, s_turned2_hi)[n], (NT, 1)[n] * b)
                a.activation(xhl[n][:, 0, :, 0:C], xs[n][:, :, :], ACT.Copy).then_inc((s_hi1, s_hi2)[n], 1)

            def head_high(dst, src, done, count, ready, waits, scale):
                act.wait_ge(done, count)
                for q, v in waits:
                    act.wait_ge(q, v)
                a.activation(dst[:, 0, 0:T], src[:, 0:T], ACT.Copy, scale=scale).then_inc(ready, 1)

            qkv_out = 1.0 / (LN_SCALE * W_SCALE) * Q_SCALE

            def turned_rows(f):
                act.wait_ge(s_turned1_hi, f + 1)
                if later(f):
                    act.wait_ge(s_dots_done, NT * f)
                a.activation(xT[0][:, 0, :, :].rearrange("p c t -> p (c t)"), as16(turn[0], NC * TP),
                             ACT.Copy).then_inc(s_T1_hi, 1)
                act.wait_ge(s_turned1_lo, f + 1)
                a.activation(xT[0][:, 1, :, :].rearrange("p c t -> p (c t)"), as16(turn[1], NC * TP),
                             ACT.Copy).then_inc(s_T1_lo, 1)

            def exp_cosines(f):
                for t in range(NT):
                    act.wait_ge(s_cos_ready, NT * f + t + 1)
                    if t == 0 and later(f):
                        act.wait_ge(s_exp1_lo, NT * f)
                        act.wait_ge(s_att_done, NT * f)
                    a.activation(exp1[:, t, t * P:T], cosine[:, t, t * P:T], ACT.Exp, bias=log_p[:, :],
                                 scale=1.0 / (LN_SCALE * LN_SCALE))
                    a.activation(exp1_hl[:, 0, t, t * P:T], cosine[:, t, t * P:T], ACT.Exp, bias=log_p[:, :],
                                 scale=1.0 / (LN_SCALE * LN_SCALE)).then_inc(s_exp1_hi, 1)

            def turned_rows_2(f):
                act.wait_ge(s_turned2_hi, f + 1)
                if later(f):
                    act.wait_ge(s_xm_ready, E * f)
                a.activation(xT[1][:, 0, :, :].rearrange("p c t -> p (c t)"), as16(turn[0], NC * TP),
                             ACT.Copy).then_inc(s_T2_hi, 1)

            def turned_mask(f):
                act.wait_ge(s_mask_turned, f + 1)
                if later(f):
                    act.wait_ge(s_mask_stored, 16 * f)
                a.activation(maskT[:, :], as16(turn[1], TP)[0:E, :], ACT.Copy).then_inc(s_mask_row, 1)

            def route_exp(f):
                act.wait_ge(s_weigh_pool, 6 * f + 4)
                a.activation(lg[:, 7, :, :], lg[:, 6, :, :], ACT.Exp).then_inc(s_route_exp, 1)

            def exp_scores(n, i):
                act.wait_ge(s_scores_out, NT * n + i + 1)
                a.activation(neg_max[:, i:i + 1], row_max[:, i:i + 1], ACT.Identity, bias=log_p[:, :],
                             scale=-SCORE_SCALE).then_inc(s_negmax_ready, 1)
                act.wait_ge(s_negmax_ready, NT * n + i + 1)
                if i == 0:
                    if later(n):
                        act.wait_ge(s_pT_lo_turned, n)
                        act.wait_ge(s_sum2_s, n)
                        act.wait_ge(s_exp2_lo, n)
                sl = slice(S_OFF[i], S_OFF[i] + KEYS[i])
                a.activation(exp2[:, sl], scores[:, sl], ACT.Exp, bias=neg_max[:, i:i + 1],
                             scale=SCORE_SCALE, accum_out=sum2[:, i:i + 1]).then_inc(s_exp2_full, 1)
                a.activation(exp2_hl[:, 0, sl], scores[:, sl], ACT.Exp, bias=neg_max[:, i:i + 1],
                             scale=SCORE_SCALE).then_inc(s_exp2_hi, 1)

            def turned_probs(n):
                act.wait_ge(s_pT_hi_turned, n + 1)
                if later(n):
                    act.wait_ge(s_pv_done, n)
                a.activation(pT[:, 0, :], as16(turn[1], PW), ACT.Copy).then_inc(s_pT_hi, 1)

            def step(i, g1, f, m, n):
                def scale_pairs(lo, hi):
                    for p in range(lo, hi) if n is not None else ():
                        t, q = p // (E // 2), p % (E // 2)
                        act.wait_ge(s_pair_done, PAIRS * n + p + 1)
                        if p == 0:
                            act.wait_ge(s_out_w_ready, n + 1)
                        if q == 0 and t == 2:
                            act.wait_ge(s_tile_summed, 2 * NT * n + 1)
                        elif q == 0 and later(n):
                            act.wait_ge(s_tile_summed, 2 * NT * n - (1 if t == 0 else 3))
                        a.activation(prod[:, t % 2, q, :], pair_bank(n, p)[:, C:2 * C], ACT.Copy,
                                     scale=out_w[:, t, 2 * q + 1:2 * q + 2]).then_inc(s_pair_scaled, 1)

                def high_v():
                    head_high(vT, qkv_bank[2], s_v_done, E * (m + 1), s_v_hi,
                              [(s_v_turned, m)] if later(m) else [], qkv_out)

                if f is not None:
                    if not early(m):
                        exp_cosines(f)
                if n is not None:
                    if not final(n):
                        for i in range(NT):
                            exp_scores(n, i)
                        turned_probs(n)
                    head_high(aoT, probs_bank(n), s_pv_done, n + 1, s_ao_hi,
                              [(s_pair_done, PAIRS * n)] if later(n) else [], 1.0 / (P_SCALE * Q_SCALE))
                if f is not None:
                    high(1, f)
                if m is not None:
                    head_high(qT, qkv_bank[0], s_q_done, m + 1, s_q_hi,
                              [(s_scores_done, NT * m)] if later(m) else [], qkv_out)
                if f is not None:
                    turned_rows_2(f)
                scale_pairs(0, 2)
                if early(m):
                    high(0, g1)
                if f is not None:
                    turned_mask(f)
                scale_pairs(2, 3)
                if f is not None:
                    route_exp(f)
                scale_pairs(3, 5)
                if g1 is not None and not early(m):
                    high(0, g1)
                scale_pairs(5, 6)
                if m is not None:
                    head_high(kT, qkv_bank[1], s_k_done, m + 1, s_k_hi,
                              [(s_scores_done, NT * m)] if later(m) else [], qkv_out)
                if final(m):
                    scale_pairs(6, 8)
                    exp_scores(m, 0)
                    scale_pairs(8, 9)
                    exp_scores(m, 1)
                    scale_pairs(9, 10)
                    exp_scores(m, 2)
                    high_v()
                    turned_probs(m)
                    scale_pairs(10, 12)
                else:
                    scale_pairs(6, PAIRS)
                if g1 is not None:
                    turned_rows(g1)
                if m is not None and not final(m):
                    high_v()

            split_in(0, 0)
            act.wait_ge(s_zeroed, 2)
            act.wait_ge(s_consts, 2)
            load_weights(0, q_proj)
            slot(0, 0)
            load_weights(1, k_proj)
            slot(1, 1)
            load_weights(2, v_proj)
            slot(2, 0)
            high(0, 0)
            act.wait_ge(s_w_loaded, 16 * 3 * NC)
            looped_slots(act, slot)
            act.dma_start(stage_o[:, :, :].rearrange("p a n -> p (a n)").rearrange("p (e c) -> p e c", e=E),
                          o_proj.rearrange("e d c -> d e c")).then_inc(s_wo_loaded, 16)
            turned_rows(0)
            slot(7, 1, 2 * NC)
            slot(8, 0, 2 * NC + 1)
            act.wait_ge(s_setup_dve, 9)
            a.activation(w_sim[:, :, 0, :], stage_sim[:, 3, :, :], ACT.Copy).then_inc(s_sim_hi, 1)
            act.wait_ge(s_small_loaded, 16 * (NC + 1))
            a.activation(gate_tmp[:, 1, :], gate_tmp[:, 0, :], ACT.Exp, scale=-1.0).then_inc(s_gate_exp, 1)
            exp_cosines(0)
            slot(9, 1)
            high(0, 1)
            slot(10, 0)
            high(1, 0)
            slot(11, 1)
            turned_rows(1)
            slot(12, 0)
            turned_rows_2(0)
            slot(13, 1)
            turned_mask(0)
            slot(14, 0)
            slot(15, 1)
            exp_cosines(1)
            route_exp(0)
            act.wait_ge(s_wo_loaded, 16)
            for k in range(2):
                a.activation(w_o[:, 0, k * (E * C // 2):(k + 1) * (E * C // 2)], stage_o[:, k, :], ACT.Copy,
                             scale=W_SCALE).then_inc(s_w_hi, 1)
            pipeline(act, step)

        @block.vector
        def _(dve):
            v = nc.vector

            v.memset(xin[96:P, :, NT - 1, :], 0.0).then_inc(s_zeroed, 1)
            v.memset(h[96:P, :, NT - 1, :], 0.0).then_inc(s_zeroed, 1)
            v.memset(read_xT[:, :, :], 0.0).then_inc(s_zeroed, 1)
            dve.wait_ge(s_tokw_hi, 1)
            v.scalar_tensor_tensor(w_tok[:, 1, :, :].rearrange("p c n -> p (c n)"),
                                   stage_tok[:, 0, :, :].rearrange("p c n -> p (c n)"), W_SCALE,
                                   w_tok[:, 0, :, :].rearrange("p c n -> p (c n)"),
                                   ALU.mult, ALU.subtract).then_inc(s_tokw_lo, 1)
            dve.wait_ge(s_zeroed, 3)
            dve.wait_ge(s_setup_pe, 1)
            for at in (0, 32):
                v.tensor_copy(read_xT[:, :, at:at + B],
                              bank[4][:, 0:NC * B].rearrange("p (c b) -> p c b", c=NC)).then_inc(s_setup_dve, 1)
            dve.wait_ge(s_small_loaded, 16 * (NC + 1))
            v.tensor_tensor(stage_sim[:, 1, :, :], stage_sim[:, 0, :, :], stage_sim[:, 0, :, :],
                            ALU.mult).then_inc(s_setup_dve, 1)
            dve.wait_ge(s_setup_pe, 2)
            dve.wait_ge(s_read_loaded, 32)
            v.tensor_tensor(read_row[:, :], bank[4][0:RR, 0:C], read_bias[:, :], ALU.add).then_inc(s_setup_dve, 1)
            dve.wait_ge(s_setup_dve, 4)
            v.tensor_scalar(read_hl[:, :], read_row[:, :], R_SCALE, None, ALU.mult).then_inc(s_setup_dve, 1)
            dve.wait_ge(s_setup_dve, 5)
            v.scalar_tensor_tensor(read_hl[32:RR, :], read_row[32:RR, :], R_SCALE, read_hl[32:RR, :],
                                   ALU.mult, ALU.subtract).then_inc(s_setup_dve, 1)

            def split_low(b, par):
                for c in range(NC):
                    dve.wait_ge(s_in_hi, NC * b + c + 1)
                    v.scalar_tensor_tensor(xinT[:, par, 1, c, :], bank[2 + c][:, 0:TP], X_SCALE, xinT[:, par, 0, c, :],
                                           ALU.mult, ALU.subtract).then_inc(s_in_lo, 1)

            def slot(b, par, piece=None):
                if b is not B - 1:
                    split_low(b + 1, 1 - par)
                if piece is not None:
                    dve.wait_ge(s_w_hi, piece + 1)
                    v.scalar_tensor_tensor(qkv_pieces(w_qkv_lo)[:, piece, :], qkv_pieces(stage)[:, piece, :], W_SCALE,
                                           qkv_pieces(w_qkv_hi)[:, piece, :], ALU.mult, ALU.subtract).then_inc(s_w_lo, 1)

            def output_weights_low(k):
                sl = slice(k * (E * C // 2), (k + 1) * (E * C // 2))
                dve.wait_ge(s_w_hi, 3 * NC + k + 1)
                v.scalar_tensor_tensor(w_o[:, 1, sl], stage_o[:, k, :], W_SCALE, w_o[:, 0, sl],
                                       ALU.mult, ALU.subtract).then_inc(s_w_lo, 1)

            def router_directions():
                dve.wait_ge(s_setup_pool, 5)
                v.tensor_scalar(sim_norm[:, 2, :], sim_norm[:, 1, :], NORM_EPS, 1.0 / LN_SCALE, ALU.max,
                                ALU.mult).then_inc(s_setup_dve, 1)
                dve.wait_ge(s_setup_dve, 8)
                v.reciprocal(sim_norm[:, 3, :], sim_norm[:, 2, :]).then_inc(s_routed_dve, 1)
                dve.wait_ge(s_routed_dve, 1)
                v.tensor_tensor(stage_sim[:, 3, :, :], stage_sim[:, 0, :, :],
                                sim_norm[:, 3, :].unsqueeze(1).broadcast_to([P, NC, E]), ALU.mult).then_inc(s_setup_dve, 1)

            def router_low():
                dve.wait_ge(s_sim_hi, 1)
                v.tensor_tensor(w_sim[:, :, 1, :], stage_sim[:, 3, :, :], w_sim[:, :, 0, :],
                                ALU.subtract).then_inc(s_sim_lo, 1)
                dve.wait_ge(s_gate_exp, 1)
                v.tensor_scalar(gate_tmp[:, 2, :], gate_tmp[:, 1, :], 1.0, None, ALU.add).then_inc(s_setup_dve, 1)
                dve.wait_ge(s_setup_dve, 10)
                v.reciprocal(sig[:, :], gate_tmp[:, 2, :]).then_inc(s_setup_dve, 1)

            def norm_sums(n, b, t):
                v.bn_stats(stats[n][:, t, :], h[:, b, t, :]).then_inc((s_stats1, s_stats2)[n], 1)

            def norm_stats(n, b, sums=True):
                st, mo = (s_stats1, s_stats2)[n], (s_moments1, s_moments2)[n]
                for t in range(NT):
                    if sums:
                        norm_sums(n, b, t)
                for t in range(NT):
                    dve.wait_ge(st, NT * b + t + 1).then_inc(s_dve_passed, 1)
                    v.bn_aggr(moments[n][:, t, :], stats[n][:, t, :]).then_inc(mo, 1)

            def norm_apply(n, b):
                dve.wait_ge((s_scale1, s_scale2)[n], b + 1)
                if later(b):
                    dve.wait_ge((s_lo1, s_lo2)[n], b)
                if n == 0 and later(b):
                    dve.wait_ge(s_hx_ready, b).then_inc(s_dve_passed, 1)
                for t in range(NT):
                    v.tensor_scalar(xs[n][:, t, :], h[:, b, t, :], moments[n][:, t, 0:1], small[n][:, 4, t:t + 1],
                                    ALU.subtract, ALU.mult).then_inc((s_xs1, s_xs2)[n], 1)

            def head_low(dst, src, hi, count, ready, scale):
                dve.wait_ge(hi, count)
                v.scalar_tensor_tensor(dst[:, 1, 0:T], src[:, 0:T], scale, dst[:, 0, 0:T],
                                       ALU.mult, ALU.subtract).then_inc(ready, 1)

            qkv_out = 1.0 / (LN_SCALE * W_SCALE) * Q_SCALE

            def add_pair(n, p):
                t, e0 = p // (E // 2), 2 * (p % (E // 2))
                dve.wait_ge(s_pair_scaled, PAIRS * n + p + 1)
                if e0:
                    dve.wait_ge(s_pair_added, PAIRS * n + p)
                v.scalar_tensor_tensor(h[:, n, t, :], pair_bank(n, p)[:, 0:C], out_w[:, t, e0:e0 + 1], h[:, n, t, :],
                                       ALU.mult, ALU.add).then_inc(s_pair_added, 1)

            def last_tile(n):
                t, first = NT - 1, PAIRS - E // 2
                p_of = prod[:, t % 2, :, :]
                add_pair(n, first)
                add_pair(n, first + 1)
                v.tensor_tensor(last_sum[:, 0, :], p_of[:, 0, :], p_of[:, 1, :], ALU.add).then_inc(s_last_summed, 1)
                add_pair(n, first + 2)
                dve.wait_ge(s_last_summed, 1)
                dve.wait_ge(s_pair_added, PAIRS * n + first + 3)
                v.tensor_tensor(h[:, n, t, :], last_sum[:, 0, :], h[:, n, t, :], ALU.add).then_inc(s_last_summed, 1)
                dve.wait_ge(s_last_summed, 2)
                add_pair(n, first + 3)
                v.tensor_tensor(last_sum[:, 1, :], p_of[:, 2, :], p_of[:, 3, :], ALU.add).then_inc(s_last_summed, 1)
                dve.wait_ge(s_last_summed, 3)
                dve.wait_ge(s_pair_added, PAIRS * (n + 1))
                v.tensor_tensor(h[:, n, t, :], last_sum[:, 1, :], h[:, n, t, :], ALU.add).then_inc(s_last_ready, 1)

            def route(b):
                at = [0]

                def after(ins):
                    ins.then_inc(s_route_dve, 1)
                    at[0] += 1
                    dve.wait_ge(s_route_dve, RP * b + at[0])

                L, M = lg[:, 2, :, :], lg[:, 3, :, :]
                square = [x.rearrange("p t (a b) -> p t a b", a=E) for x in (cmp[:, k, :, :] for k in range(4))]
                mine = L.unsqueeze(3).broadcast_to([P, NT, E, E])
                others = L.unsqueeze(2).broadcast_to([P, NT, E, E])
                dve.wait_ge(s_logits_done, b + 1)
                v.tensor_copy(logit_parts[:, :, :].rearrange("p t e -> p (t e)"),
                              turn[0][:, 0:NT * 2 * E]).then_inc(s_logits_out, 1)
                dve.wait_ge(s_logits_out, b + 1)
                after(v.tensor_tensor(lg[:, 0, :, :], logit_parts[:, :, 0:E], logit_parts[:, :, E:2 * E], ALU.add))
                dve.wait_ge(s_rnorm2, b + 1)
                after(v.tensor_tensor(lg[:, 1, :, :], lg[:, 0, :, :],
                                      small[1][:, 5, :].unsqueeze(2).broadcast_to([P, NT, E]), ALU.mult))
                if later(b):
                    dve.wait_ge(s_weigh_pool, 6 * b)
                after(v.tensor_tensor(L, lg[:, 1, :, :], sig[:, :].unsqueeze(1).broadcast_to([P, NT, E]), ALU.subtract))
                v.tensor_scalar(M, L, 0.0, None, ALU.is_gt)
                v.tensor_scalar(lg[:, 4, :, :], L, 0.0, None, ALU.max)
                v.tensor_tensor(square[0], others, mine, ALU.is_gt)
                after(v.tensor_tensor(square[1], others, mine, ALU.is_equal))
                v.tensor_reduce(row3[:, 0, :], M, AX_X, ALU.max)
                after(v.tensor_tensor(cmp[:, 2, :, :], cmp[:, 1, :, :],
                                      lower[:, :, :].rearrange("p a b -> p (a b)").unsqueeze(1).broadcast_to([P, NT, E * E]),
                                      ALU.mult))
                v.tensor_scalar(row3[:, 1, :], row3[:, 0, :], 0.0, None, ALU.is_equal)
                after(v.tensor_tensor(cmp[:, 3, :, :], cmp[:, 2, :, :], cmp[:, 0, :, :], ALU.add))
                after(v.tensor_reduce(lg[:, 5, :, :].rearrange("p t e -> p (t e)"),
                                      cmp[:, 3, :, :].rearrange("p t (a b) -> p (t a) b", a=E), AX_X, ALU.add))
                after(v.scalar_tensor_tensor(lg[:, 0, :, :], lg[:, 5, :, :], 2.0,
                                             row3[:, 1, :].unsqueeze(2).broadcast_to([P, NT, E]),
                                             ALU.is_lt, ALU.mult))
                if later(b):
                    dve.wait_ge(s_mask_turned, b)
                v.tensor_tensor(mask16[:, :, :], lg[:, 0, :, :], M, ALU.add).then_inc(s_mask_ready, 1)
                v.tensor_tensor(lg[:, 8, :, :], lg[:, 0, :, :], M, ALU.add).then_inc(s_mask_ready, 1)
                assert at[0] == RP

            def mask_tokens(b, e):
                if e % (E // 2) == 0:
                    dve.wait_ge(s_mask_loaded[e // (E // 2)], 16 * (b + 1))
                if e == 0:
                    dve.wait_ge(s_T2_hi, b + 1)
                    dve.wait_ge(s_T2_lo, b + 1)
                if later(b):
                    dve.wait_ge(s_v_done, E * (b - 1) + e + 1)
                v.tensor_tensor(xm[:, e, :, 0:T], xT[1][:, :, :, 0:T].rearrange("p a c t -> p (a c) t"),
                                mask_all[:, e, 0:T].unsqueeze(1).broadcast_to([P, 2 * NC, T]),
                                ALU.mult).then_inc(s_xm_ready, 1)

            def cosines(f, t):
                dve.wait_ge(s_invn_ready, NT * f + t + 1)
                dve.wait_ge(s_dots_done, NT * f + t + 1)
                if t == 0 and later(f):
                    dve.wait_ge(s_exp1_hi, NT * f)
                v.tensor_tensor(cosine[:, t, t * P:T], work[t % 2][:, t * P:T], inv_norms[:, t, t * P:T],
                                ALU.mult).then_inc(s_cos_ready, 1)

            def exp_low(f, t):
                dve.wait_ge(s_exp1_hi, NT * f + t + 1)
                if t == 0 and later(f):
                    dve.wait_ge(s_att_done, NT * f)
                v.tensor_tensor(exp1_hl[:, 1, t, t * P:T], exp1[:, t, t * P:T], exp1_hl[:, 0, t, t * P:T],
                                ALU.subtract).then_inc(s_exp1_lo, 1)

            def exp_lower(f):
                dve.wait_ge(s_exp1_turned, f + 1)
                turned = as16(turn[1], NC * TP).rearrange("p (a w) -> p a w", a=2)
                for j in range(1, NT):
                    at = sum(range(1, j)) * P
                    v.tensor_copy(exp1_hl[:, :, j, 0:j * P], turned[:, :, at:at + j * P]).then_inc(s_exp1_square, 1)

            def residual(f):
                dve.wait_ge(s_hx_ready, f + 1).then_inc(s_dve_passed, 1)
                for t in range(NT):
                    rows = P if t < NT - 1 else LAST
                    dve.wait_ge(s_att_done, NT * f + t + 1)
                    v.reciprocal(inv_sum1[0:rows, t:t + 1], att_bank[t][0:rows, C:C + 1]).then_inc(s_sum1_i, 1)
                    dve.wait_ge(s_sum1_i, NT * f + t + 1)
                    v.scalar_tensor_tensor(h[0:rows, f, t, :], att_bank[t][0:rows, 0:C], inv_sum1[0:rows, t:t + 1],
                                           hx[0:rows, t, :], ALU.mult, ALU.add).then_inc(s_h2_ready, 1)
                    if t == 1:
                        dve.wait_ge(s_h2_ready, NT * f + 1).then_inc(s_dve_passed, 1)
                        norm_sums(1, f, 0)
                for t in (1, 2):
                    dve.wait_ge(s_h2_ready, NT * f + t + 1).then_inc(s_dve_passed, 1)
                    norm_sums(1, f, t)
                norm_stats(1, f, sums=False)

            def low_2(f):
                dve.wait_ge(s_hi2, f + 1)
                if later(f):
                    dve.wait_ge(s_turned2_lo, f)
                v.tensor_tensor(xhl[1][:, 1, :, :], xs[1][:, :, :], xhl[1][:, 0, :, :],
                                ALU.subtract).then_inc(s_lo2, 1)

            def turned_low_2(f):
                dve.wait_ge(s_turned2_lo, f + 1)
                v.tensor_copy(xT[1][:, 1, :, :].rearrange("p c t -> p (c t)"),
                              as16(turn[1], NC * TP)).then_inc(s_T2_lo, 1)

            def weight_max(f):
                dve.wait_ge(s_weigh_pool, 6 * f + 3)
                v.tensor_reduce(row3[:, 2, :], lg[:, 9, :, :], AX_X, ALU.max).then_inc(s_weigh_dve, 1)

            def weight_sum(f):
                dve.wait_ge(s_route_exp, f + 1)
                v.tensor_reduce(row3[:, 3, :], lg[:, 7, :, :], AX_X, ALU.add).then_inc(s_weigh_dve, 1)
                dve.wait_ge(s_weigh_dve, 3 * f + 2)
                v.reciprocal(row3[:, 4, :], row3[:, 3, :]).then_inc(s_weigh_dve, 1)

            def mask_scores(n, i, src):
                dve.wait_ge(s_scores_done, NT * n + i + 1).then_inc(s_dve_passed, 1)
                if i == 0 and later(n):
                    dve.wait_ge(s_exp2_hi, NT * n).then_inc(s_dve_passed, 1)
                    dve.wait_ge(s_negmax_ready, NT * n).then_inc(s_dve_passed, 1)
                v.tensor_tensor_reduce(scores[:, S_OFF[i]:S_OFF[i] + KEYS[i]], src[:, 0:KEYS[i]],
                                       causal[:, TP - P - i * P:TP - P - i * P + KEYS[i]], 1.0, -3e38,
                                       ALU.add, ALU.max, row_max[:, i:i + 1]).then_inc(s_scores_out, 1)

            def turned_values(n):
                dve.wait_ge(s_v_turned, n + 1)
                if later(n):
                    dve.wait_ge(s_pv_done, n)
                v.tensor_copy(v_tok[:, :, :, :].rearrange("p a t d -> p (a t d)"),
                              as16(bank[4] if final(n) else turn[0], 2 * NT * D)).then_inc(s_v_tok_ready, 1)

            def turned_probs_low(n):
                dve.wait_ge(s_pT_lo_turned, n + 1)
                if final(n):
                    dve.wait_ge(s_pv_done, n)
                v.tensor_copy(pT[:, 1, :], as16(turn[0], PW)).then_inc(s_pT_lo, 1)

            def step(i, g1, f, m, n):
                def pairs(a, b):
                    if n is not None:
                        for p in range(a, b):
                            add_pair(n, p)

                def F(fn, *a):
                    if f is not None:
                        fn(f, *a)

                for t in range(NT):
                    if not early(m) and not (t < 2 and second(m)):
                        F(cosines, t)
                if not early(m) and not second(m):
                    F(exp_low, 0)
                    F(exp_low, 1)
                if n is not None:
                    for i in range(NT) if not final(n) else ():
                        if i == NT - 1:
                            F(exp_low, 2)
                            F(exp_lower)
                        mask_scores(n, i, out_bank[i % 2])
                elif f is not None and not early(m):
                    exp_low(f, 2)
                    exp_lower(f)
                if g1 is not None:
                    norm_stats(0, g1)
                if n is not None and not final(n):
                    turned_values(n)
                F(residual)
                if n is not None and not final(n):
                    turned_probs_low(n)
                if f is not None:
                    norm_apply(1, f)
                if n is not None:
                    head_low(aoT, probs_bank(n), s_ao_hi, n + 1, s_ao_lo, 1.0 / (P_SCALE * Q_SCALE))
                    v.tensor_scalar(sum2_scaled[:, :], sum2[:, :], W_SCALE / P_SCALE, None,
                                    ALU.mult).then_inc(s_sum2_s, 1)
                F(low_2)
                if n is not None:
                    dve.wait_ge(s_sum2_s, n + 1)
                    v.reciprocal(inv_sum2[:, :], sum2_scaled[:, :]).then_inc(s_sum2_i, 1)
                    dve.wait_ge(s_sum2_i, n + 1)
                    v.tensor_tensor(out_w[:, :, :], route_w[:, n, :, :],
                                    inv_sum2[:, :].unsqueeze(2).broadcast_to([P, NT, E]),
                                    ALU.mult).then_inc(s_out_w_ready, 1)
                    dve.wait_ge(s_out_w_ready, n + 1)
                if m is not None:
                    head_low(qT, qkv_bank[0], s_q_hi, m + 1, s_q_lo, qkv_out)
                F(turned_low_2)
                pairs(0, 1)
                if early(m):
                    norm_apply(0, g1)
                F(route)
                if early(m):
                    output_weights_low(0)
                    output_weights_low(1)
                pairs(1, 3)
                F(weight_max)
                pairs(3, 4)
                F(weight_sum)
                if g1 is not None and not early(m):
                    norm_apply(0, g1)
                pairs(4, 6)
                if m is not None:
                    head_low(kT, qkv_bank[1], s_k_hi, m + 1, s_k_lo, qkv_out)
                if final(m):
                    pairs(6, 8)
                    for i in range(NT):
                        mask_scores(m, i, last_bank[i])
                    pairs(8, 10)
                    head_low(vT, qkv_bank[2], s_v_hi, m + 1, s_v_lo, qkv_out)
                    turned_probs_low(m)
                    pairs(10, 11)
                    turned_values(m)
                    pairs(11, 12)
                    return
                if final(n):
                    pairs(6, 8)
                    last_tile(n)
                    return
                for e in range(E):
                    if e < 6:
                        pairs(6 + e, 7 + e)
                    if f is not None:
                        mask_tokens(f, e)
                    if early(m) and e == 0:
                        head_low(vT, qkv_bank[2], s_v_hi, m + 1, s_v_lo, qkv_out)
                    if early(m) and e == 3:
                        cosines(g1, 0)
                    if early(m) and e == 4:
                        cosines(g1, 1)
                    if early(m) and e == 6:
                        exp_low(g1, 0)
                        exp_low(g1, 1)
                    if e == E - 2 and m is not None and not early(m):
                        head_low(vT, qkv_bank[2], s_v_hi, m + 1, s_v_lo, qkv_out)

            split_low(0, 0)
            slot(0, 0)
            dve.wait_ge(s_setup_pe, 3)
            v.tensor_copy(sim_norm[:, 0, :], bank[5][:, 0:E]).then_inc(s_setup_dve, 1)
            slot(1, 1)
            dve.wait_ge(s_h_ready, 1)
            norm_stats(0, 0)
            slot(2, 0)
            router_directions()
            norm_apply(0, 0)
            looped_slots(dve, slot)
            slot(7, 1, 2 * NC)
            for t in range(NT):
                cosines(0, t)
            dve.wait_ge(s_h_ready, 2)
            norm_stats(0, 1)
            slot(8, 0, 2 * NC + 1)
            router_low()
            for t in range(NT):
                exp_low(0, t)
            exp_lower(0)
            slot(9, 1)
            norm_apply(0, 1)
            residual(0)
            slot(10, 0)
            norm_apply(1, 0)
            slot(11, 1)
            low_2(0)
            slot(12, 0)
            turned_low_2(0)
            dve.wait_ge(s_consts, 2)
            route(0)
            cosines(1, 0)
            cosines(1, 1)
            slot(13, 1)
            weight_max(0)
            slot(14, 0)
            for e in range(E):
                mask_tokens(0, e)
                if e == 1:
                    cosines(1, 2)
                if e == 4:
                    for t in range(NT):
                        exp_low(1, t)
                if e == 5:
                    exp_lower(1)
            weight_sum(0)
            dve.wait_ge(s_h_ready, B)
            pipeline(dve, step)

        @block.tensor
        def _(pe):
            t_ = nc.tensor
            def turn_in(b, par):
                pe.wait_ge(s_x_loaded1 if par else s_x_loaded0, 16 * LOADS * (b // 2 + 1) if isinstance(b, int)
                           else (b + (2 - par)) * (8 * LOADS))
                for c in range(NC):
                    if later(b):
                        pe.wait_ge(s_in_lo, NC * (b - 1) + c + 1)
                    for t in range(NT):
                        last = t_.transpose(bank[2 + c][:, t * P:(t + 1) * P], xin[:, par, t, c * P:(c + 1) * P], ident[:, :])
                    last.then_inc(s_in_turned, 1)

            def project(b, par):
                pe.wait_ge(s_in_lo, NC * (b + 1))
                for t in range(NT):
                    if later(b) and t == 0:
                        pe.wait_ge(s_h_first, b)
                    if later(b) and t == NT - 1:
                        pe.wait_ge(s_h_ready, b)
                    dst = bank[t // 2][:, (t % 2) * C:(t % 2 + 1) * C]
                    for c in range(NC):
                        for xp, wp in ((0, 0), (0, 1), (1, 0)):
                            t_.matmul(dst, xinT[:, par, xp, c, t * P:(t + 1) * P], w_tok[:, wp, c, :],
                                      start=(c == 0 and xp == 0 and wp == 0), stop=False)
                    last = t_.matmul(dst, pick[0:RR, b, :].broadcast_to([RR, P]), read_hl[:, :], start=False, stop=True)
                    if t == NT - 2:
                        last.then_inc(s_tok_first, 1)
                last.then_inc(s_tok_done, 1)

            def slot(b, par, piece=None):
                if b is not B - 1:
                    turn_in(b + 1, 1 - par)
                project(b, par)

            pe.wait_ge(s_consts, 1)
            turn_in(0, 0)
            pe.wait_ge(s_read_loaded, 32)
            for c in range(NC):
                last = t_.transpose(bank[4][:, c * B:(c + 1) * B], read_x[:, c * P:(c + 1) * P], ident[0:B, 0:B])
            last.then_inc(s_setup_pe, 1)
            pe.wait_ge(s_tok_loaded, 16)
            pe.wait_ge(s_setup_dve, 2)
            for c in range(NC):
                last = t_.matmul(bank[4][0:RR, 0:C], read_xT[:, c, :], stage_tok[:, 1, c, :],
                                 start=(c == 0), stop=(c == NC - 1))
            last.then_inc(s_setup_pe, 1)
            pe.wait_ge(s_setup_dve, 3)
            pe.wait_ge(s_consts, 2)
            for c in range(NC):
                last = t_.matmul(bank[5][:, 0:E], ones[:, :], stage_sim[:, 1, c, :], start=(c == 0), stop=(c == NC - 1))
            last.then_inc(s_setup_pe, 1)

            def turn_rows(n, b, part, dst, done):
                for c in range(NC):
                    for t in range(NT):
                        last = t_.transpose(as16(dst, NC * TP)[:, c * TP + t * P:c * TP + (t + 1) * P],
                                            xhl[n][:, part, t, c * P:(c + 1) * P], ident16[:, :])
                last.then_inc(done, 1)

            def turn_first(b):
                pe.wait_ge(s_hi1, b + 1)
                if not isinstance(b, int) or b > 1:
                    pe.wait_ge(s_logits_out, b)
                    pe.wait_ge(s_mask_row, b)
                turn_rows(0, b, 0, turn[0], s_turned1_hi)
                pe.wait_ge(s_lo1, b + 1)
                turn_rows(0, b, 1, turn[1], s_turned1_lo)

            def split_product(dst, left, right, starts, stops, done=None):
                k = 0
                for lp, rp in ((0, 0), (0, 1), (1, 0)):
                    last = t_.matmul(dst, left[lp], right[rp], start=(starts and k == 0), stop=(stops and k == 2),
                                     skip_group_check=True)
                    k += 1
                if done is not None:
                    last.then_inc(done, 1)

            def unit(m, which, e):
                done = (s_q_done, s_k_done, s_v_done)[which]
                if which == 0:
                    pe.wait_ge(s_xm_ready, E * m + e + 1)
                if e == 0:
                    if which == 0 and later(m):
                        pe.wait_ge(s_q_lo, m)
                    if which == 1 and later(m):
                        pe.wait_ge(s_k_lo, m)
                    if which == 2 and later(m):
                        pe.wait_ge(s_v_lo, m)
                dst = qkv_bank[which][:, 0:T]
                for c in range(NC):
                    split_product(dst, [w_qkv[:, p, which, c, e, :] for p in range(2)],
                                  [xm[:, e, p * NC + c, 0:T] for p in range(2)],
                                  e == 0 and c == 0, e == E - 1 and c == NC - 1,
                                  done if (e == E - 1 or which == 2) and c == NC - 1 else None)

            def dots(f, t, m=None):
                if t == 1 and m is not None and later(m):
                    pe.wait_ge(s_v_lo, m)
                if t == 0:
                    pe.wait_ge(s_T1_hi, f + 1)
                    pe.wait_ge(s_T1_lo, f + 1)
                    if later(f):
                        pe.wait_ge(s_h2_ready, NT * f)
                if t == 2:
                    pe.wait_ge(s_cos_ready, NT * f + 1)
                for c in range(NC):
                    split_product(work[t % 2][:, t * P:T], [xT[0][:, p, c, t * P:(t + 1) * P] for p in range(2)],
                                  [xT[0][:, p, c, t * P:T] for p in range(2)], c == 0, c == NC - 1,
                                  s_dots_done if c == NC - 1 else None)

            def turn_exp(f):
                pe.wait_ge(s_exp1_lo, NT * f + NT - 1)
                k = 0
                for p in range(2):
                    for j in range(1, NT):
                        for i in range(j):
                            last = t_.transpose(as16(turn[1], NC * TP)[:, k * P:(k + 1) * P],
                                                exp1_hl[:, p, i, j * P:(j + 1) * P], ident16[:, :])
                            k += 1
                last.then_inc(s_exp1_turned, 1)

            def attend(f, t):
                if t == 0:
                    pe.wait_ge(s_exp1_lo, NT * (f + 1))
                    pe.wait_ge(s_exp1_square, (NT - 1) * (f + 1))
                    pe.wait_ge(s_cos_ready, NT * (f + 1))
                for j in range(NT):
                    for k, (ep, xp, n) in enumerate(((0, 0, C + 1), (0, 1, C), (1, 0, C + 1))):
                        last = t_.matmul(att_bank[t][:, 0:n], exp1_hl[:, ep, j, t * P:(t + 1) * P],
                                         xhl[0][:, xp, j, 0:n], start=(j == 0 and k == 0),
                                         stop=(j == NT - 1 and k == 2), skip_group_check=True)
                last.then_inc(s_att_done, 1)

            def logits(f):
                pe.wait_ge(s_T2_hi, f + 1)
                pe.wait_ge(s_T2_lo, f + 1)
                for t in range(NT):
                    dst = turn[0][:, t * 2 * E:(t + 1) * 2 * E]
                    for c in range(NC):
                        t_.matmul(dst, xT[1][:, 0, c, t * P:(t + 1) * P], w_sim[:, c, :, :].rearrange("p a e -> p (a e)"),
                                  start=(c == 0), stop=False, skip_group_check=True)
                    for c in range(NC):
                        last = t_.matmul(dst[:, 0:E], xT[1][:, 1, c, t * P:(t + 1) * P], w_sim[:, c, 0, :],
                                         start=False, stop=(c == NC - 1), skip_group_check=True)
                last.then_inc(s_logits_done, 1)

            def turn_mask(f):
                pe.wait_ge(s_mask_ready, 2 * (f + 1))
                pe.wait_ge(s_T2_lo, f + 1)
                for t in range(NT):
                    last = t_.transpose(as16(turn[1], TP)[0:E, t * P:(t + 1) * P], mask16[:, t, :], ident16[:, :])
                last.then_inc(s_mask_turned, 1)

            def score(n, i):
                if i == 0:
                    pe.wait_ge(s_q_lo, n + 1)
                    pe.wait_ge(s_k_lo, n + 1)
                    if later(n):
                        pe.wait_ge(s_pair_added, PAIRS * n)
                if i == 2:
                    pe.wait_ge(s_scores_out, NT * n + 1)
                split_product(out_bank[i % 2][:, 0:KEYS[i]], [qT[:, p, i * P:(i + 1) * P] for p in range(2)],
                              [kT[:, p, 0:KEYS[i]] for p in range(2)], True, True, s_scores_done)

            def last_scores(n):
                pe.wait_ge(s_q_lo, n + 1)
                pe.wait_ge(s_k_lo, n + 1)
                for i in range(NT):
                    split_product(last_bank[i][:, 0:KEYS[i]], [qT[:, p, i * P:(i + 1) * P] for p in range(2)],
                                  [kT[:, p, 0:KEYS[i]] for p in range(2)], True, True, s_scores_done)

            def turn_v(n):
                pe.wait_ge(s_v_hi, n + 1)
                pe.wait_ge(s_v_lo, n + 1)
                for p in range(2):
                    for t in range(NT):
                        last = t_.transpose(as16(bank[4] if final(n) else turn[0], 2 * NT * D)[:, (p * NT + t) * D:(p * NT + t + 1) * D],
                                                vT[:, p, t * P:(t + 1) * P], ident16[:, :])
                last.then_inc(s_v_turned, 1)

            def turn_probs(n, f=None):
                pe.wait_ge(s_exp2_hi, NT * (n + 1))
                pe.wait_ge(s_exp2_lo, n + 1)
                if final(n):
                    pe.wait_ge(s_scores_out, NT * (n + 1))
                else:
                    pe.wait_ge(s_v_tok_ready, n + 1)
                for p, dst, done in ((1, turn[0], s_pT_lo_turned), (0, turn[1], s_pT_hi_turned)):
                    if p == 0 and f is not None:
                        pe.wait_ge(s_h2_ready, NT * (f + 1))
                    for i in range(NT):
                        for j in range(i + 1):
                            at = PT_OFF[j] + (i - j) * P
                            last = t_.transpose(as16(dst, PW)[:, at:at + P],
                                                exp2_hl[:, p, S_OFF[i] + j * P:S_OFF[i] + (j + 1) * P], ident16[:, :])
                    last.then_inc(done, 1)

            def probs_v(n):
                pe.wait_ge(s_pT_hi, n + 1)
                pe.wait_ge(s_pT_lo, n + 1)
                pe.wait_ge(s_v_tok_ready, n + 1)
                for j in range(NT):
                    nq = T - j * P
                    split_product(probs_bank(n)[:, j * P:T], [v_tok[:, p, j, :] for p in range(2)],
                                  [pT[:, p, PT_OFF[j]:PT_OFF[j] + nq] for p in range(2)], j == 0, j == NT - 1,
                                  s_pv_done if j == NT - 1 else None)

            def pair(n, p):
                t, q = p // (E // 2), p % (E // 2)
                if p == 0:
                    if not later(n):
                        pe.wait_ge(s_w_lo, 3 * NC + 2)
                    pe.wait_ge(s_ao_hi, n + 1)
                    pe.wait_ge(s_ao_lo, n + 1)
                ahead = 4 if final(n) else 2
                if p >= ahead:
                    pe.wait_ge(s_pair_added, PAIRS * n + p - ahead + 1)
                split_product(pair_bank(n, p)[:, :], [aoT[:, k, t * P:(t + 1) * P] for k in range(2)],
                              [w_o[:, k, 2 * q * C:(2 * q + 2) * C] for k in range(2)], True, True, s_pair_done)

            def step(i, g1, f, m, n):
                def F(fn, *a):
                    if f is not None:
                        fn(f, *a)

                def M(*us):
                    if m is not None:
                        for u in us:
                            unit(m, u // E, u % E)

                def N(fn, *a):
                    if n is not None:
                        fn(n, *a)

                if early(m):
                    M(*range(5))
                    turn_exp(f)
                    M(5)
                    for t in range(NT):
                        attend(f, t)
                    M(*range(6, 13))
                    pe.wait_ge(s_hi2, f + 1)
                    turn_rows(1, f, 0, turn[0], s_turned2_hi)
                    M(13)
                    pe.wait_ge(s_lo2, f + 1)
                    turn_rows(1, f, 1, turn[1], s_turned2_lo)
                    M(14)
                    logits(f)
                    M(*range(15, 19))
                    turn_mask(f)
                    M(*range(19, 22))
                    turn_first(g1)
                    M(22, 23)
                    return

                M(0)
                F(dots, 0)
                F(dots, 1, m)
                M(*(1, 2, 3) if second(m) else (1,))
                F(dots, 2)
                if not final(n):
                    N(score, 0)
                    N(score, 1)
                if not second(m):
                    M(2)
                F(turn_exp)
                if not second(m):
                    M(3)
                if not final(n):
                    N(score, 2)
                if f is not None:
                    pe.wait_ge(s_T1_hi, f + 1)
                elif n == B - 2:
                    pe.wait_ge(s_logits_out, B)
                    pe.wait_ge(s_mask_row, B)
                N(turn_v)
                M(4)
                for t in range(NT):
                    F(attend, t)
                M(5)
                if f is None:
                    M(6, 7)
                if not final(n):
                    N(turn_probs, f)
                M(8 if f is None else 6)
                N(probs_v)
                if f is not None:
                    M(7, 8)
                if f is not None:
                    pe.wait_ge(s_hi2, f + 1)
                    if n is not None:
                        pe.wait_ge(s_pT_lo, n + 1)
                    turn_rows(1, f, 0, turn[0], s_turned2_hi)
                M(9)
                if f is not None:
                    pe.wait_ge(s_lo2, f + 1)
                    turn_rows(1, f, 1, turn[1], s_turned2_lo)
                N(pair, 0)
                M(10)
                F(logits)
                N(pair, 1)
                M(11, 12)
                N(pair, 2)
                M(13)
                F(turn_mask)
                N(pair, 3)
                M(14)
                N(pair, 4)
                M(15)
                N(pair, 5)
                if final(m):
                    for k in range(4):
                        M(16 + k)
                        N(pair, 6 + k)
                        if k == 1:
                            last_scores(m)
                    M(20, 21, 22, 23)
                    turn_probs(m)
                    N(pair, 10)
                    N(pair, 11)
                    return
                for k in range(6):
                    M(16 + k)
                    N(pair, 6 + k)
                if g1 is not None:
                    turn_first(g1)
                M(22, 23)

            pe.wait_ge(s_tokw_lo, 1)
            pe.wait_ge(s_setup_dve, 6)
            pe.wait_ge(s_picked, 4)
            slot(0, 0)
            slot(1, 1)
            slot(2, 0)
            looped_slots(pe, slot)
            turn_first(0)
            slot(7, 1)
            for t in range(NT):
                dots(0, t)
            slot(8, 0)
            slot(9, 1)
            turn_exp(0)
            for t in range(NT):
                attend(0, t)
            slot(10, 0)
            slot(11, 1)
            turn_first(1)
            slot(12, 0)
            pe.wait_ge(s_hi2, 1)
            pe.wait_ge(s_T1_hi, 2)
            turn_rows(1, 0, 0, turn[0], s_turned2_hi)
            pe.wait_ge(s_lo2, 1)
            pe.wait_ge(s_T1_lo, 2)
            turn_rows(1, 0, 1, turn[1], s_turned2_lo)
            dots(1, 0)
            dots(1, 1)
            pe.wait_ge(s_sim_lo, 1)
            logits(0)
            slot(13, 1)
            turn_mask(0)
            slot(14, 0)
            slot(15, 1)
            dots(1, 2)
            pe.wait_ge(s_h_ready, B)
            pe.wait_ge(s_w_lo, 3 * NC)
            pipeline(pe, step)


_INS = ['x', 'L0_tok_W', 'L0_tok_b', 'L0_ffn_sim_matrix', 'L0_ffn_gates', 'L0_ffn_q_proj', 'L0_ffn_k_proj',
        'L0_ffn_v_proj', 'L0_ffn_o_proj']


def kernel(**inputs):
    import numpy as _np
    import concourse.bacc as _bacc
    from concourse import mybir as _mybir
    from concourse.bass_utils import run_bass_kernel_spmd as _run

    nc = _bacc.Bacc("TRN2", target_bir_lowering=False, num_devices=1)
    arrays, args = {}, []
    for name in _INS:
        a = _np.ascontiguousarray(inputs[name])
        arrays[f"in_{name}_dram"] = a
        args.append(nc.dram_tensor(f"in_{name}_dram", a.shape, _mybir.dt.from_np(a.dtype), kind="ExternalInput").ap())
    B, T1, C = inputs['x'].shape
    args.append(nc.dram_tensor("out_0_dram", (B, T1 - 1, C), _mybir.dt.from_np(_np.dtype('float32')),
                               kind="ExternalOutput").ap())
    audio_tower_kernel(nc, *args)
    r = _run(nc, [arrays], core_ids=[0])
    return r.results[0]["out_0_dram"]
```
